# Optimizing a Trainium2 kernel written in Bass

```python
import numpy as np
import jax
import jax.numpy as jnp

def _softmax(x, axis=-1):
    return jax.nn.softmax(x, axis=axis)

def _gelu(x):
    return jax.nn.gelu(x, approximate=True)

def _silu(x):
    return jax.nn.silu(x)

def _sigmoid(x):
    return jax.nn.sigmoid(x)

def _layernorm(x, axis=-1, eps=1e-05):
    m = jnp.mean(x, axis=axis, keepdims=True)
    v = jnp.var(x, axis=axis, keepdims=True)
    return (x - m) / jnp.sqrt(v + eps)

def _scatter_add(tgt, idx, src, axis=0):
    return tgt.at[idx].add(src)

def _segment_sum(src, seg, n):
    return jax.ops.segment_sum(src, seg, n)
kernel_name = 'mk_seq_postln_d1_jaxref_r4_c726ed'

def setup_inputs(seed: int=0):
    np.random.seed(seed)
    _w = jnp.asarray

    def _L0_attn_setup():
        import jax, jax.numpy as jnp
        import numpy as np
        HIDDEN = 256
        HEADS = 16
        HEAD_DIM = HIDDEN // HEADS
        MAX_SEQ = 512

        def _rope_tables():
            inv_freq = 1.0 / 10000.0 ** (jnp.arange(0, HEAD_DIM, 2, dtype=jnp.float32) / HEAD_DIM)
            t = jnp.arange(MAX_SEQ, dtype=jnp.float32)
            freqs = t[:, None] * inv_freq[None, :]
            return (jnp.cos(freqs), jnp.sin(freqs))
        key = jax.random.key(seed)
        k1, k2, k3 = jax.random.split(key, 3)
        x = jax.random.normal(k1, (2, 512, HIDDEN), dtype=jnp.float32)
        qkv_w = jax.random.normal(k2, (HIDDEN, 3 * HIDDEN), dtype=jnp.float32) * 0.02
        qkv_b = jnp.zeros((3 * HIDDEN,), dtype=jnp.float32)
        out_w = jax.random.normal(k3, (HIDDEN, HIDDEN), dtype=jnp.float32) * 0.02
        out_b = jnp.zeros((HIDDEN,), dtype=jnp.float32)
        return {'x': x, 'qkv_w': qkv_w, 'qkv_b': qkv_b, 'out_w': out_w, 'out_b': out_b}
    _L0_attn_in = _L0_attn_setup()

    def _L0_ffn_setup():
        import jax, jax.numpy as jnp
        import numpy as np
        TOP_K = 2
        EPS = 1e-05

        def layer_norm(x, g, b):
            mu = jnp.mean(x, axis=-1, keepdims=True)
            var = jnp.mean(jnp.square(x - mu), axis=-1, keepdims=True)
            return (x - mu) * jax.lax.rsqrt(var + EPS) * g + b
        key = jax.random.key(seed)
        ks = jax.random.split(key, 12)
        B, S, D, F, E = (2, 512, 256, 1024, 8)
        std = 0.02
        return {'x': jax.random.normal(ks[0], (B, S, D), jnp.float32), 'g1': jnp.ones((D,), jnp.float32), 'be1': jnp.zeros((D,), jnp.float32), 'mix_w': jax.random.normal(ks[1], (D, D), jnp.float32) * std, 'mix_b': jnp.zeros((D,), jnp.float32), 'g2': jnp.ones((D,), jnp.float32), 'be2': jnp.zeros((D,), jnp.float32), 'router_w': jax.random.normal(ks[2], (D, E), jnp.float32) * std, 'w1': jax.random.normal(ks[3], (E, D, F), jnp.float32) * std, 'b1': jnp.zeros((E, F), jnp.float32), 'w2': jax.random.normal(ks[4], (E, F, D), jnp.float32) * std, 'b2': jnp.zeros((E, D), jnp.float32)}
    _L0_ffn_in = _L0_ffn_setup()
    _d = {'L0_attn_x': _L0_attn_in['x'], 'L0_attn_qkv_w': _L0_attn_in['qkv_w'], 'L0_attn_qkv_b': _L0_attn_in['qkv_b'], 'L0_attn_out_w': _L0_attn_in['out_w'], 'L0_attn_out_b': _L0_attn_in['out_b'], 'L0_ffn_g1': _L0_ffn_in['g1'], 'L0_ffn_be1': _L0_ffn_in['be1'], 'L0_ffn_mix_w': _L0_ffn_in['mix_w'], 'L0_ffn_mix_b': _L0_ffn_in['mix_b'], 'L0_ffn_g2': _L0_ffn_in['g2'], 'L0_ffn_be2': _L0_ffn_in['be2'], 'L0_ffn_router_w': _L0_ffn_in['router_w'], 'L0_ffn_w1': _L0_ffn_in['w1'], 'L0_ffn_b1': _L0_ffn_in['b1'], 'L0_ffn_w2': _L0_ffn_in['w2'], 'L0_ffn_b2': _L0_ffn_in['b2']}
    _x0 = _d['L0_attn_x']
    _d['L0_attn_x'] = jax.random.normal(jax.random.fold_in(jax.random.key(seed), 1), (2, 2048, 256), dtype=_x0.dtype)
    del _x0
    return _d

def reference(L0_attn_x, L0_attn_qkv_w, L0_attn_qkv_b, L0_attn_out_w, L0_attn_out_b, L0_ffn_g1, L0_ffn_be1, L0_ffn_mix_w, L0_ffn_mix_b, L0_ffn_g2, L0_ffn_be2, L0_ffn_router_w, L0_ffn_w1, L0_ffn_b1, L0_ffn_w2, L0_ffn_b2):

    def _L0_attn_ref(x, qkv_w, qkv_b, out_w, out_b):
        import jax, jax.numpy as jnp
        import numpy as np
        HIDDEN = 256
        HEADS = 16
        HEAD_DIM = HIDDEN // HEADS
        MAX_SEQ = 512

        def _rope_tables():
            inv_freq = 1.0 / 10000.0 ** (jnp.arange(0, HEAD_DIM, 2, dtype=jnp.float32) / HEAD_DIM)
            t = jnp.arange(MAX_SEQ, dtype=jnp.float32)
            freqs = t[:, None] * inv_freq[None, :]
            return (jnp.cos(freqs), jnp.sin(freqs))
        b, s, _ = x.shape
        qkv = x @ qkv_w + qkv_b
        qkv = qkv.reshape(b, s, HEADS, 3 * HEAD_DIM).transpose(0, 2, 1, 3)
        q, k, v = jnp.split(qkv, 3, axis=-1)
        cos_tab, sin_tab = _rope_tables()
        cos = cos_tab[:HEADS][None, :, None, :]
        sin = sin_tab[:HEADS][None, :, None, :]

        def rot(u):
            u1 = u[..., :HEAD_DIM // 2]
            u2 = u[..., HEAD_DIM // 2:]
            return jnp.concatenate([u1 * cos - u2 * sin, u2 * cos + u1 * sin], axis=-1)
        q = rot(q)
        k = rot(k)
        scores = jnp.einsum('bhqd,bhkd->bhqk', q, k) / HEAD_DIM ** 0.5
        attn = jax.nn.softmax(scores.astype(jnp.float32), axis=-1).astype(scores.dtype)
        out = jnp.einsum('bhqk,bhkd->bhqd', attn, v)
        out = out.transpose(0, 2, 1, 3).reshape(b, s, HEADS * HEAD_DIM)
        return out @ out_w + out_b

    def _L0_ffn_ref(x, g1, be1, mix_w, mix_b, g2, be2, router_w, w1, b1, w2, b2):
        import jax, jax.numpy as jnp
        import numpy as np
        TOP_K = 2
        EPS = 1e-05

        def layer_norm(x, g, b):
            mu = jnp.mean(x, axis=-1, keepdims=True)
            var = jnp.mean(jnp.square(x - mu), axis=-1, keepdims=True)
            return (x - mu) * jax.lax.rsqrt(var + EPS) * g + b
        res = x
        n = layer_norm(x, g1, be1)
        x = res + n + (n @ mix_w + mix_b)
        res = x
        n = layer_norm(x, g2, be2)
        B, S, D = n.shape
        E = w1.shape[0]
        flat = n.reshape(-1, D)
        probs = jax.nn.softmax(flat @ router_w, axis=-1)
        topw, topi = jax.lax.top_k(probs, TOP_K)
        combine = jnp.sum(jax.nn.one_hot(topi, E, dtype=flat.dtype) * topw[..., None], axis=1)
        h = jax.nn.silu(jnp.einsum('td,edf->tef', flat, w1) + b1)
        y = jnp.einsum('tef,efd->ted', h, w2) + b2
        out = jnp.einsum('te,ted->td', combine, y)
        return res + out.reshape(B, S, D)
    x = L0_attn_x
    x = _layernorm(x + _L0_attn_ref(x, L0_attn_qkv_w, L0_attn_qkv_b, L0_attn_out_w, L0_attn_out_b), axis=-1)
    x = _layernorm(x + _L0_ffn_ref(x, L0_ffn_g1, L0_ffn_be1, L0_ffn_mix_w, L0_ffn_mix_b, L0_ffn_g2, L0_ffn_be2, L0_ffn_router_w, L0_ffn_w1, L0_ffn_b1, L0_ffn_w2, L0_ffn_b2), axis=-1)
    return x

_drawn_inputs = setup_inputs


def setup_inputs(seed=0):
    import zlib

    import numpy as np

    out = dict(_drawn_inputs(seed))
    spreads = {'L0_attn_qkv_b': (0.0, 0.1),
     'L0_attn_out_b': (0.0, 0.1),
     'L0_ffn_g1': (1.0, 0.2),
     'L0_ffn_be1': (0.0, 0.1),
     'L0_ffn_mix_b': (0.0, 0.1),
     'L0_ffn_g2': (1.0, 0.6),
     'L0_ffn_be2': (0.0, 0.8),
     'L0_ffn_b1': (0.0, 0.8),
     'L0_ffn_b2': (0.0, 0.8)}
    factors = {'L0_attn_qkv_w': 8.0, 'L0_ffn_router_w': 5.081, 'L0_ffn_w1': 6.157, 'L0_ffn_w2': 5.835}
    for name, (base, spread) in spreads.items():
        noise = np.random.default_rng([zlib.crc32(name.encode()), seed]).standard_normal(out[name].shape)
        drawn = base * np.exp(spread * noise) if base else spread * noise
        out[name] = jnp.asarray(drawn.astype(out[name].dtype))
    for name, factor in factors.items():
        out[name] = (out[name] * factor).astype(out[name].dtype)
    return out
```

```python
import concourse.bass as bass
from concourse import mybir
from contextlib import ExitStack

F32 = mybir.dt.float32
BF16 = mybir.dt.bfloat16
I32 = mybir.dt.int32
U32 = mybir.dt.uint32
ALU = mybir.AluOpType
ACT = mybir.ActivationFunctionType
AX = mybir.AxisListType

B, S, D = 2, 2048, 256
H, HD = 16, 16
E, F = 8, 1024
P = 128
BH = B * H
T = B * S
NT = T // P
KT = S // P
QC = S // 512
KC = D // P
GT = 4
GROUPS = NT // GT
PARTS = 3
Q_ORDER = (0, 0, 0, 1, 1, 2)
K_ORDER = (0, 1, 2, 0, 1, 0)
ROWS = HD * len(Q_ORDER)
ROWS_M = ROWS + PARTS
EPS = 1e-5
GAP = 110.0
REGION = T + P
TILES = 72


class Mem:

    def __init__(self, nc, stack):
        self.nc, self.stack = nc, stack

    def sb(self, name, shape, dtype):
        return self.stack.enter_context(self.nc.sbuf_tensor(name, shape, dtype))

    def ps(self, name, shape, dtype=F32):
        return self.stack.enter_context(self.nc.psum_tensor(name, shape, dtype))

    def sem(self, name):
        return self.stack.enter_context(self.nc.semaphore(name))


class Chain:

    def __init__(self, engine, sem, base=0):
        self.engine, self.sem, self.base, self.n = engine, sem, base, 0

    def then(self, instruction):
        instruction.then_inc(self.sem, 1)
        self.n += 1
        self.engine.wait_ge(self.sem, self.base + self.n)


def constants(nc, dram, keep):
    with ExitStack() as stack:
        m = Mem(nc, stack)
        b_in = m.sb("co_b_in", [E, F + D], F32)
        b_rest = m.sb("co_b_rest", [E, F + D], F32)
        b_parts = m.sb("co_b_parts", [E, PARTS, F + D], BF16)
        filled = m.sem("co_filled")
        loaded = m.sem("co_loaded")
        step = m.sem("co_step")
        split = m.sem("co_split")
        stored = m.sem("co_stored")
        with nc.Block() as block:

            @block.sync
            def _(sp):
                sp.dma_start(b_in[:, 0:F], dram["b1"]).then_inc(loaded, 16)
                sp.dma_start(b_in[:, F:], dram["b2"]).then_inc(loaded, 16)
                sp.wait_ge(split, 1)
                sp.dma_start(dram["b_parts"].rearrange("t e n -> e t n"), b_parts[:, :, :]).then_inc(stored, 16)
                sp.wait_ge(stored, 16)

            @block.vector
            def _(dve):
                v = nc.vector
                steps = Chain(dve, step)
                dve.wait_ge(loaded, 32)
                steps.then(v.tensor_copy(b_parts[:, 0, :], b_in[:, :]))
                steps.then(v.tensor_tensor(b_rest[:, :], b_in[:, :], b_parts[:, 0, :], ALU.subtract))
                steps.then(v.tensor_copy(b_parts[:, 1, :], b_rest[:, :]))
                v.tensor_tensor(b_parts[:, 2, :], b_rest[:, :], b_parts[:, 1, :], ALU.subtract).then_inc(split, 1)

            @block.gpsimd
            def _(pool):
                for tile in (keep["identity"], keep["identity16"]):
                    nc.gpsimd.memset(tile[:, :], 0.0).then_inc(filled, 1)
                pool.wait_ge(filled, 2)
                for tile in (keep["identity"], keep["identity16"]):
                    nc.gpsimd.affine_select(out=tile[:, :], in_=tile[:, :], compare_op=ALU.not_equal, fill=1.0,
                                            base=0, pattern=[[-1, P]], channel_multiplier=1)


def project(nc, dram, keep, hi_all, squares, key_sum):
    with ExitStack() as stack:
        m = Mem(nc, stack)
        raw = m.sb("qkv_raw", [P, KC + 1, H * 3 * HD], F32)
        trig = m.sb("trig", [P, 2, H, HD // 2], F32)
        rot_a = m.sb("rot_a", [P, KC + 1, H, HD // 2], F32)
        rot_b = m.sb("rot_b", [P, KC + 1, H, HD // 2], F32)
        w_qk = m.sb("w_qk", [P, KC + 1, 4, P], F32)
        w_v = m.sb("w_v", [P, KC + 1, D], F32)
        bias_qk = m.sb("bias_qk", [P, 4], F32)
        x_in = m.sb("x_in", [P, 2, GT, D], F32)
        xT = m.sb("xT", [P, 2, KC, 512], F32)
        lower = m.sb("qk_lower", [P, 4, PARTS - 1, 512], BF16)
        rest = m.sb("qk_rest", [P, 4, 512], F32)
        p_x = [m.ps(f"p_x{i}", [P, 512]) for i in range(KC)]
        p_qk = [m.ps(f"p_qk{i}", [P, 512]) for i in range(4)]
        p_v = [m.ps(f"p_v{i}", [P, 2, D]) for i in range(2)]

        loaded_w = m.sem("pj_loaded_w")
        loaded_x = [m.sem(f"pj_loaded_x{i}") for i in range(2)]
        rot_step = m.sem("pj_rot_step")
        weights_rotated = m.sem("pj_weights_rotated")
        bias_turned = m.sem("pj_bias_turned")
        bias_ready = m.sem("pj_bias_ready")
        x_turned = m.sem("pj_x_turned")
        xT_ready = [m.sem(f"pj_xT_ready{i}") for i in range(KC)]
        qk_done = m.sem("pj_qk_done")
        v_done = m.sem("pj_v_done")
        hi_ready = m.sem("pj_hi_ready")
        rest_ready = m.sem("pj_rest_ready")
        mid_ready = m.sem("pj_mid_ready")
        lo_ready = m.sem("pj_lo_ready")
        v_ready = m.sem("pj_v_ready")
        stored = [m.sem(f"pj_stored{i}") for i in range(4)]

        x_rows = dram["x"].rearrange("b s c -> (b s) c")
        identity, v_all = keep["identity"], keep["v_all"]

        with nc.Block() as block:

            def store_parts(sp, b, c):
                for ft in range(4):
                    sp.wait_ge(lo_ready, b * (4 * QC) + 4 * c + ft + 1 + 4)
                    rows = bass.ds(b * D + (ft % 2) * P, P)
                    cols = slice(c * 512, (c + 1) * 512)
                    sp.dma_start(dram["qk"][ft // 2][0, rows, cols], hi_all[:, ft, bass.ds(b * S + c * 512, 512)]
                                 ).then_inc(stored[ft], 16)
                    sp.dma_start(dram["qk"][ft // 2][1:, rows, cols].rearrange("t r n -> r t n"), lower[:, ft, :, :]
                                 ).then_inc(stored[ft], 16)

            @block.sync
            def _(sp):
                sp.dma_start(raw[:, 0:KC, :], dram["qkv_w"].rearrange("(s p) n -> p s n", p=P)).then_inc(loaded_w, 16)
                sp.dma_start(raw[:, KC, :], dram["qkv_b"].partition_broadcast(P)).then_inc(loaded_w, 16)
                sp.dma_start(trig[:, :, :, :].rearrange("p t h j -> p (t h j)"),
                             dram["trig"].partition_broadcast(P)).then_inc(loaded_w, 16)
                sp.sem_inc(x_turned, 4)
                for i in range(4):
                    sp.sem_inc(stored[i], 32)
                with sp.Fori(0, B) as b:
                    for c in range(QC):
                        g = b * QC + c
                        sp.wait_ge(x_turned, b * (2 * QC) + 2 * c + 2)
                        sp.dma_start(x_in[:, c % 2, :, :],
                                     x_rows[bass.ds(g * 512, 512), :].rearrange("(a p) n -> p a n", p=P)
                                     ).then_inc(loaded_x[c % 2], 16)
                        if c == 0:
                            continue
                        store_parts(sp, b, c - 1)
                    store_parts(sp, b, QC - 1)
                for i in range(4):
                    sp.wait_ge(stored[i], 32 * (GROUPS + 1))

            @block.vector
            def _(dve):
                steps = Chain(dve, rot_step)
                dve.wait_ge(loaded_w, 48)
                heads = raw[:, :, :].rearrange("p s (h w) -> p s h w", w=3 * HD)
                cos = trig[:, 0, :, :].unsqueeze(1).broadcast_to([P, KC + 1, H, HD // 2])
                sin = trig[:, 1, :, :].unsqueeze(1).broadcast_to([P, KC + 1, H, HD // 2])
                for n in range(2):
                    u1 = heads[:, :, :, n * HD:n * HD + 8]
                    u2 = heads[:, :, :, n * HD + 8:n * HD + 16]
                    out = w_qk[:, :, 2 * n:2 * n + 2, :].rearrange("p s t (h w) -> p s (t h) w", w=HD)
                    nc.vector.tensor_tensor(rot_a[:, :, :, :], u1, cos, ALU.mult)
                    steps.then(nc.vector.tensor_tensor(rot_b[:, :, :, :], u2, sin, ALU.mult))
                    steps.then(nc.vector.tensor_tensor(out[:, :, :, 0:8], rot_a[:, :, :, :], rot_b[:, :, :, :],
                                                       ALU.subtract))
                    nc.vector.tensor_tensor(rot_a[:, :, :, :], u2, cos, ALU.mult)
                    steps.then(nc.vector.tensor_tensor(rot_b[:, :, :, :], u1, sin, ALU.mult))
                    steps.then(nc.vector.tensor_tensor(out[:, :, :, 8:16], rot_a[:, :, :, :], rot_b[:, :, :, :],
                                                       ALU.add))
                nc.vector.tensor_scalar(w_qk[:, :, 0:2, :], w_qk[:, :, 0:2, :], HD ** -0.5, None, ALU.mult)
                nc.vector.tensor_copy(w_v[:, :, :].rearrange("p s (h w) -> p s h w", w=HD),
                                      heads[:, :, :, 2 * HD:]).then_inc(weights_rotated, 1)
                dve.wait_ge(bias_turned, 1)
                nc.vector.tensor_copy(bias_qk[:, :], p_qk[0][:, :].rearrange("p (t n) -> p t n", t=4)[:, :, 0]
                                      ).then_inc(bias_ready, 1)
                dve.sem_inc(rest_ready, 4)
                dve.sem_inc(xT_ready[1], 1)
                dve.sem_inc(v_ready, 2)
                with dve.Fori(0, B) as b:
                    for c in range(QC):
                        g = b * QC + c
                        dve.wait_ge(x_turned, b * (2 * QC) + 2 * c + 2 + 4)
                        nc.vector.tensor_copy(xT[:, c % 2, 1, :], p_x[1][:, :]).then_inc(xT_ready[1], 1)
                        for ft in range(4):
                            at = b * (4 * QC) + 4 * c + ft
                            dve.wait_ge(hi_ready, at + 1)
                            dve.wait_ge(lo_ready, at + 1)
                            nc.vector.scalar_tensor_tensor(rest[:, ft, :], p_qk[ft][:, :], bias_qk[:, ft:ft + 1],
                                                           hi_all[:, ft, bass.ds(b * S + c * 512, 512)], ALU.add, ALU.subtract
                                                           ).then_inc(rest_ready, 1)
                        for i in range(2):
                            dve.wait_ge(v_done, b * (2 * QC) + 2 * c + i + 1)
                            dst = v_all[:, bass.ds(b * H, H), 4 * c + 2 * i:4 * c + 2 * i + 2, :]
                            nc.vector.tensor_tensor(
                                dst.rearrange("p h a w -> p a h w"),
                                p_v[i][:, :, :].rearrange("p a (h w) -> p a h w", w=HD),
                                w_v[:, KC, :].rearrange("p (h w) -> p h w", w=HD).unsqueeze(1)
                                .broadcast_to([P, 2, H, HD]), ALU.add).then_inc(v_ready, 1)

            @block.scalar
            def _(act):
                act.sem_inc(xT_ready[0], 1)
                act.wait_ge(bias_ready, 1)
                with act.Fori(0, B) as b:
                    for c in range(QC):
                        act.wait_ge(x_turned, b * (2 * QC) + 2 * c + 1 + 4)
                        nc.scalar.activation(xT[:, c % 2, 0, :], p_x[0][:, :], ACT.Identity
                                             ).then_inc(xT_ready[0], 1)
                        for ft in range(5):
                            if ft < 4:
                                at = b * (4 * QC) + 4 * c + ft
                                act.wait_ge(qk_done, at + 1)
                                hi = hi_all[:, ft, bass.ds(b * S + c * 512, 512)]
                                total = key_sum[:, ft - 2, bass.ds(b * QC + c, 1)] if ft >= 2 else None
                                nc.scalar.activation(hi, p_qk[ft][:, :], ACT.Identity, bias=bias_qk[:, ft:ft + 1],
                                                     accum_out=total).then_inc(hi_ready, 1)
                            if ft > 0:
                                at = b * (4 * QC) + 4 * c + ft - 1
                                act.wait_ge(rest_ready, at + 1 + 4)
                                act.wait_ge(stored[ft - 1], b * (32 * QC) + 32 * c + 32)
                                nc.scalar.activation(lower[:, ft - 1, 0, :], rest[:, ft - 1, :], ACT.Identity
                                                     ).then_inc(mid_ready, 1)

            @block.gpsimd
            def _(pool):
                pool.sem_inc(lo_ready, 4)
                with pool.Fori(0, B) as b:
                    for c in range(QC):
                        for ft in range(4):
                            pool.wait_ge(mid_ready, b * (4 * QC) + 4 * c + ft + 1)
                            nc.gpsimd.tensor_tensor(lower[:, ft, 1, :], rest[:, ft, :], lower[:, ft, 0, :],
                                                    ALU.subtract).then_inc(lo_ready, 1)
                            hi = hi_all[:, ft, bass.ds(b * S + c * 512, 512)]
                            nc.gpsimd.tensor_tensor(squares[:, ft, bass.ds(b * S + c * 512, 512)], hi, hi, ALU.mult)

            @block.tensor
            def _(pe):
                pe.wait_ge(weights_rotated, 1)
                for ft in range(4):
                    last = nc.tensor.transpose(p_qk[0][:, ft * P:(ft + 1) * P], w_qk[:, KC, ft, :], identity[:, :])
                last.then_inc(bias_turned, 1)
                pe.wait_ge(bias_ready, 1)
                with pe.Fori(0, B) as b:
                    for c in range(QC):
                        pe.wait_ge(loaded_x[c % 2], b * (8 * QC) + 16 * (c // 2 + 1))
                        for kc in range(KC):
                            pe.wait_ge(xT_ready[kc], b * QC + c + 1)
                            for a in range(GT):
                                last = nc.tensor.transpose(p_x[kc][:, a * P:(a + 1) * P],
                                                           x_in[:, c % 2, a, kc * P:(kc + 1) * P], identity[:, :])
                            last.then_inc(x_turned, 1)
                        for kc in range(KC):
                            pe.wait_ge(xT_ready[kc], b * QC + c + 2)
                        for ft in range(4):
                            pe.wait_ge(rest_ready, b * (4 * QC) + 4 * c + ft + 1)
                            for kc in range(KC):
                                last = nc.tensor.matmul(p_qk[ft][:, :], w_qk[:, kc, ft, :], xT[:, c % 2, kc, :],
                                                        start=(kc == 0), stop=(kc == KC - 1))
                            last.then_inc(qk_done, 1)
                        for i in range(2):
                            pe.wait_ge(v_ready, b * (2 * QC) + 2 * c + i + 1)
                            for a in range(2):
                                tok = (2 * i + a) * P
                                for kc in range(KC):
                                    last = nc.tensor.matmul(p_v[i][:, a, :], xT[:, c % 2, kc, tok:tok + P],
                                                            w_v[:, kc, :], start=(kc == 0), stop=(kc == KC - 1))
                            last.then_inc(v_done, 1)


def load_head(engine, dram, bh, q_rows, k_rows, loaded):
    for n, (part_q, part_k) in enumerate(zip(Q_ORDER, K_ORDER)):
        rows = slice(n * HD, (n + 1) * HD)
        engine.dma_start(q_rows[rows, :], dram["qk"][0][part_q, bass.ds(bh * HD, HD), :]).then_inc(loaded, 16)
        engine.dma_start(k_rows[rows, :], dram["qk"][1][part_k, bass.ds(bh * HD, HD), :]).then_inc(loaded, 16)


def maxima(nc, dram, keep):
    with ExitStack() as stack:
        m = Mem(nc, stack)
        q_rows = m.sb("mx_q", [P, S], BF16)
        k_rows = m.sb("mx_k", [P, S], BF16)
        negmax = m.sb("mx_negmax", [P, KT], F32)
        rest1 = m.sb("mx_rest1", [P, KT], F32)
        rest2 = m.sb("mx_rest2", [P, KT], F32)
        columns = m.sb("mx_columns", [P, P], BF16)
        parts = columns[:, 0:PARTS * KT].rearrange("p (t a) -> p t a", t=PARTS)
        turned = m.sb("mx_turned", [PARTS * KT, P], BF16)
        p_s = [m.ps(f"mx_s{i}", [P, S]) for i in range(2)]
        loaded = m.sem("mx_loaded")
        scored = m.sem("mx_scored")
        reduced = m.sem("mx_reduced")
        split = m.sem("mx_split")
        parts_ready = m.sem("mx_parts_ready")
        parts_turned = m.sem("mx_parts_turned")
        row_ready = m.sem("mx_row_ready")
        stored = m.sem("mx_stored")
        p_turn = p_s[0][:, 0:P // 2].bitcast(BF16)

        with nc.Block() as block:

            @block.sync
            def _(sp):
                wide = sp.value_load(keep["wide"][0:1, 0:1], min_val=0, max_val=P)
                with sp.If(wide > 0):
                    sp.sem_inc(stored, 16)
                    sp.sem_inc(parts_turned, 1)
                    with sp.Fori(0, BH) as bh:
                        sp.wait_ge(parts_turned, bh + 1)
                        load_head(sp, dram, bh, q_rows, k_rows, loaded)
                        sp.wait_ge(row_ready, bh + 1)
                        sp.dma_start(dram["negmax"][bass.ds(bh, 1), :, :].rearrange("o t (a n) -> (o t a) n", n=P),
                                     turned[:, :]).then_inc(stored, 16)
                    sp.wait_ge(stored, 16 * (BH + 1))

            @block.tensor
            def _(pe):
                wide = pe.value_load(keep["wide"][0:1, 0:1], min_val=0, max_val=P)
                with pe.If(wide > 0):
                    with pe.Fori(0, BH) as bh:
                        pe.wait_ge(loaded, (bh + 1) * (16 * 12))
                        for qt in range(KT):
                            if qt >= 2:
                                pe.wait_ge(reduced, bh * KT + qt - 1)
                            for c in range(QC):
                                last = nc.tensor.matmul(p_s[qt % 2][:, c * 512:(c + 1) * 512],
                                                        q_rows[0:ROWS, qt * P:(qt + 1) * P],
                                                        k_rows[0:ROWS, c * 512:(c + 1) * 512], start=True, stop=True)
                            last.then_inc(scored, 1)
                        pe.wait_ge(parts_ready, bh + 1)
                        nc.tensor.transpose(p_turn, columns[:, :],
                                            keep["identity16"][:, :]).then_inc(parts_turned, 1)
                        pe.wait_ge(row_ready, bh + 1)

            @block.vector
            def _(dve):
                wide = dve.value_load(keep["wide"][0:1, 0:1], min_val=0, max_val=P)
                with dve.If(wide > 0):
                    nc.vector.memset(columns[:, :], 0.0)
                    with dve.Fori(0, BH) as bh:
                        steps = Chain(dve, split, bh * 4)
                        for qt in range(KT):
                            dve.wait_ge(scored, bh * KT + qt + 1)
                            nc.vector.tensor_reduce(negmax[:, qt:qt + 1], p_s[qt % 2][:, :], AX.X, ALU.max, negate=True
                                                    ).then_inc(reduced, 1)
                        dve.wait_ge(reduced, bh * KT + KT)
                        dve.wait_ge(parts_turned, bh + 1)
                        steps.then(nc.vector.tensor_copy(parts[:, 0, :], negmax[:, :]))
                        steps.then(nc.vector.tensor_tensor(rest1[:, :], negmax[:, :], parts[:, 0, :], ALU.subtract))
                        steps.then(nc.vector.tensor_copy(parts[:, 1, :], rest1[:, :]))
                        steps.then(nc.vector.tensor_tensor(rest2[:, :], rest1[:, :], parts[:, 1, :], ALU.subtract))
                        nc.vector.tensor_copy(parts[:, 2, :], rest2[:, :]).then_inc(parts_ready, 1)
                        dve.wait_ge(parts_turned, bh + 2)
                        dve.wait_ge(stored, bh * 16 + 16)
                        nc.vector.tensor_copy(turned[:, :], p_turn[0:PARTS * KT, :]).then_inc(row_ready, 1)


def attention(nc, dram, keep):
    G3 = 3
    CHUNKS = KT * QC
    NG = -(-CHUNKS // G3)
    RING = 4
    PAIR = 2 * NG
    LOADS = 16 * 13
    assert PAIR % RING == 0
    with ExitStack() as stack:
        m = Mem(nc, stack)
        q_rows = [m.sb(f"at_q{u}", [P, S], BF16) for u in range(2)]
        k_rows = [m.sb(f"at_k{u}", [P, S], BF16) for u in range(2)]
        probs = m.sb("at_probs", [P, RING, G3 * 512], F32)
        v_one = [m.sb(f"at_v{u}", [P, KT, 2 * HD], F32) for u in range(2)]
        o_sb = [m.sb(f"at_o{u}", [P, 512], F32) for u in range(2)]
        rden = [m.sb(f"at_rden{u}", [P, 4, QC], F32) for u in range(2)]
        p_s = [m.ps(f"at_s{i}", [P, G3 * 512]) for i in range(2)]
        p_o = [m.ps(f"at_po{u}", [P, 512]) for u in range(2)]
        loaded = [m.sem(f"at_loaded{u}") for u in range(2)]
        ones_ready = m.sem("at_ones_ready")
        v_copied = [m.sem(f"at_v_copied{u}") for u in range(2)]
        scored = m.sem("at_scored")
        exp_done = m.sem("at_exp_done")
        weighed = m.sem("at_weighed")
        o_copied = m.sem("at_o_copied")
        o_turned = m.sem("at_o_turned")
        rden_ready = m.sem("at_rden_ready")
        normed = m.sem("at_normed")
        v_all, attn = keep["v_all"], keep["attn"]

        def chunks(g):
            return range(g * G3, min((g + 1) * G3, CHUNKS))

        with nc.Block() as block:

            @block.sync
            def _(sp):
                sp.sem_inc(scored, PAIR)
                sp.wait_ge(ones_ready, 2)
                with sp.Fori(0, BH // 2) as pair:
                    for u in range(2):
                        sp.wait_ge(scored, pair * PAIR + (u + 1) * NG)
                        load_head(sp, dram, pair * 2 + u, q_rows[u], k_rows[u], loaded[u])
                        sp.dma_start(q_rows[u][ROWS:ROWS_M, :],
                                     dram["negmax"][bass.ds(pair * 2 + u, 1), :, :].rearrange("o t n -> (o t) n")
                                     ).then_inc(loaded[u], 16)

            @block.gpsimd
            def _(pool):
                for u in range(2):
                    nc.gpsimd.memset(v_one[u][:, :, HD:], 1.0)
                pool.sem_inc(weighed, PAIR)
                with pool.Fori(0, BH // 2) as pair:
                    for u in range(2):
                        pool.wait_ge(weighed, pair * PAIR + (u + 1) * NG)
                        nc.gpsimd.tensor_copy(v_one[u][:, :, 0:HD],
                                              v_all[:, bass.ds(pair * 2 + u, 1), :, :]
                                              .rearrange("p o a w -> p (o a) w")).then_inc(v_copied[u], 1)

            @block.scalar
            def _(act):
                with act.Fori(0, BH // 2) as pair:
                    for n in range(PAIR):
                        width = 512 * len(chunks(n % NG))
                        act.wait_ge(scored, pair * PAIR + n + 1 + PAIR)
                        act.wait_ge(weighed, pair * PAIR + n + 1 - RING + PAIR)
                        nc.scalar.activation(probs[:, n % RING, 0:width], p_s[n % 2][:, 0:width], ACT.Exp
                                             ).then_inc(exp_done, 1)

            @block.tensor
            def _(pe):
                def score(pair, n):
                    u, g = n // NG % 2, n % NG
                    if g == 0:
                        pe.wait_ge(loaded[u], pair * LOADS + LOADS)
                    for i, c in enumerate(chunks(g)):
                        kt, qc = c // QC, c % QC
                        last = nc.tensor.matmul(p_s[n % 2][:, i * 512:(i + 1) * 512],
                                                k_rows[u][0:ROWS_M, kt * P:(kt + 1) * P],
                                                q_rows[u][0:ROWS_M, qc * 512:(qc + 1) * 512], start=True, stop=True)
                    last.then_inc(scored, 1)

                def weigh(pair, n):
                    u, g = n // NG, n % NG
                    if g == 0:
                        pe.wait_ge(v_copied[u], pair + 1)
                        pe.wait_ge(normed, pair * 2 + u + 1)
                    for i, c in enumerate(chunks(g)):
                        kt, qc = c // QC, c % QC
                        last = nc.tensor.matmul(p_o[u][32 * qc:32 * qc + 32, :], v_one[u][:, kt, :],
                                                probs[:, n % RING, i * 512:(i + 1) * 512],
                                                start=(kt == 0), stop=(kt == KT - 1))
                    last.then_inc(weighed, 1)

                def turn(pair, u):
                    pe.wait_ge(o_copied, pair * 2 + u + 1)
                    for i in range(4):
                        last = nc.tensor.transpose(p_o[u][:, i * P:(i + 1) * P], o_sb[u][:, i * P:(i + 1) * P],
                                                   keep["identity"][:, :])
                    last.then_inc(o_turned, 1)

                def heads(pair, is_last):
                    for n in range(PAIR):
                        pe.wait_ge(exp_done, pair * PAIR + n + 1)
                        if n + 2 < PAIR:
                            score(pair, n + 2)
                        elif not is_last:
                            score(pair + 1, n + 2 - PAIR)
                        weigh(pair, n)
                        if n == NG + 2:
                            turn(pair, 0)
                    turn(pair, 1)

                pe.sem_inc(normed, 2)
                score(0, 0)
                score(0, 1)
                with pe.Fori(0, BH // 2 - 1) as pair:
                    heads(pair, False)
                heads(BH // 2 - 1, True)

            @block.vector
            def _(dve):
                for u in range(2):
                    nc.vector.memset(k_rows[u][ROWS:ROWS_M, :], 1.0).then_inc(ones_ready, 1)
                with dve.Fori(0, BH // 2) as pair:
                    for u in range(2):
                        dve.wait_ge(weighed, pair * PAIR + (u + 1) * NG + PAIR)
                        nc.vector.tensor_copy(o_sb[u][:, :], p_o[u][:, :]).then_inc(o_copied, 1)
                        turned = p_o[u][:, :].rearrange("p (i j w) -> p i j w", i=4, j=QC)
                        dve.wait_ge(o_turned, pair * 2 + u + 1)
                        nc.vector.reciprocal(rden[u][:, :, :], turned[:, :, :, HD]).then_inc(rden_ready, 1)
                        dve.wait_ge(rden_ready, pair * 2 + u + 1)
                        out = attn[:, bass.ds(pair * 2 + u, 1), :, :].rearrange("p o (j i) w -> p i (o j) w", i=4)
                        nc.vector.tensor_tensor(out, turned[:, :, :, 0:HD],
                                                rden[u][:, :, :].unsqueeze(3).broadcast_to([P, 4, QC, HD]),
                                                ALU.mult).then_inc(normed, 1)


def bounds(nc, dram, keep, hi_all, squares, key_sum):
    with ExitStack() as stack:
        m = Mem(nc, stack)
        R = 32 * B
        select = m.sb("bd_select", [P, KC, 32], BF16)
        key_mean = m.sb("bd_key_mean", [P, KC, B, 32], BF16)
        mean = m.sb("bd_mean", [P, KC, B], F32)
        longest = m.sb("bd_longest", [R, 1], F32)
        bound = m.sb("bd_bound", [R, S], F32)
        negmid = m.sb("bd_negmid", [R, S], BF16)
        zeros = m.sb("bd_zeros", [BH, (PARTS - 1) * S], BF16)
        widest = m.sb("bd_widest", [P, 1], F32)
        narrow = m.sb("bd_narrow", [P, 1], BF16)
        ones = m.sb("bd_ones", [P, P], BF16)
        p_q = m.ps("bd_pq", [P, S])
        p_k = m.ps("bd_pk", [P, S])
        filled = m.sem("bd_filled")
        selected = m.sem("bd_selected")
        zeroed = m.sem("bd_zeroed")
        step = m.sem("bd_step")
        mean_ready = m.sem("bd_mean_ready")
        k_normed = m.sem("bd_k_normed")
        q_normed = m.sem("bd_q_normed")
        longest_ready = m.sem("bd_longest_ready")
        averaged = m.sem("bd_averaged")
        bound_ready = m.sem("bd_bound_ready")
        mid_ready = m.sem("bd_mid_ready")
        narrow_ready = m.sem("bd_narrow_ready")
        counted = m.sem("bd_counted")
        stored = m.sem("bd_stored")

        with nc.Block() as block:

            @block.gpsimd
            def _(pool):
                nc.gpsimd.memset(select[:, :, :], 1.0).then_inc(filled, 1)
                for kc in range(KC):
                    pool.wait_ge(filled, 2 * kc + 1)
                    nc.gpsimd.affine_select(out=select[:, kc, :], in_=select[:, kc, :], compare_op=ALU.is_ge,
                                            fill=0.0, base=P * kc, pattern=[[-HD, 32]], channel_multiplier=1
                                            ).then_inc(filled, 1)
                    pool.wait_ge(filled, 2 * kc + 2)
                    nc.gpsimd.affine_select(out=select[:, kc, :], in_=select[:, kc, :], compare_op=ALU.is_ge,
                                            fill=0.0, base=HD - 1 - P * kc, pattern=[[HD, 32]],
                                            channel_multiplier=-1).then_inc(filled, 1)
                pool.wait_ge(filled, 5)
                pool.sem_inc(selected, 1)

            @block.sync
            def _(sp):
                sp.wait_ge(zeroed, 1)
                sp.dma_start(dram["negmax"][:, 1:, :].rearrange("h t n -> h (t n)"), zeros[:, :]).then_inc(stored, 16)
                sp.wait_ge(mid_ready, 1)
                for b in range(B):
                    sp.dma_start(dram["negmax"][b * H:(b + 1) * H, 0, :], negmid[32 * b:32 * b + H, :]
                                 ).then_inc(stored, 16)
                sp.wait_ge(stored, 16 * (1 + B))

            @block.tensor
            def _(pe):
                def per_head(dst, b, weights, moving, sem):
                    for c in range(QC):
                        tok = slice(b * S + c * 512, b * S + (c + 1) * 512)
                        for kc in range(KC):
                            last = nc.tensor.matmul(dst[32 * b:32 * b + 32, c * 512:(c + 1) * 512],
                                                    weights(kc, b), moving(kc, tok),
                                                    start=(kc == 0), stop=(kc == KC - 1))
                    last.then_inc(sem, 1)

                pe.wait_ge(selected, 1)
                for b in range(B):
                    per_head(p_k, b, lambda kc, b: select[:, kc, :], lambda kc, t: squares[:, 2 + kc, t], k_normed)
                for b in range(B):
                    per_head(p_q, b, lambda kc, b: select[:, kc, :], lambda kc, t: squares[:, kc, t], q_normed)
                pe.wait_ge(longest_ready, 1)
                pe.wait_ge(mean_ready, 1)
                for b in range(B):
                    per_head(p_k, b, lambda kc, b: key_mean[:, kc, b, :], lambda kc, t: hi_all[:, kc, t], averaged)
                pe.wait_ge(narrow_ready, 1)
                nc.tensor.matmul(p_q[:, 0:1], ones[:, :], narrow[:, :], start=True, stop=True).then_inc(counted, 1)

            @block.scalar
            def _(act):
                act.wait_ge(longest_ready, 1)
                act.wait_ge(q_normed, B)
                nc.scalar.activation(bound[:, :], p_q[0:R, :], ACT.Sqrt, scale=longest[:, 0:1]
                                     ).then_inc(bound_ready, 1)

            @block.vector
            def _(dve):
                v = nc.vector
                steps = Chain(dve, step)
                v.memset(zeros[:, :].bitcast(U32), 0).then_inc(zeroed, 1)
                v.memset(ones[:, :], 1.0)
                v.memset(widest[:, :], 0.0)
                steps.then(v.tensor_reduce(mean[:, :, :], key_sum[:, :, :].rearrange("p k (b c) -> p k b c", b=B),
                                           AX.X, ALU.add))
                steps.then(v.tensor_scalar(mean[:, :, :], mean[:, :, :], -0.5 / S, None, ALU.mult))
                dve.wait_ge(selected, 1)
                for kc in range(KC):
                    for b in range(B):
                        last = v.tensor_scalar(key_mean[:, kc, b, :], select[:, kc, :], mean[:, kc, b:b + 1], None,
                                               ALU.mult)
                last.then_inc(mean_ready, 1)
                dve.wait_ge(k_normed, B)
                v.tensor_reduce(longest[:, :], p_k[0:R, :], AX.X, ALU.max).then_inc(longest_ready, 1)
                dve.wait_ge(bound_ready, 1)
                dve.wait_ge(averaged, B)
                v.scalar_tensor_tensor(negmid[:, :], bound[:, :], -0.5, p_k[0:R, :], ALU.mult, ALU.add
                                       ).then_inc(mid_ready, 1)
                steps.then(v.scalar_tensor_tensor(bound[:, :], p_k[0:R, :], 2.0, bound[:, :], ALU.mult, ALU.add))
                steps.then(v.tensor_reduce(widest[0:R, :], bound[:, :], AX.X, ALU.max))
                v.tensor_scalar(narrow[:, :], widest[:, :], GAP, None, ALU.is_le).then_inc(narrow_ready, 1)
                dve.wait_ge(counted, 1)
                v.tensor_scalar(keep["wide"][:, :], p_q[:, 0:1], -1.0, float(P), ALU.mult, ALU.add
                                ).then_inc(keep["wide_ready"], 1)


def inverse_root(dve, steps, out, var, w):
    v, half, y = dve, w["half"], out
    steps.then(v.tensor_scalar(w["bits"], var.bitcast(I32), 1, None, ALU.logical_shift_right))
    steps.then(v.tensor_scalar(y.bitcast(I32), w["bits"], -1.0, float(0x5F3759DF), ALU.mult, ALU.add))
    steps.then(v.tensor_scalar(half, var, -0.5, None, ALU.mult))
    for _ in range(4):
        steps.then(v.tensor_tensor(w["t"], y, y, ALU.mult))
        steps.then(v.tensor_tensor(w["t"], w["t"], half, ALU.mult))
        steps.then(v.scalar_tensor_tensor(w["t"], w["t"], 0.5, y, ALU.add, ALU.mult))
        steps.then(v.tensor_tensor(y, y, w["t"], ALU.add))


LN_STEPS = 1 + 4 + 3 + 4 * 4 + 1 + 1


def layer_norm(dve, steps, out, inp, w):
    for a in range(GT):
        last = dve.bn_stats(w["stats"][:, a, :], inp[:, a, :])
    steps.then(last)
    stats = w["stats"]
    dve.tensor_tensor(w["apart"], stats[:, :, 1], stats[:, :, 4], ALU.subtract)
    dve.tensor_tensor(w["mean2"], stats[:, :, 1], stats[:, :, 4], ALU.add)
    steps.then(dve.tensor_tensor(w["var"], stats[:, :, 2], stats[:, :, 5], ALU.add))
    steps.then(dve.scalar_tensor_tensor(w["apart"], w["apart"], 0.25, w["apart"], ALU.mult, ALU.mult))
    steps.then(dve.scalar_tensor_tensor(w["var"], w["var"], 1.0 / D, w["apart"], ALU.mult, ALU.add))
    steps.then(dve.tensor_scalar(w["var"], w["var"], EPS, None, ALU.add))
    inverse_root(dve, steps, w["rstd"], w["var"], w)
    steps.then(dve.scalar_tensor_tensor(w["shift"], w["mean2"], -0.5, w["rstd"], ALU.mult, ALU.mult))
    for a in range(GT):
        last = dve.tensor_scalar(out[:, a, :], inp[:, a, :], w["rstd"][:, a:a + 1], w["shift"][:, a:a + 1],
                                 ALU.mult, ALU.add)
    steps.then(last)


def norm_scratch(m, name):
    w = {"stats": m.sb(name + "_stats", [P, GT, 6], F32),
         "bits": m.sb(name + "_bits", [P, GT], I32)}
    for n in ("var", "apart", "mean2", "rstd", "shift", "half", "t"):
        w[n] = m.sb(f"{name}_{n}", [P, GT], F32)
    return {n: t[tuple(slice(None) for _ in t.shape)] for n, t in w.items()}


def route(nc, dram, keep):
    with ExitStack() as stack:
        m = Mem(nc, stack)
        out_w = m.sb("rt_out_w", [P, KC, D], F32)
        mix_w = m.sb("rt_mix_w", [P, KC, D], F32)
        router_w = m.sb("rt_router_w", [P, KC, E], F32)
        rows = {n: m.sb("rt_" + n, [P, D], F32) for n in ("out_b", "g1", "be1", "mix_b", "g2", "be2")}
        x_in = m.sb("rt_x_in", [P, 2, GT, D], F32)
        a_nat = m.sb("rt_a_nat", [P, GT, D], F32)
        z = m.sb("rt_z", [P, GT, D], F32)
        x1 = m.sb("rt_x1", [P, GT, D], F32)
        norm1 = m.sb("rt_norm1", [P, GT, D], F32)
        total = m.sb("rt_total", [P, GT, D], F32)
        x2 = m.sb("rt_x2", [P, GT, D], F32)
        norm2 = m.sb("rt_norm2", [P, GT, D], F32)
        turned = m.sb("rt_turned", [P, KC, 512], F32)
        w = norm_scratch(m, "rt_ln")
        logit = m.sb("rt_logit", [P, GT, E], F32)
        lmax = m.sb("rt_lmax", [P, GT], F32)
        prob = m.sb("rt_prob", [P, GT, E], F32)
        psum_ = m.sb("rt_psum", [P, GT], F32)
        top = m.sb("rt_top", [P, GT, 8], F32)
        top_i = m.sb("rt_top_i", [P, GT, 8], U32)
        top_f = m.sb("rt_top_f", [P, 2, GT], F32)
        chosen = m.sb("rt_chosen", [P, 2, GT, E], F32)
        both = m.sb("rt_both", [P, GT, E], BF16)
        place = m.sb("rt_place", [P, GT, E], F32)
        picked = m.sb("rt_picked", [P, 2, GT, E], F32)
        pos_f = m.sb("rt_pos_f", [P, 2, GT], F32)
        pos = m.sb("rt_pos", [P, 2, GT], U32)
        iota_e = m.sb("rt_iota_e", [P, E], F32)
        lower = m.sb("rt_lower", [P, P], BF16)
        ones = m.sb("rt_ones", [P, P], BF16)
        zero_rows = m.sb("rt_zero_rows", [P, D], F32)
        spare = m.sb("rt_spare", [P, 1], F32)
        p_t = m.ps("rt_pt", [P, KC, 512])
        p_y = m.ps("rt_py", [P, GT, D])
        p_r = m.ps("rt_pr", [P, GT, E])
        p_c = m.ps("rt_pc", [P, 2, GT, E])
        carry = keep["carry"]

        loaded_w = m.sem("rt_loaded_w")
        loaded_x = [m.sem(f"rt_loaded_x{u}") for u in range(2)]
        constants_ready = m.sem("rt_constants_ready")
        step = m.sem("rt_step")
        copied = m.sem("rt_copied")
        x_biased = m.sem("rt_x_biased")
        turned_done = m.sem("rt_turned_done")
        evac_a = m.sem("rt_evac_a")
        evac_d = m.sem("rt_evac_d")
        projected = m.sem("rt_projected")
        norm1_ready = m.sem("rt_norm1_ready")
        total_ready = m.sem("rt_total_ready")
        x2_ready = m.sem("rt_x2_ready")
        kept = m.sem("rt_kept")
        norm2_ready = m.sem("rt_norm2_ready")
        logits_done = m.sem("rt_logits_done")
        shifted = m.sem("rt_shifted")
        exp_done = m.sem("rt_exp_done")
        both_ready = m.sem("rt_both_ready")
        counted = m.sem("rt_counted")
        placed = m.sem("rt_placed")
        scattered = m.sem("rt_scattered")
        sent = m.sem("rt_sent")
        rows_zeroed = m.sem("rt_rows_zeroed")
        padded = m.sem("rt_padded")
        mapped = m.sem("rt_mapped")
        made = m.sem("rt_made")
        scratch = {"iota_e": iota_e, "iota_t": m.sb("rt_iota_t", [P, TILES], F32),
                   "tiles_i": m.sb("rt_tiles_i", [P, E], I32), "last": m.sb("rt_last", [P, 1], F32),
                   "tile": m.sb("rt_tile", [P, TILES], F32), "row": m.sb("rt_row", [P, TILES], F32),
                   "behind": m.sb("rt_behind", [P, 2 * NT, E - 1], F32),
                   "unused": m.sb("rt_unused", [P, 2 * NT], F32),
                   "passed": m.sb("rt_passed", [P, TILES, E], F32)}
        scratch.update({n: m.sb("rt_" + n, [P, E], F32) for n in ("count", "tiles", "cum", "cum2")})
        x_rows = dram["x"].rearrange("b s c -> (b s) c")
        STEPS = 3 * LN_STEPS + 25

        def kept_view(g):
            b, c = g
            return keep["attn"][:, bass.ds(b * H, H), c * GT:(c + 1) * GT, :].rearrange("p h a w -> p a h w")

        def heads(tile):
            return tile.rearrange("p a (h w) -> p a h w", w=HD)

        def spread(name):
            return rows[name][:, :].unsqueeze(1).broadcast_to([P, GT, D])

        with nc.Block() as block:

            @block.sync
            def _(sp):
                for dst, src in ((out_w, "out_w"), (mix_w, "mix_w"), (router_w, "router_w")):
                    sp.dma_start(dst[:, :, :], dram[src].rearrange("(s p) n -> p s n", p=P)).then_inc(loaded_w, 16)
                for name in rows:
                    sp.dma_start(rows[name][:, :], dram[name].partition_broadcast(P)).then_inc(loaded_w, 16)
                sp.sem_inc(x_biased, 2)
                with sp.Fori(0, B) as b:
                    for c in range(QC):
                        sp.wait_ge(x_biased, b * QC + c + 1)
                        sp.dma_start(x_in[:, c % 2, :, :],
                                     x_rows[bass.ds((b * QC + c) * 512, 512), :].rearrange("(a p) n -> p a n", p=P)
                                     ).then_inc(loaded_x[c % 2], 16)
                sp.wait_ge(mapped, 1)
                sp.wait_ge(sent, GROUPS + 1)
                sp.wait_ge(rows_zeroed, 1)
                for e in range(E):
                    end = sp.value_load(keep["ends"][0:1, e:e + 1], min_val=0, max_val=E * REGION - P)
                    sp.dma_start(dram["rows_in"][bass.ds(end, P), :], zero_rows[:, :]).then_inc(padded, 16)
                sp.wait_ge(padded, 16 * E)

            @block.gpsimd
            def _(pool):
                nc.gpsimd.iota(iota_e[:, :], pattern=[[1, E]], base=0, channel_multiplier=0,
                               allow_small_or_imprecise_dtypes=True).then_inc(constants_ready, 1)
                nc.gpsimd.iota(scratch["iota_t"][:, :], pattern=[[1, TILES]], base=0, channel_multiplier=0,
                               allow_small_or_imprecise_dtypes=True)
                nc.gpsimd.memset(ones[:, :], 1.0).then_inc(constants_ready, 1)
                nc.gpsimd.memset(zero_rows[:, :], 0.0).then_inc(rows_zeroed, 1)
                pool.wait_ge(constants_ready, 2)
                nc.gpsimd.affine_select(out=lower[:, :], in_=ones[:, :], compare_op=ALU.is_gt, fill=0.0,
                                        base=0, pattern=[[1, P]], channel_multiplier=-1
                                        ).then_inc(constants_ready, 1)
                pool.wait_ge(loaded_w, 16 * 9)
                pool.sem_inc(kept, 1)
                pool.sem_inc(sent, 1)
                with pool.Fori(0, B) as b:
                    for c in range(QC):
                        g = b * QC + c
                        pool.wait_ge(loaded_x[c % 2], b * (16 * QC // 2) + 16 * (c // 2 + 1))
                        nc.gpsimd.tensor_tensor(total[:, :, :], x_in[:, c % 2, :, :], spread("out_b"), ALU.add
                                                ).then_inc(x_biased, 1)
                        pool.wait_ge(norm1_ready, g + 1)
                        nc.gpsimd.tensor_tensor(total[:, :, :], x1[:, :, :], norm1[:, :, :], ALU.add
                                                ).then_inc(total_ready, 1)
                        pool.wait_ge(total_ready, g * 2 + 1)
                        nc.gpsimd.tensor_tensor(total[:, :, :], total[:, :, :], spread("mix_b"), ALU.add
                                                ).then_inc(total_ready, 1)
                        pool.wait_ge(x2_ready, g + 1)
                        pool.wait_ge(placed, g + 1)
                        nc.gpsimd.tensor_tensor(kept_view((b, c)), heads(x1[:, :, :]), heads(x2[:, :, :]), ALU.add
                                                ).then_inc(kept, 1)
                        for n in range(2):
                            for a in range(GT):
                                nc.gpsimd.indirect_dma_start(
                                    out=dram["rows_in"], in_=norm2[:, a, :], in_offset=None,
                                    out_offset=bass.IndirectOffsetOnAxis(ap=pos[:, n, a:a + 1], axis=0)
                                ).then_inc(scattered, 16)
                        pool.wait_ge(scattered, (g + 1) * (16 * 2 * GT))
                        pool.sem_inc(sent, 1)

            @block.scalar
            def _(act):
                act.sem_inc(evac_a, 3)
                with act.Fori(0, B) as b:
                    for c in range(QC):
                        g = b * QC + c
                        nc.scalar.activation(heads(a_nat[:, :, :]), kept_view((b, c)), ACT.Identity
                                             ).then_inc(copied, 1)
                        for n in range(3):
                            act.wait_ge(turned_done, g * 6 + 2 * n + 1)
                            nc.scalar.activation(turned[:, 0, :], p_t[:, 0, :], ACT.Identity).then_inc(evac_a, 1)
                        act.wait_ge(shifted, g + 1)
                        nc.scalar.activation(prob[:, :, :], logit[:, :, :], ACT.Exp).then_inc(exp_done, 1)

            @block.tensor
            def _(pe):
                def turn(src, g, n):
                    for kc in range(KC):
                        pe.wait_ge([evac_a, evac_d][kc], g * 3 + n + 3)
                        for a in range(GT):
                            last = nc.tensor.transpose(p_t[:, kc, a * P:(a + 1) * P], src[:, a, kc * P:(kc + 1) * P],
                                                       keep["identity"][:, :])
                        last.then_inc(turned_done, 1)
                    for kc in range(KC):
                        pe.wait_ge([evac_a, evac_d][kc], g * 3 + n + 4)

                def product(dst, weights):
                    for a in range(GT):
                        for kc in range(KC):
                            last = nc.tensor.matmul(dst[:, a, :], turned[:, kc, a * P:(a + 1) * P],
                                                    weights[:, kc, :], start=(kc == 0), stop=(kc == KC - 1))
                    return last

                pe.wait_ge(loaded_w, 16 * 9)
                pe.wait_ge(constants_ready, 3)
                with pe.Fori(0, B) as b:
                    for c in range(QC):
                        g = b * QC + c
                        pe.wait_ge(copied, g + 1)
                        turn(a_nat, g, 0)
                        product(p_y, out_w).then_inc(projected, 1)
                        pe.wait_ge(norm1_ready, g + 1)
                        turn(norm1, g, 1)
                        product(p_y, mix_w).then_inc(projected, 1)
                        pe.wait_ge(norm2_ready, g + 1)
                        turn(norm2, g, 2)
                        product(p_r, router_w).then_inc(logits_done, 1)
                        pe.wait_ge(both_ready, g + 1)
                        nc.tensor.matmul(p_c[:, 0, :, :], lower[:, :], both[:, :, :], start=True, stop=True)
                        nc.tensor.matmul(p_c[:, 1, :, :], ones[:, :], both[:, :, :], start=True, stop=True,
                                         skip_group_check=True).then_inc(counted, 1)

            @block.vector
            def _(dve):
                v = nc.vector
                dve.wait_ge(constants_ready, 3)
                v.tensor_scalar(carry[:, :], iota_e[:, :], float(REGION), None, ALU.mult).then_inc(step, 1)
                dve.wait_ge(step, 1)
                dve.wait_ge(loaded_w, 16 * 9)
                dve.sem_inc(evac_d, 3)
                with dve.Fori(0, B) as b:
                    for c in range(QC):
                        g = b * QC + c
                        steps = Chain(dve, step, b * (STEPS * QC) + STEPS * c + 1)

                        def evacuate(n):
                            dve.wait_ge(turned_done, g * 6 + 2 * n + 2)
                            v.tensor_copy(turned[:, 1, :], p_t[:, 1, :]).then_inc(evac_d, 1)

                        evacuate(0)
                        dve.wait_ge(projected, g * 2 + 1)
                        dve.wait_ge(x_biased, g + 1 + 2)
                        steps.then(v.tensor_tensor(z[:, :, :], p_y[:, :, :], total[:, :, :], ALU.add))
                        dve.wait_ge(kept, g + 1)
                        layer_norm(v, steps, x1, z, w)
                        layer_norm(v, steps, norm1, x1, w)
                        steps.then(v.tensor_tensor(norm1[:, :, :], norm1[:, :, :], spread("g1"), ALU.mult))
                        v.tensor_tensor(norm1[:, :, :], norm1[:, :, :], spread("be1"), ALU.add
                                        ).then_inc(norm1_ready, 1)
                        evacuate(1)
                        dve.wait_ge(projected, g * 2 + 2)
                        dve.wait_ge(total_ready, g * 2 + 2)
                        v.tensor_tensor(x2[:, :, :], p_y[:, :, :], total[:, :, :], ALU.add).then_inc(x2_ready, 1)
                        dve.wait_ge(x2_ready, g + 1)
                        dve.wait_ge(sent, g + 1)
                        layer_norm(v, steps, norm2, x2, w)
                        steps.then(v.tensor_tensor(norm2[:, :, :], norm2[:, :, :], spread("g2"), ALU.mult))
                        v.tensor_tensor(norm2[:, :, :], norm2[:, :, :], spread("be2"), ALU.add
                                        ).then_inc(norm2_ready, 1)
                        evacuate(2)
                        dve.wait_ge(logits_done, g + 1)
                        steps.then(v.tensor_reduce(lmax[:, :], p_r[:, :, :], AX.X, ALU.max))
                        v.tensor_tensor(logit[:, :, :], p_r[:, :, :],
                                        lmax[:, :].unsqueeze(2).broadcast_to([P, GT, E]), ALU.subtract
                                        ).then_inc(shifted, 1)
                        dve.wait_ge(exp_done, g + 1)
                        steps.then(v.tensor_reduce(psum_[:, :], prob[:, :, :], AX.X, ALU.add))
                        steps.then(v.reciprocal(psum_[:, :], psum_[:, :]))
                        steps.then(v.tensor_tensor(prob[:, :, :], prob[:, :, :],
                                                   psum_[:, :].unsqueeze(2).broadcast_to([P, GT, E]), ALU.mult))
                        v.tensor_copy(spare[:, :], prob[:, 0, 0:1])
                        for a in range(GT):
                            last = v.max(top[:, a, :], prob[:, a, :])
                        steps.then(last)
                        v.tensor_copy(spare[:, :], prob[:, 0, 0:1])
                        for a in range(GT):
                            last = v.max_index(top_i[:, a, :], top[:, a, :], prob[:, a, :])
                        steps.then(last)
                        steps.then(v.tensor_copy(keep["weight"][:, bass.ds(g, 1), :, :]
                                                 .rearrange("p o n a -> p (o n) a"),
                                                 top[:, :, 0:2].rearrange("p a n -> p n a")))
                        steps.then(v.tensor_copy(top_f[:, :, :], top_i[:, :, 0:2].rearrange("p a n -> p n a")))
                        for n in range(2):
                            steps.then(v.tensor_tensor(chosen[:, n, :, :],
                                                       iota_e[:, :].unsqueeze(1).broadcast_to([P, GT, E]),
                                                       top_f[:, n, :].unsqueeze(2).broadcast_to([P, GT, E]),
                                                       ALU.is_equal))
                        v.tensor_tensor(both[:, :, :], chosen[:, 0, :, :], chosen[:, 1, :, :], ALU.add
                                        ).then_inc(both_ready, 1)
                        dve.wait_ge(counted, g + 1)
                        for a in range(GT):
                            steps.then(v.tensor_tensor(place[:, a, :], p_c[:, 0, a, :], carry[:, :], ALU.add))
                            steps.then(v.tensor_tensor(carry[:, :], carry[:, :], p_c[:, 1, a, :], ALU.add))
                        for n in range(2):
                            steps.then(v.tensor_tensor(picked[:, n, :, :], chosen[:, n, :, :], place[:, :, :],
                                                       ALU.mult))
                        steps.then(v.tensor_reduce(pos_f[:, :, :], picked[:, :, :, :], AX.X, ALU.add))
                        steps.then(v.tensor_copy(keep["place"][:, bass.ds(g, 1), :, :]
                                                 .rearrange("p o n a -> p (o n) a"), pos_f[:, :, :]))
                        v.tensor_copy(pos[:, :, :], pos_f[:, :, :]).then_inc(placed, 1)
                        assert steps.n == STEPS, steps.n
                plan(nc, dve, m, carry, keep, scratch, made, mapped)


def plan(nc, dve, m, carry, keep, scratch, made, mapped):
    v = nc.vector
    steps = Chain(dve, made)
    iota_e, iota_t = scratch["iota_e"], scratch["iota_t"]
    count, tiles_i, tiles, cum, cum2, last, tile = (scratch[n] for n in (
        "count", "tiles_i", "tiles", "cum", "cum2", "last", "tile"))
    passed, row = scratch["passed"], scratch["row"]
    steps.then(v.tensor_copy(keep["ends"][:, :], carry[:, :]))
    steps.then(v.scalar_tensor_tensor(count[:, :], iota_e[:, :], -float(REGION), carry[:, :], ALU.mult, ALU.add))
    steps.then(v.tensor_scalar(tiles_i[:, :], count[:, :], float(P - 1), None, ALU.add))
    steps.then(v.tensor_scalar(tiles_i[:, :], tiles_i[:, :], 7, None, ALU.logical_shift_right))
    steps.then(v.tensor_copy(tiles[:, :], tiles_i[:, :]))
    steps.then(v.tensor_copy(cum[:, :], tiles[:, :]))
    for k in (1, 2, 4):
        steps.then(v.tensor_copy(cum2[:, 0:k], cum[:, 0:k]))
        steps.then(v.tensor_tensor(cum2[:, k:], cum[:, k:], cum[:, 0:E - k], ALU.add))
        cum, cum2 = cum2, cum
    steps.then(v.tensor_scalar(last[:, :], cum[:, E - 1:E], -1.0, None, ALU.add))
    steps.then(v.tensor_scalar(tile[:, :], iota_t[:, :], last[:, 0:1], None, ALU.min))
    steps.then(v.tensor_tensor(passed[:, :, :], cum[:, :].unsqueeze(1).broadcast_to([P, TILES, E]),
                               tile[:, :].unsqueeze(2).broadcast_to([P, TILES, E]), ALU.is_le))
    steps.then(v.tensor_reduce(row[:, :], passed[:, :, :], AX.X, ALU.add))
    steps.then(v.tensor_copy(keep["tile_expert"][:, :], row[:, :]))
    steps.then(v.tensor_scalar(count[:, :], tiles[:, :], -float(P), float(REGION), ALU.mult, ALU.add))
    steps.then(v.tensor_tensor(passed[:, :, :], passed[:, :, :],
                               count[:, :].unsqueeze(1).broadcast_to([P, TILES, E]), ALU.mult))
    steps.then(v.tensor_reduce(row[:, :], passed[:, :, :], AX.X, ALU.add))
    steps.then(v.scalar_tensor_tensor(row[:, :], tile[:, :], float(P), row[:, :], ALU.mult, ALU.add))
    steps.then(v.tensor_copy(keep["tile_row"][:, :], row[:, :]))
    steps.then(v.tensor_scalar(cum[:, :], iota_e[:, :], float(REGION), None, ALU.mult))
    n = 2 * NT
    place = keep["place"][:, :, :, :].rearrange("p g n a -> p (g n a)")
    steps.then(v.tensor_tensor(scratch["behind"][:, :, :], place.unsqueeze(2).broadcast_to([P, n, E - 1]),
                               cum[:, 1:].unsqueeze(1).broadcast_to([P, n, E - 1]), ALU.is_ge))
    steps.then(v.tensor_tensor(scratch["behind"][:, :, :], scratch["behind"][:, :, :],
                               count[:, 0:E - 1].unsqueeze(1).broadcast_to([P, n, E - 1]), ALU.mult))
    steps.then(v.tensor_reduce(scratch["unused"][:, :], scratch["behind"][:, :, :], AX.X, ALU.add))
    steps.then(v.tensor_tensor(place, place, scratch["unused"][:, :], ALU.subtract))
    v.tensor_copy(keep["pos"][:, :, :, :].rearrange("p g n a -> p (g n a)"), place).then_inc(mapped, 1)


def experts(nc, dram, keep):
    FC = F // P
    with ExitStack() as stack:
        m = Mem(nc, stack)
        w2 = m.sb("ex_w2", [P, E, FC, D], F32)
        b1_rows = m.sb("ex_b1_rows", [P, E, F], BF16)
        b2_rows = m.sb("ex_b2_rows", [P, E, D], BF16)
        ones = m.sb("ex_ones", [P, P], BF16)
        x_in = m.sb("ex_x_in", [P, 2, D], F32)
        xT = m.sb("ex_xT", [P, 2, KC, P], F32)
        h = m.sb("ex_h", [P, 2, F], F32)
        hT = m.sb("ex_hT", [P, FC, P], F32)
        y = m.sb("ex_y", [P, 2, D], F32)
        p_x = m.ps("ex_px", [P, KC, P])
        p_h = [m.ps(f"ex_ph{u}", [P, F]) for u in range(2)]
        p_t = m.ps("ex_pt", [P, FC, P])
        p_y = m.ps("ex_py", [P, D])
        loaded_w = m.sem("ex_loaded_w")
        zeroed = m.sem("ex_zeroed")
        ones_ready = m.sem("ex_ones_ready")
        b_placed = m.sem("ex_b_placed")
        loaded_x = [m.sem(f"ex_loaded_x{u}") for u in range(2)]
        x_turned = m.sem("ex_x_turned")
        xT_ready = m.sem("ex_xT_ready")
        hidden = m.sem("ex_hidden")
        h_ready = m.sem("ex_h_ready")
        h_turned = m.sem("ex_h_turned")
        hT_a = m.sem("ex_hT_a")
        hT_d = m.sem("ex_hT_d")
        y_done = m.sem("ex_y_done")
        y_ready = m.sem("ex_y_ready")
        stored = m.sem("ex_stored")
        y_free = m.sem("ex_y_free")
        identity = keep["identity"]

        with nc.Block() as block:

            @block.sync
            def _(sp):
                for e in range(E):
                    sp.dma_start(keep["w1"][:, e, :, :], dram["w1"][e].rearrange("(s p) n -> p s n", p=P)
                                 ).then_inc(loaded_w, 16)
                    sp.dma_start(w2[:, e, :, :], dram["w2"][e].rearrange("(s p) n -> p s n", p=P)
                                 ).then_inc(loaded_w, 16)
                sp.wait_ge(zeroed, 2)
                for t in range(PARTS):
                    sp.dma_start(b1_rows[t:t + 1, :, :], dram["b_parts"][t:t + 1, :, 0:F]).then_inc(b_placed, 16)
                    sp.dma_start(b2_rows[t:t + 1, :, :], dram["b_parts"][t:t + 1, :, F:]).then_inc(b_placed, 16)
                sp.sem_inc(x_turned, 2)
                with sp.Fori(0, TILES // 2) as pair:
                    for u in range(2):
                        row = sp.value_load(keep["tile_row"][0:1, bass.ds(pair * 2 + u, 1)], min_val=0,
                                            max_val=E * REGION - P)
                        sp.wait_ge(x_turned, pair * 2 + u + 1)
                        sp.dma_start(x_in[:, u, :], dram["rows_in"][bass.ds(row, P), :]).then_inc(loaded_x[u], 16)

            @block.gpsimd
            def _(pool):
                nc.gpsimd.memset(b1_rows[:, :, :], 0.0).then_inc(zeroed, 1)
                nc.gpsimd.memset(b2_rows[:, :, :], 0.0).then_inc(zeroed, 1)
                pool.sem_inc(y_free, 2)
                with pool.Fori(0, TILES // 2) as pair:
                    for u in range(2):
                        pool.wait_ge(y_ready, pair * 2 + u + 2)
                        pool.dma_start(dram["rows_out"][bass.ds((pair * 2 + u) * P, P), :], y[:, u, :]).then_inc(stored, 16)
                        pool.wait_ge(stored, pair * 32 + 16 * (u + 1))
                        pool.sem_inc(y_free, 1)

            @block.scalar
            def _(act):
                act.sem_inc(hT_a, 1)
                with act.Fori(0, TILES // 2) as pair:
                    for u in range(2):
                        act.wait_ge(hidden, pair * 2 + u + 1)
                        act.wait_ge(h_turned, pair * 2 + u + 1)
                        nc.scalar.activation(h[:, u, :], p_h[u][:, :], ACT.Silu).then_inc(h_ready, 1)
                        act.wait_ge(h_turned, pair * 2 + u + 3)
                        nc.scalar.activation(hT[:, 0:FC // 2, :], p_t[:, 0:FC // 2, :], ACT.Identity
                                             ).then_inc(hT_a, 1)

            @block.vector
            def _(dve):
                v = nc.vector
                v.memset(ones[:, :], 1.0).then_inc(ones_ready, 1)
                dve.sem_inc(hT_d, 1)
                dve.sem_inc(y_ready, 1)
                dve.wait_ge(x_turned, 3)
                v.tensor_copy(xT[:, 0, :, :], p_x[:, :, :]).then_inc(xT_ready, 1)
                dve.wait_ge(x_turned, 4)
                v.tensor_copy(xT[:, 1, :, :], p_x[:, :, :]).then_inc(xT_ready, 1)

                def tile(pair, u, is_last):
                    i = pair * 2 + u
                    dve.wait_ge(h_turned, i + 3)
                    v.tensor_copy(hT[:, FC // 2:, :], p_t[:, FC // 2:, :]).then_inc(hT_d, 1)
                    dve.wait_ge(y_done, i + 1)
                    dve.wait_ge(y_free, i + 1)
                    v.tensor_copy(y[:, u, :], p_y[:, :]).then_inc(y_ready, 1)
                    if not is_last:
                        dve.wait_ge(x_turned, i + 5)
                        v.tensor_copy(xT[:, u, :, :], p_x[:, :, :]).then_inc(xT_ready, 1)

                with dve.Fori(0, TILES // 2 - 1) as pair:
                    for u in range(2):
                        tile(pair, u, False)
                for u in range(2):
                    tile(TILES // 2 - 1, u, True)

            @block.tensor
            def _(pe):
                def turn_x(pair, u, i):
                    pe.wait_ge(loaded_x[u], pair * 16 + 16)
                    if not (isinstance(i, int) and i == 0):
                        pe.wait_ge(xT_ready, i)
                    for kc in range(KC):
                        last = nc.tensor.transpose(p_x[:, kc, :], x_in[:, u, kc * P:(kc + 1) * P], identity[:, :])
                    last.then_inc(x_turned, 1)

                def hide(u, i):
                    e = pe.value_load(keep["tile_expert"][0:1, bass.ds(i, 1)], min_val=0, max_val=E - 1)
                    pe.wait_ge(xT_ready, i + 1)
                    for c in range(F // 512):
                        cut = slice(c * 512, (c + 1) * 512)
                        nc.tensor.matmul(p_h[u][:, cut], ones[:, :],
                                         b1_rows[:, bass.ds(e, 1), cut].rearrange("p o n -> p (o n)"),
                                         start=True, stop=False)
                        for kc in range(KC):
                            last = nc.tensor.matmul(p_h[u][:, cut], xT[:, u, kc, :],
                                                    keep["w1"][:, bass.ds(e, 1), kc, cut]
                                                    .rearrange("p o n -> p (o n)"),
                                                    start=False, stop=(kc == KC - 1))
                    last.then_inc(hidden, 1)
                    return e

                def turn_h(u, i):
                    pe.wait_ge(h_ready, i + 1)
                    pe.wait_ge(hT_a, i + 1)
                    pe.wait_ge(hT_d, i + 1)
                    for fc in range(FC):
                        last = nc.tensor.transpose(p_t[:, fc, :], h[:, u, fc * P:(fc + 1) * P], identity[:, :])
                    last.then_inc(h_turned, 1)

                def reduce(i):
                    e = pe.value_load(keep["tile_expert"][0:1, bass.ds(i, 1)], min_val=0, max_val=E - 1)
                    pe.wait_ge(hT_a, i + 2)
                    pe.wait_ge(hT_d, i + 2)
                    pe.wait_ge(y_ready, i + 1)
                    nc.tensor.matmul(p_y[:, :], ones[:, :],
                                     b2_rows[:, bass.ds(e, 1), :].rearrange("p o n -> p (o n)"),
                                     start=True, stop=False)
                    for fc in range(FC):
                        last = nc.tensor.matmul(p_y[:, :], hT[:, fc, :],
                                                w2[:, bass.ds(e, 1), fc, :].rearrange("p o n -> p (o n)"),
                                                start=False, stop=(fc == FC - 1))
                    last.then_inc(y_done, 1)

                def tile(pair, u, is_last):
                    i = pair * 2 + u
                    turn_h(u, i)
                    if not (is_last and u == 1):
                        hide(1 - u, i + 1)
                    reduce(i)
                    if not is_last:
                        turn_x(pair + 1, u, i + 2)

                pe.sem_inc(h_turned, 2)
                pe.wait_ge(ones_ready, 1)
                pe.wait_ge(b_placed, 16 * 2 * PARTS)
                pe.wait_ge(loaded_w, 16 * 2 * E)
                turn_x(0, 0, 0)
                turn_x(0, 1, 1)
                hide(0, 0)
                with pe.Fori(0, TILES // 2 - 1) as pair:
                    for u in range(2):
                        tile(pair, u, False)
                for u in range(2):
                    tile(TILES // 2 - 1, u, True)


def combine(nc, dram, keep):
    with ExitStack() as stack:
        m = Mem(nc, stack)
        got = m.sb("cb_got", [P, 2, 2, GT, D], F32)
        pos = m.sb("cb_pos", [P, 2, 2, GT], U32)
        weight = m.sb("cb_weight", [P, 2, 2, GT], F32)
        total = m.sb("cb_total", [P, GT, D], F32)
        out = m.sb("cb_out", [P, 2, GT, D], F32)
        spare = m.sb("cb_spare", [P, 1], F32)
        w = norm_scratch(m, "cb_ln")
        listed = m.sem("cb_listed")
        gathered = [m.sem(f"cb_gathered{u}") for u in range(2)]
        added = m.sem("cb_added")
        step = m.sem("cb_step")
        stored = [m.sem(f"cb_stored{u}") for u in range(2)]
        STEPS = 2 + LN_STEPS
        out_rows = dram["out"].rearrange("b s c -> (b s) c")

        with nc.Block() as block:

            @block.gpsimd
            def _(pool):
                pool.sem_inc(added, 2)
                with pool.Fori(0, B) as b:
                    for c in range(QC):
                        g = b * QC + c
                        pool.wait_ge(added, g + 1)
                        nc.gpsimd.tensor_copy(weight[:, c % 2, :, :], keep["weight"][:, bass.ds(g, 1), :, :]
                                              .rearrange("p o n a -> p (o n) a"))
                        nc.gpsimd.tensor_copy(pos[:, c % 2, :, :], keep["pos"][:, bass.ds(g, 1), :, :]
                                              .rearrange("p o n a -> p (o n) a")).then_inc(listed, 1)
                        pool.wait_ge(listed, g + 1)
                        nc.gpsimd.tensor_tensor(spare[:, :], weight[:, c % 2, 0, 0:1], weight[:, c % 2, 1, 0:1],
                                                ALU.add)
                        for a in range(GT):
                            for n in range(2):
                                nc.gpsimd.indirect_dma_start(
                                    out=got[:, c % 2, n, a, :], out_offset=None, in_=dram["rows_out"],
                                    in_offset=bass.IndirectOffsetOnAxis(ap=pos[:, c % 2, n, a:a + 1], axis=0)
                                ).then_inc(gathered[c % 2], 16)

            @block.vector
            def _(dve):
                v = nc.vector
                with dve.Fori(0, B) as b:
                    for c in range(QC):
                        g = b * QC + c
                        steps = Chain(dve, step, b * (STEPS * QC) + STEPS * c)
                        dve.wait_ge(gathered[c % 2], b * (128 * QC // 2) + 128 * (c // 2 + 1))
                        for a in range(GT):
                            kept = keep["attn"][:, bass.ds(b * H, H), c * GT + a, :]
                            last = v.scalar_tensor_tensor(
                                total[:, a, :].rearrange("p (h w) -> p h w", w=HD),
                                got[:, c % 2, 0, a, :].rearrange("p (h w) -> p h w", w=HD),
                                weight[:, c % 2, 0, a:a + 1], kept, ALU.mult, ALU.add)
                        steps.then(last)
                        for a in range(GT):
                            last = v.scalar_tensor_tensor(total[:, a, :], got[:, c % 2, 1, a, :],
                                                          weight[:, c % 2, 1, a:a + 1], total[:, a, :],
                                                          ALU.mult, ALU.add)
                        steps.then(last)
                        dve.sem_inc(added, 1)
                        dve.wait_ge(stored[c % 2], b * (16 * QC // 2) + 16 * (c // 2) + 16)
                        layer_norm(v, steps, out[:, c % 2, :, :], total, w)
                        assert steps.n == STEPS, steps.n

            @block.sync
            def _(sp):
                for u in range(2):
                    sp.sem_inc(stored[u], 16)
                with sp.Fori(0, B) as b:
                    for c in range(QC):
                        g = b * QC + c
                        sp.wait_ge(step, b * (STEPS * QC) + STEPS * (c + 1))
                        sp.dma_start(out_rows[bass.ds(g * 512, 512), :].rearrange("(a p) n -> p a n", p=P),
                                     out[:, c % 2, :, :]).then_inc(stored[c % 2], 16)
                for u in range(2):
                    sp.wait_ge(stored[u], 16 * (GROUPS // 2 + 1))


def program(nc, dram):
    with ExitStack() as stack:
        m = Mem(nc, stack)
        keep = {
            "identity": m.sb("identity", [P, P], F32),
            "identity16": m.sb("identity16", [P, P], BF16),
            "carry": m.sb("carry", [P, E], F32),
            "ends": m.sb("ends", [P, E], I32),
            "tile_expert": m.sb("tile_expert", [P, TILES], I32),
            "tile_row": m.sb("tile_row", [P, TILES], I32),
            "weight": m.sb("weight", [P, GROUPS, 2, GT], F32),
            "pos": m.sb("pos", [P, GROUPS, 2, GT], U32),
            "place": m.sb("place", [P, GROUPS, 2, GT], F32),
            "wide": m.sb("wide", [P, 1], I32),
            "wide_ready": m.sem("wide_ready"),
            "attn": m.sb("attn", [P, BH, KT, HD], F32),
        }
        with ExitStack() as early:
            keep["v_all"] = Mem(nc, early).sb("v_all", [P, BH, KT, HD], F32)
            constants(nc, dram, keep)
            with ExitStack() as first:
                f = Mem(nc, first)
                hi_all = f.sb("hi_all", [P, 4, T], BF16)
                squares = f.sb("squares", [P, 4, T], BF16)
                key_sum = f.sb("key_sum", [P, KC, GROUPS], F32)
                project(nc, dram, keep, hi_all, squares, key_sum)
                bounds(nc, dram, keep, hi_all, squares, key_sum)
            maxima(nc, dram, keep)
            attention(nc, dram, keep)
        keep["w1"] = m.sb("w1_all", [P, E, KC, F], F32)
        route(nc, dram, keep)
        experts(nc, dram, keep)
        combine(nc, dram, keep)


_NAMES = {'x': 'L0_attn_x', 'qkv_w': 'L0_attn_qkv_w', 'qkv_b': 'L0_attn_qkv_b', 'out_w': 'L0_attn_out_w',
          'out_b': 'L0_attn_out_b', 'g1': 'L0_ffn_g1', 'be1': 'L0_ffn_be1', 'mix_w': 'L0_ffn_mix_w',
          'mix_b': 'L0_ffn_mix_b', 'g2': 'L0_ffn_g2', 'be2': 'L0_ffn_be2', 'router_w': 'L0_ffn_router_w',
          'w1': 'L0_ffn_w1', 'b1': 'L0_ffn_b1', 'w2': 'L0_ffn_w2', 'b2': 'L0_ffn_b2'}


def _trig_table():
    import numpy as np
    inv_freq = (1.0 / 10000.0 ** (np.arange(0, HD, 2, dtype=np.float32) / np.float32(HD))).astype(np.float32)
    angle = np.arange(H, dtype=np.float32)[:, None] * inv_freq[None, :]
    return np.stack([np.cos(angle), np.sin(angle)]).astype(np.float32).reshape(-1)


def kernel(**inputs):
    import numpy as _np
    import concourse.bacc as _bacc
    from concourse import mybir as _mybir
    from concourse.bass_utils import run_bass_kernel_spmd as _run

    nc = _bacc.Bacc("TRN2", target_bir_lowering=False, num_devices=1)
    arrays, dram = {}, {}
    for short, name in _NAMES.items():
        arrays["in_" + short] = _np.ascontiguousarray(inputs[name])
    arrays["in_trig"] = _trig_table()
    for name, a in arrays.items():
        dram[name[3:]] = nc.dram_tensor(name, a.shape, _mybir.dt.from_np(a.dtype), kind="ExternalInput").ap()
    dram["out"] = nc.dram_tensor("out_0", (B, S, D), F32, kind="ExternalOutput").ap()
    dram["qk"] = [nc.dram_tensor(f"{n}_parts", (PARTS, BH * HD, S), BF16, kind="Internal").ap() for n in "qk"]
    dram["negmax"] = nc.dram_tensor("negmax", (BH, PARTS, S), BF16, kind="Internal").ap()
    dram["b_parts"] = nc.dram_tensor("b_parts", (PARTS, E, F + D), BF16, kind="Internal").ap()
    for n, rows in (("rows_in", E * REGION), ("rows_out", TILES * P)):
        dram[n] = nc.dram_tensor(n, (rows, D), F32, kind="Internal").ap()
    program(nc, dram)
    r = _run(nc, [arrays], core_ids=[0])
    return r.results[0]["out_0"]
```

```python
import concourse.bass as bass
from concourse import mybir
from contextlib import ExitStack

F32 = mybir.dt.float32
BF16 = mybir.dt.bfloat16
I32 = mybir.dt.int32
U32 = mybir.dt.uint32
ALU = mybir.AluOpType
ACT = mybir.ActivationFunctionType
AX = mybir.AxisListType

B, S, D = 2, 2048, 256
H, HD = 16, 16
E, F = 8, 1024
P = 128
BH = B * H
T = B * S
NT = T // P
KT = S // P
QC = S // 512
KC = D // P
GT = 4
GROUPS = NT // GT
PARTS = 3
Q_ORDER = (0, 0, 0, 1, 1, 2)
K_ORDER = (0, 1, 2, 0, 1, 0)
ROWS = HD * len(Q_ORDER)
ROWS_M = ROWS + PARTS
EPS = 1e-5
GAP = 110.0
REGION = T + P
ROW = D + 2
TILES = 72


class Mem:

    def __init__(self, nc, stack):
        self.nc, self.stack = nc, stack

    def sb(self, name, shape, dtype):
        return self.stack.enter_context(self.nc.sbuf_tensor(name, shape, dtype))

    def ps(self, name, shape, dtype=F32):
        return self.stack.enter_context(self.nc.psum_tensor(name, shape, dtype))

    def sem(self, name):
        return self.stack.enter_context(self.nc.semaphore(name))


class Chain:

    def __init__(self, engine, sem, base=0):
        self.engine, self.sem, self.base, self.n = engine, sem, base, 0

    def then(self, instruction):
        instruction.then_inc(self.sem, 1)
        self.n += 1
        self.engine.wait_ge(self.sem, self.base + self.n)


def constants(nc, dram, keep):
    with ExitStack() as stack:
        m = Mem(nc, stack)
        lines = E * F // P
        b_in = m.sb("co_b_in", [P, P], F32)
        p_b = m.ps("co_pb", [P, P])
        zeroed = m.sem("co_zeroed")
        filled = m.sem("co_filled")
        loaded = m.sem("co_loaded")
        turned = m.sem("co_turned")
        with nc.Block() as block:

            @block.sync
            def _(sp):
                sp.wait_ge(zeroed, 1)
                sp.dma_start(b_in[0:lines, :], dram["b1"].rearrange("e (c p) -> (e c) p", p=P)
                             ).then_inc(loaded, 16)

            @block.tensor
            def _(pe):
                pe.wait_ge(filled, 4)
                pe.wait_ge(loaded, 16)
                nc.tensor.transpose(p_b[:, :], b_in[:, :], keep["identity"][:, :]).then_inc(turned, 1)

            @block.vector
            def _(dve):
                nc.vector.memset(b_in[:, :], 0.0).then_inc(zeroed, 1)
                dve.wait_ge(turned, 1)
                nc.vector.tensor_copy(keep["b1"][:, :, :].rearrange("p e c -> p (e c)"), p_b[:, 0:lines])

            @block.gpsimd
            def _(pool):
                for tile in (keep["identity"], keep["identity16"]):
                    nc.gpsimd.memset(tile[:, :], 0.0).then_inc(filled, 1)
                pool.wait_ge(filled, 2)
                for tile in (keep["identity"], keep["identity16"]):
                    nc.gpsimd.affine_select(out=tile[:, :], in_=tile[:, :], compare_op=ALU.not_equal, fill=1.0,
                                            base=0, pattern=[[-1, P]], channel_multiplier=1).then_inc(filled, 1)


def project(nc, dram, keep, hi_all, squares, key_sum):
    with ExitStack() as stack:
        m = Mem(nc, stack)
        raw = m.sb("qkv_raw", [P, KC + 1, H * 3 * HD], F32)
        trig = m.sb("trig", [P, 2, H, HD // 2], F32)
        rot_a = m.sb("rot_a", [P, KC + 1, H, HD // 2], F32)
        rot_b = m.sb("rot_b", [P, KC + 1, H, HD // 2], F32)
        w_qk = m.sb("w_qk", [P, KC + 1, 4, P], F32)
        w_v = m.sb("w_v", [P, KC + 1, D], F32)
        bias_qk = m.sb("bias_qk", [P, 4], F32)
        x_in = m.sb("x_in", [P, 2, GT, D], F32)
        xT = m.sb("xT", [P, 2, KC, 512], F32)
        lower = m.sb("qk_lower", [P, 4, PARTS - 1, 512], BF16)
        rest = m.sb("qk_rest", [P, 4, 512], F32)
        p_x = [m.ps(f"p_x{i}", [P, 512]) for i in range(KC)]
        p_qk = [m.ps(f"p_qk{i}", [P, 512]) for i in range(4)]
        p_v = [m.ps(f"p_v{i}", [P, 2, D]) for i in range(2)]

        loaded_w = m.sem("pj_loaded_w")
        loaded_x = [m.sem(f"pj_loaded_x{i}") for i in range(2)]
        rot_step = m.sem("pj_rot_step")
        weights_rotated = m.sem("pj_weights_rotated")
        bias_turned = m.sem("pj_bias_turned")
        bias_ready = m.sem("pj_bias_ready")
        x_turned = m.sem("pj_x_turned")
        xT_ready = [m.sem(f"pj_xT_ready{i}") for i in range(KC)]
        qk_done = m.sem("pj_qk_done")
        v_done = m.sem("pj_v_done")
        hi_ready = m.sem("pj_hi_ready")
        rest_ready = m.sem("pj_rest_ready")
        mid_ready = m.sem("pj_mid_ready")
        lo_ready = m.sem("pj_lo_ready")
        v_ready = m.sem("pj_v_ready")
        stored = [m.sem(f"pj_stored{i}") for i in range(4)]

        x_rows = dram["x"].rearrange("b s c -> (b s) c")
        identity, v_all = keep["identity"], keep["v_all"]

        with nc.Block() as block:

            def store_parts(sp, b, c):
                for ft in range(4):
                    sp.wait_ge(lo_ready, b * (4 * QC) + 4 * c + ft + 1 + 4)
                    rows = bass.ds(b * D + (ft % 2) * P, P)
                    cols = slice(c * 512, (c + 1) * 512)
                    sp.dma_start(dram["qk"][ft // 2][0, rows, cols], hi_all[:, ft, bass.ds(b * S + c * 512, 512)]
                                 ).then_inc(stored[ft], 16)
                    sp.dma_start(dram["qk"][ft // 2][1:, rows, cols].rearrange("t r n -> r t n"), lower[:, ft, :, :]
                                 ).then_inc(stored[ft], 16)

            @block.sync
            def _(sp):
                sp.dma_start(raw[:, 0:KC, :], dram["qkv_w"].rearrange("(s p) n -> p s n", p=P)).then_inc(loaded_w, 16)
                sp.dma_start(raw[:, KC, :], dram["qkv_b"].partition_broadcast(P)).then_inc(loaded_w, 16)
                sp.dma_start(trig[:, :, :, :].rearrange("p t h j -> p (t h j)"),
                             dram["trig"].partition_broadcast(P)).then_inc(loaded_w, 16)
                sp.sem_inc(x_turned, 4)
                for i in range(4):
                    sp.sem_inc(stored[i], 32)
                with sp.Fori(0, B) as b:
                    for c in range(QC):
                        g = b * QC + c
                        sp.wait_ge(x_turned, b * (2 * QC) + 2 * c + 2)
                        sp.dma_start(x_in[:, c % 2, :, :],
                                     x_rows[bass.ds(g * 512, 512), :].rearrange("(a p) n -> p a n", p=P)
                                     ).then_inc(loaded_x[c % 2], 16)
                        if c == 0:
                            continue
                        store_parts(sp, b, c - 1)
                    store_parts(sp, b, QC - 1)
                for i in range(4):
                    sp.wait_ge(stored[i], 32 * (GROUPS + 1))

            @block.vector
            def _(dve):
                steps = Chain(dve, rot_step)
                dve.wait_ge(loaded_w, 48)
                heads = raw[:, :, :].rearrange("p s (h w) -> p s h w", w=3 * HD)
                cos = trig[:, 0, :, :].unsqueeze(1).broadcast_to([P, KC + 1, H, HD // 2])
                sin = trig[:, 1, :, :].unsqueeze(1).broadcast_to([P, KC + 1, H, HD // 2])
                for n in range(2):
                    u1 = heads[:, :, :, n * HD:n * HD + 8]
                    u2 = heads[:, :, :, n * HD + 8:n * HD + 16]
                    out = w_qk[:, :, 2 * n:2 * n + 2, :].rearrange("p s t (h w) -> p s (t h) w", w=HD)
                    nc.vector.tensor_tensor(rot_a[:, :, :, :], u1, cos, ALU.mult)
                    steps.then(nc.vector.tensor_tensor(rot_b[:, :, :, :], u2, sin, ALU.mult))
                    steps.then(nc.vector.tensor_tensor(out[:, :, :, 0:8], rot_a[:, :, :, :], rot_b[:, :, :, :],
                                                       ALU.subtract))
                    nc.vector.tensor_tensor(rot_a[:, :, :, :], u2, cos, ALU.mult)
                    steps.then(nc.vector.tensor_tensor(rot_b[:, :, :, :], u1, sin, ALU.mult))
                    steps.then(nc.vector.tensor_tensor(out[:, :, :, 8:16], rot_a[:, :, :, :], rot_b[:, :, :, :],
                                                       ALU.add))
                nc.vector.tensor_scalar(w_qk[:, :, 0:2, :], w_qk[:, :, 0:2, :], HD ** -0.5, None, ALU.mult)
                nc.vector.tensor_copy(w_v[:, :, :].rearrange("p s (h w) -> p s h w", w=HD),
                                      heads[:, :, :, 2 * HD:]).then_inc(weights_rotated, 1)
                dve.wait_ge(bias_turned, 1)
                nc.vector.tensor_copy(bias_qk[:, :], p_qk[0][:, :].rearrange("p (t n) -> p t n", t=4)[:, :, 0]
                                      ).then_inc(bias_ready, 1)
                dve.sem_inc(rest_ready, 4)
                dve.sem_inc(xT_ready[1], 1)
                dve.sem_inc(v_ready, 2)
                with dve.Fori(0, B) as b:
                    for c in range(QC):
                        g = b * QC + c
                        dve.wait_ge(x_turned, b * (2 * QC) + 2 * c + 2 + 4)
                        nc.vector.tensor_copy(xT[:, c % 2, 1, :], p_x[1][:, :]).then_inc(xT_ready[1], 1)
                        for ft in range(4):
                            at = b * (4 * QC) + 4 * c + ft
                            dve.wait_ge(hi_ready, at + 1)
                            dve.wait_ge(lo_ready, at + 1)
                            nc.vector.scalar_tensor_tensor(rest[:, ft, :], p_qk[ft][:, :], bias_qk[:, ft:ft + 1],
                                                           hi_all[:, ft, bass.ds(b * S + c * 512, 512)], ALU.add, ALU.subtract
                                                           ).then_inc(rest_ready, 1)
                        for i in range(2):
                            dve.wait_ge(v_done, b * (2 * QC) + 2 * c + i + 1)
                            dst = v_all[:, bass.ds(b * H, H), 4 * c + 2 * i:4 * c + 2 * i + 2, :]
                            nc.vector.tensor_tensor(
                                dst.rearrange("p h a w -> p a h w"),
                                p_v[i][:, :, :].rearrange("p a (h w) -> p a h w", w=HD),
                                w_v[:, KC, :].rearrange("p (h w) -> p h w", w=HD).unsqueeze(1)
                                .broadcast_to([P, 2, H, HD]), ALU.add).then_inc(v_ready, 1)

            @block.scalar
            def _(act):
                act.sem_inc(xT_ready[0], 1)
                act.wait_ge(bias_ready, 1)
                with act.Fori(0, B) as b:
                    for c in range(QC):
                        act.wait_ge(x_turned, b * (2 * QC) + 2 * c + 1 + 4)
                        nc.scalar.activation(xT[:, c % 2, 0, :], p_x[0][:, :], ACT.Identity
                                             ).then_inc(xT_ready[0], 1)
                        for ft in range(5):
                            if ft < 4:
                                at = b * (4 * QC) + 4 * c + ft
                                act.wait_ge(qk_done, at + 1)
                                hi = hi_all[:, ft, bass.ds(b * S + c * 512, 512)]
                                total = key_sum[:, ft - 2, bass.ds(b * QC + c, 1)] if ft >= 2 else None
                                nc.scalar.activation(hi, p_qk[ft][:, :], ACT.Identity, bias=bias_qk[:, ft:ft + 1],
                                                     accum_out=total).then_inc(hi_ready, 1)
                            if ft > 0:
                                at = b * (4 * QC) + 4 * c + ft - 1
                                act.wait_ge(rest_ready, at + 1 + 4)
                                act.wait_ge(stored[ft - 1], b * (32 * QC) + 32 * c + 32)
                                nc.scalar.activation(lower[:, ft - 1, 0, :], rest[:, ft - 1, :], ACT.Identity
                                                     ).then_inc(mid_ready, 1)

            @block.gpsimd
            def _(pool):
                pool.sem_inc(lo_ready, 4)
                with pool.Fori(0, B) as b:
                    for c in range(QC):
                        for ft in range(4):
                            pool.wait_ge(mid_ready, b * (4 * QC) + 4 * c + ft + 1)
                            nc.gpsimd.tensor_tensor(lower[:, ft, 1, :], rest[:, ft, :], lower[:, ft, 0, :],
                                                    ALU.subtract).then_inc(lo_ready, 1)
                            hi = hi_all[:, ft, bass.ds(b * S + c * 512, 512)]
                            nc.gpsimd.tensor_tensor(squares[:, ft, bass.ds(b * S + c * 512, 512)], hi, hi, ALU.mult)

            @block.tensor
            def _(pe):
                pe.wait_ge(weights_rotated, 1)
                for ft in range(4):
                    last = nc.tensor.transpose(p_qk[0][:, ft * P:(ft + 1) * P], w_qk[:, KC, ft, :], identity[:, :])
                last.then_inc(bias_turned, 1)
                pe.wait_ge(bias_ready, 1)
                with pe.Fori(0, B) as b:
                    for c in range(QC):
                        pe.wait_ge(loaded_x[c % 2], b * (8 * QC) + 16 * (c // 2 + 1))
                        for kc in range(KC):
                            pe.wait_ge(xT_ready[kc], b * QC + c + 1)
                            for a in range(GT):
                                last = nc.tensor.transpose(p_x[kc][:, a * P:(a + 1) * P],
                                                           x_in[:, c % 2, a, kc * P:(kc + 1) * P], identity[:, :])
                            last.then_inc(x_turned, 1)
                        for kc in range(KC):
                            pe.wait_ge(xT_ready[kc], b * QC + c + 2)
                        for ft in range(4):
                            pe.wait_ge(rest_ready, b * (4 * QC) + 4 * c + ft + 1)
                            for kc in range(KC):
                                last = nc.tensor.matmul(p_qk[ft][:, :], w_qk[:, kc, ft, :], xT[:, c % 2, kc, :],
                                                        start=(kc == 0), stop=(kc == KC - 1))
                            last.then_inc(qk_done, 1)
                        for i in range(2):
                            pe.wait_ge(v_ready, b * (2 * QC) + 2 * c + i + 1)
                            for a in range(2):
                                tok = (2 * i + a) * P
                                for kc in range(KC):
                                    last = nc.tensor.matmul(p_v[i][:, a, :], xT[:, c % 2, kc, tok:tok + P],
                                                            w_v[:, kc, :], start=(kc == 0), stop=(kc == KC - 1))
                            last.then_inc(v_done, 1)


def load_head(engine, dram, bh, q_rows, k_rows, loaded):
    for n, (part_q, part_k) in enumerate(zip(Q_ORDER, K_ORDER)):
        rows = slice(n * HD, (n + 1) * HD)
        engine.dma_start(q_rows[rows, :], dram["qk"][0][part_q, bass.ds(bh * HD, HD), :]).then_inc(loaded, 16)
        engine.dma_start(k_rows[rows, :], dram["qk"][1][part_k, bass.ds(bh * HD, HD), :]).then_inc(loaded, 16)


def maxima(nc, dram, keep):
    with ExitStack() as stack:
        m = Mem(nc, stack)
        q_rows = m.sb("mx_q", [P, S], BF16)
        k_rows = m.sb("mx_k", [P, S], BF16)
        negmax = m.sb("mx_negmax", [P, KT], F32)
        rest1 = m.sb("mx_rest1", [P, KT], F32)
        rest2 = m.sb("mx_rest2", [P, KT], F32)
        columns = m.sb("mx_columns", [P, P], BF16)
        parts = columns[:, 0:PARTS * KT].rearrange("p (t a) -> p t a", t=PARTS)
        turned = m.sb("mx_turned", [PARTS * KT, P], BF16)
        p_s = [m.ps(f"mx_s{i}", [P, S]) for i in range(2)]
        loaded = m.sem("mx_loaded")
        scored = m.sem("mx_scored")
        reduced = m.sem("mx_reduced")
        split = m.sem("mx_split")
        parts_ready = m.sem("mx_parts_ready")
        parts_turned = m.sem("mx_parts_turned")
        row_ready = m.sem("mx_row_ready")
        stored = m.sem("mx_stored")
        p_turn = p_s[0][:, 0:P // 2].bitcast(BF16)

        with nc.Block() as block:

            @block.sync
            def _(sp):
                wide = sp.value_load(keep["wide"][0:1, 0:1], min_val=0, max_val=P)
                with sp.If(wide > 0):
                    sp.sem_inc(stored, 16)
                    sp.sem_inc(parts_turned, 1)
                    with sp.Fori(0, BH) as bh:
                        sp.wait_ge(parts_turned, bh + 1)
                        load_head(sp, dram, bh, q_rows, k_rows, loaded)
                        sp.wait_ge(row_ready, bh + 1)
                        sp.dma_start(dram["negmax"][bass.ds(bh, 1), :, :].rearrange("o t (a n) -> (o t a) n", n=P),
                                     turned[:, :]).then_inc(stored, 16)
                    sp.wait_ge(stored, 16 * (BH + 1))

            @block.tensor
            def _(pe):
                wide = pe.value_load(keep["wide"][0:1, 0:1], min_val=0, max_val=P)
                with pe.If(wide > 0):
                    with pe.Fori(0, BH) as bh:
                        pe.wait_ge(loaded, (bh + 1) * (16 * 12))
                        for qt in range(KT):
                            if qt >= 2:
                                pe.wait_ge(reduced, bh * KT + qt - 1)
                            for c in range(QC):
                                last = nc.tensor.matmul(p_s[qt % 2][:, c * 512:(c + 1) * 512],
                                                        q_rows[0:ROWS, qt * P:(qt + 1) * P],
                                                        k_rows[0:ROWS, c * 512:(c + 1) * 512], start=True, stop=True)
                            last.then_inc(scored, 1)
                        pe.wait_ge(parts_ready, bh + 1)
                        nc.tensor.transpose(p_turn, columns[:, :],
                                            keep["identity16"][:, :]).then_inc(parts_turned, 1)
                        pe.wait_ge(row_ready, bh + 1)

            @block.vector
            def _(dve):
                wide = dve.value_load(keep["wide"][0:1, 0:1], min_val=0, max_val=P)
                with dve.If(wide > 0):
                    nc.vector.memset(columns[:, :], 0.0)
                    with dve.Fori(0, BH) as bh:
                        steps = Chain(dve, split, bh * 4)
                        for qt in range(KT):
                            dve.wait_ge(scored, bh * KT + qt + 1)
                            nc.vector.tensor_reduce(negmax[:, qt:qt + 1], p_s[qt % 2][:, :], AX.X, ALU.max, negate=True
                                                    ).then_inc(reduced, 1)
                        dve.wait_ge(reduced, bh * KT + KT)
                        dve.wait_ge(parts_turned, bh + 1)
                        steps.then(nc.vector.tensor_copy(parts[:, 0, :], negmax[:, :]))
                        steps.then(nc.vector.tensor_tensor(rest1[:, :], negmax[:, :], parts[:, 0, :], ALU.subtract))
                        steps.then(nc.vector.tensor_copy(parts[:, 1, :], rest1[:, :]))
                        steps.then(nc.vector.tensor_tensor(rest2[:, :], rest1[:, :], parts[:, 1, :], ALU.subtract))
                        nc.vector.tensor_copy(parts[:, 2, :], rest2[:, :]).then_inc(parts_ready, 1)
                        dve.wait_ge(parts_turned, bh + 2)
                        dve.wait_ge(stored, bh * 16 + 16)
                        nc.vector.tensor_copy(turned[:, :], p_turn[0:PARTS * KT, :]).then_inc(row_ready, 1)


def bounds(nc, dram, keep, hi_all, squares, key_sum):
    with ExitStack() as stack:
        m = Mem(nc, stack)
        R = 32 * B
        select = m.sb("bd_select", [P, KC, 32], BF16)
        key_mean = m.sb("bd_key_mean", [P, KC, B, 32], BF16)
        mean = m.sb("bd_mean", [P, KC, B], F32)
        longest = m.sb("bd_longest", [R, 1], F32)
        bound = m.sb("bd_bound", [R, S], F32)
        negmid = m.sb("bd_negmid", [R, S], BF16)
        zeros = m.sb("bd_zeros", [BH, (PARTS - 1) * S], BF16)
        widest = m.sb("bd_widest", [P, 1], F32)
        narrow = m.sb("bd_narrow", [P, 1], BF16)
        ones = m.sb("bd_ones", [P, P], BF16)
        p_q = m.ps("bd_pq", [P, S])
        p_k = m.ps("bd_pk", [P, S])
        filled = m.sem("bd_filled")
        selected = m.sem("bd_selected")
        zeroed = m.sem("bd_zeroed")
        step = m.sem("bd_step")
        mean_ready = m.sem("bd_mean_ready")
        k_normed = m.sem("bd_k_normed")
        q_normed = m.sem("bd_q_normed")
        longest_ready = m.sem("bd_longest_ready")
        averaged = m.sem("bd_averaged")
        bound_ready = m.sem("bd_bound_ready")
        mid_ready = m.sem("bd_mid_ready")
        narrow_ready = m.sem("bd_narrow_ready")
        counted = m.sem("bd_counted")
        stored = m.sem("bd_stored")

        with nc.Block() as block:

            @block.gpsimd
            def _(pool):
                nc.gpsimd.memset(select[:, :, :], 1.0).then_inc(filled, 1)
                for kc in range(KC):
                    pool.wait_ge(filled, 2 * kc + 1)
                    nc.gpsimd.affine_select(out=select[:, kc, :], in_=select[:, kc, :], compare_op=ALU.is_ge,
                                            fill=0.0, base=P * kc, pattern=[[-HD, 32]], channel_multiplier=1
                                            ).then_inc(filled, 1)
                    pool.wait_ge(filled, 2 * kc + 2)
                    nc.gpsimd.affine_select(out=select[:, kc, :], in_=select[:, kc, :], compare_op=ALU.is_ge,
                                            fill=0.0, base=HD - 1 - P * kc, pattern=[[HD, 32]],
                                            channel_multiplier=-1).then_inc(filled, 1)
                pool.wait_ge(filled, 5)
                pool.sem_inc(selected, 1)

            @block.sync
            def _(sp):
                sp.wait_ge(zeroed, 1)
                sp.dma_start(dram["negmax"][:, 1:, :].rearrange("h t n -> h (t n)"), zeros[:, :]).then_inc(stored, 16)
                sp.wait_ge(mid_ready, 1)
                for b in range(B):
                    sp.dma_start(dram["negmax"][b * H:(b + 1) * H, 0, :], negmid[32 * b:32 * b + H, :]
                                 ).then_inc(stored, 16)
                sp.wait_ge(stored, 16 * (1 + B))

            @block.tensor
            def _(pe):
                def per_head(dst, b, weights, moving, sem):
                    for c in range(QC):
                        tok = slice(b * S + c * 512, b * S + (c + 1) * 512)
                        for kc in range(KC):
                            last = nc.tensor.matmul(dst[32 * b:32 * b + 32, c * 512:(c + 1) * 512],
                                                    weights(kc, b), moving(kc, tok),
                                                    start=(kc == 0), stop=(kc == KC - 1))
                    last.then_inc(sem, 1)

                pe.wait_ge(selected, 1)
                for b in range(B):
                    per_head(p_k, b, lambda kc, b: select[:, kc, :], lambda kc, t: squares[:, 2 + kc, t], k_normed)
                for b in range(B):
                    per_head(p_q, b, lambda kc, b: select[:, kc, :], lambda kc, t: squares[:, kc, t], q_normed)
                pe.wait_ge(longest_ready, 1)
                pe.wait_ge(mean_ready, 1)
                for b in range(B):
                    per_head(p_k, b, lambda kc, b: key_mean[:, kc, b, :], lambda kc, t: hi_all[:, kc, t], averaged)
                pe.wait_ge(narrow_ready, 1)
                nc.tensor.matmul(p_q[:, 0:1], ones[:, :], narrow[:, :], start=True, stop=True).then_inc(counted, 1)

            @block.scalar
            def _(act):
                act.wait_ge(longest_ready, 1)
                act.wait_ge(q_normed, B)
                nc.scalar.activation(bound[:, :], p_q[0:R, :], ACT.Sqrt, scale=longest[:, 0:1]
                                     ).then_inc(bound_ready, 1)

            @block.vector
            def _(dve):
                v = nc.vector
                steps = Chain(dve, step)
                v.memset(zeros[:, :].bitcast(U32), 0).then_inc(zeroed, 1)
                v.memset(ones[:, :], 1.0)
                v.memset(widest[:, :], 0.0)
                steps.then(v.tensor_reduce(mean[:, :, :], key_sum[:, :, :].rearrange("p k (b c) -> p k b c", b=B),
                                           AX.X, ALU.add))
                steps.then(v.tensor_scalar(mean[:, :, :], mean[:, :, :], -0.5 / S, None, ALU.mult))
                dve.wait_ge(selected, 1)
                for kc in range(KC):
                    for b in range(B):
                        last = v.tensor_scalar(key_mean[:, kc, b, :], select[:, kc, :], mean[:, kc, b:b + 1], None,
                                               ALU.mult)
                last.then_inc(mean_ready, 1)
                dve.wait_ge(k_normed, B)
                v.tensor_reduce(longest[:, :], p_k[0:R, :], AX.X, ALU.max).then_inc(longest_ready, 1)
                dve.wait_ge(bound_ready, 1)
                dve.wait_ge(averaged, B)
                v.scalar_tensor_tensor(negmid[:, :], bound[:, :], -0.5, p_k[0:R, :], ALU.mult, ALU.add
                                       ).then_inc(mid_ready, 1)
                steps.then(v.scalar_tensor_tensor(bound[:, :], p_k[0:R, :], 2.0, bound[:, :], ALU.mult, ALU.add))
                steps.then(v.tensor_reduce(widest[0:R, :], bound[:, :], AX.X, ALU.max))
                v.tensor_scalar(narrow[:, :], widest[:, :], GAP, None, ALU.is_le).then_inc(narrow_ready, 1)
                dve.wait_ge(counted, 1)
                v.tensor_scalar(keep["wide"][:, :], p_q[:, 0:1], -1.0, float(P), ALU.mult, ALU.add
                                ).then_inc(keep["wide_ready"], 1)


def inverse_root(dve, steps, out, var, w):
    v, half, y = dve, w["half"], out
    steps.then(v.tensor_scalar(w["bits"], var.bitcast(I32), 1, None, ALU.logical_shift_right))
    steps.then(v.tensor_scalar(y.bitcast(I32), w["bits"], -1.0, float(0x5F3759DF), ALU.mult, ALU.add))
    steps.then(v.tensor_scalar(half, var, -0.5, None, ALU.mult))
    for _ in range(4):
        steps.then(v.tensor_tensor(w["t"], y, y, ALU.mult))
        steps.then(v.tensor_tensor(w["t"], w["t"], half, ALU.mult))
        steps.then(v.scalar_tensor_tensor(w["t"], w["t"], 0.5, y, ALU.add, ALU.mult))
        steps.then(v.tensor_tensor(y, y, w["t"], ALU.add))


LN_STEPS = 1 + 4 + 3 + 4 * 4 + 1 + 1


def layer_norm(dve, steps, out, inp, w):
    for a in range(GT):
        last = dve.bn_stats(w["stats"][:, a, :], inp[:, a, :])
    steps.then(last)
    stats = w["stats"]
    dve.tensor_tensor(w["apart"], stats[:, :, 1], stats[:, :, 4], ALU.subtract)
    dve.tensor_tensor(w["mean2"], stats[:, :, 1], stats[:, :, 4], ALU.add)
    steps.then(dve.tensor_tensor(w["var"], stats[:, :, 2], stats[:, :, 5], ALU.add))
    steps.then(dve.scalar_tensor_tensor(w["apart"], w["apart"], 0.25, w["apart"], ALU.mult, ALU.mult))
    steps.then(dve.scalar_tensor_tensor(w["var"], w["var"], 1.0 / D, w["apart"], ALU.mult, ALU.add))
    steps.then(dve.tensor_scalar(w["var"], w["var"], EPS, None, ALU.add))
    inverse_root(dve, steps, w["rstd"], w["var"], w)
    steps.then(dve.scalar_tensor_tensor(w["shift"], w["mean2"], -0.5, w["rstd"], ALU.mult, ALU.mult))
    for a in range(GT):
        last = dve.tensor_scalar(out[:, a, :], inp[:, a, :], w["rstd"][:, a:a + 1], w["shift"][:, a:a + 1],
                                 ALU.mult, ALU.add)
    steps.then(last)


def norm_scratch(m, name):
    w = {"stats": m.sb(name + "_stats", [P, GT, 6], F32),
         "bits": m.sb(name + "_bits", [P, GT], I32)}
    for n in ("var", "apart", "mean2", "rstd", "shift", "half", "t"):
        w[n] = m.sb(f"{name}_{n}", [P, GT], F32)
    return {n: t[tuple(slice(None) for _ in t.shape)] for n, t in w.items()}


def attend_and_route(nc, dram, keep):
    G3 = 3
    QUAD = 4
    UNITS = H // QUAD
    CHUNKS = KT * QUAD
    NG = -(-CHUNKS // G3)
    RING = 4
    NB = UNITS * NG
    JOBS0, JOBS = UNITS - 1, 16
    assert NB % RING == 0
    with ExitStack() as stack:
        m = Mem(nc, stack)
        k_rows = keep["w1_place"][:, :].bitcast(BF16).rearrange("p (h n) -> p h n", h=H)
        probs_at = BH * KT * HD
        q_at = probs_at + RING * G3 * 512
        probs = keep["w2_place"][:, probs_at:q_at].rearrange("p (r n) -> p r n", r=RING)
        q_rows = [keep["w2_place"][:, q_at + u * 1024:q_at + (u + 1) * 1024].bitcast(BF16)
                  .rearrange("p (h n) -> p h n", h=QUAD) for u in range(2)]
        v_one = [m.sb(f"at_v{u}", [P, QUAD, KT, 2 * HD], F32) for u in range(2)]
        o_sb = [m.sb(f"at_o{u}", [P, 512], F32) for u in range(2)]
        rden = m.sb("at_rden", [P, GT, QUAD], F32)
        attn = m.sb("at_attn", [P, GT, D], F32)
        p_s = [m.ps(f"at_s{i}", [P, G3 * 512]) for i in range(2)]
        p_o = m.ps("at_po", [P, 512])
        small = m.ps("at_small", [P, 512])

        out_w = m.sb("rt_out_w", [P, KC, D], F32)
        mix_w = m.sb("rt_mix_w", [P, KC, D], F32)
        router_w = m.sb("rt_router_w", [P, KC, E], F32)
        rows = {n: m.sb("rt_" + n, [P, D], F32) for n in ("out_b", "g1", "be1", "mix_b", "g2", "be2")}
        x_in = m.sb("rt_x_in", [P, GT, D], F32)
        x1 = m.sb("rt_x1", [P, GT, D], F32)
        norm1 = m.sb("rt_norm1", [P, GT, D], F32)
        total = m.sb("rt_total", [P, GT, D], F32)
        x2 = m.sb("rt_x2", [P, GT, D], F32)
        sent_rows = m.sb("rt_sent_rows", [P, 2, GT, ROW], F32)
        turned = m.sb("rt_turned", [P, KC, 512], F32)
        w = norm_scratch(m, "rt_ln")
        logit = m.sb("rt_logit", [P, GT, E], F32)
        lmax = m.sb("rt_lmax", [P, GT], F32)
        prob = m.sb("rt_prob", [P, GT, E], F32)
        prob_sum = m.sb("rt_prob_sum", [P, GT], F32)
        top = m.sb("rt_top", [P, GT, 8], F32)
        top_i = m.sb("rt_top_i", [P, GT, 8], U32)
        top_f = m.sb("rt_top_f", [P, 2, GT], F32)
        chosen = m.sb("rt_chosen", [P, 2, GT, E], F32)
        both = m.sb("rt_both", [P, GT, E], BF16)
        place = m.sb("rt_place", [P, GT, E], F32)
        picked = m.sb("rt_picked", [P, 2, GT, E], F32)
        pos_f = m.sb("rt_pos_f", [P, 2, GT], F32)
        pos = m.sb("rt_pos", [P, 2, GT], U32)
        home = m.sb("rt_home", [P, 2, GT], I32)
        iota_e = m.sb("rt_iota_e", [P, E], F32)
        lower = m.sb("rt_lower", [P, P], BF16)
        ones = m.sb("rt_ones", [P, P], BF16)
        zero_rows = m.sb("rt_zero_rows", [P, D], F32)
        pad_home = m.sb("rt_pad_home", [P, E, 2], I32)
        spare = m.sb("rt_spare", [P, 1], F32)
        spare_v = m.sb("rt_spare_v", [P, 1], F32)
        carry = m.sb("rt_carry", [P, E], F32)
        scratch = {"iota_e": iota_e, "iota_t": m.sb("rt_iota_t", [P, TILES], F32),
                   "tiles_i": m.sb("rt_tiles_i", [P, E], I32), "last": m.sb("rt_last", [P, 1], F32),
                   "tile": m.sb("rt_tile", [P, TILES], F32), "row": m.sb("rt_row", [P, TILES], F32),
                   "passed": m.sb("rt_passed", [P, TILES, E], F32)}
        scratch.update({n: m.sb("rt_" + n, [P, E], F32) for n in ("count", "tiles", "cum", "cum2")})

        loaded_q = [m.sem(f"at_loaded_q{u}") for u in range(2)]
        loaded_k = [m.sem(f"at_loaded_k{q}") for q in range(UNITS)]
        ones_ready = m.sem("at_ones_ready")
        v_ones = m.sem("at_v_ones")
        v_copied = m.sem("at_v_copied")
        scored = m.sem("at_scored")
        exp_done = m.sem("at_exp_done")
        weighed = m.sem("at_weighed")
        o_copied = m.sem("at_o_copied")
        rden_ready = m.sem("at_rden_ready")
        small_done = m.sem("at_small_done")
        small_read = m.sem("at_small_read")
        loaded_w = m.sem("rt_loaded_w")
        loaded_x = m.sem("rt_loaded_x")
        constants_ready = m.sem("rt_constants_ready")
        carry_ready = m.sem("rt_carry_ready")
        step = m.sem("rt_step")
        x_biased = m.sem("rt_x_biased")
        norm1_ready = m.sem("rt_norm1_ready")
        total_ready = m.sem("rt_total_ready")
        x2_ready = m.sem("rt_x2_ready")
        kept = m.sem("rt_kept")
        kept_stored = m.sem("rt_kept_stored")
        norm2_ready = m.sem("rt_norm2_ready")
        doubled = m.sem("rt_doubled")
        shifted = m.sem("rt_shifted")
        router_exp = m.sem("rt_router_exp")
        both_ready = m.sem("rt_both_ready")
        placed = m.sem("rt_placed")
        scattered = m.sem("rt_scattered")
        sent = m.sem("rt_sent")
        padded = m.sem("rt_padded")
        made = m.sem("rt_made")
        mapped = m.sem("rt_mapped")
        x_rows = dram["x"].rearrange("b s c -> (b s) c")
        v_all = keep["v_all"]
        STEPS = 3 * LN_STEPS + 19

        def chunks(g):
            return range(g * G3, min((g + 1) * G3, CHUNKS))

        def spread(name):
            return rows[name][:, :].unsqueeze(1).broadcast_to([P, GT, D])

        def first_job(i):
            return (i - 1) * JOBS + JOBS0

        with nc.Block() as block:

            @block.sync
            def _(sp):
                def load_k(b, q):
                    for n, part in enumerate(K_ORDER):
                        src = dram["qk"][1][part, (b * H + q * QUAD) * HD:(b * H + (q + 1) * QUAD) * HD, :]
                        sp.dma_start(k_rows[n * HD:(n + 1) * HD, q * QUAD:(q + 1) * QUAD, :],
                                     src.rearrange("(h w) n -> w h n", w=HD)).then_inc(loaded_k[q], 16)

                def load_q(b, c, q, unit):
                    u = q % 2
                    sp.wait_ge(scored, unit * NG + NG)
                    cols = bass.ds(c * 512, 512)
                    for n, part in enumerate(Q_ORDER):
                        src = dram["qk"][0][part, (b * H + q * QUAD) * HD:(b * H + (q + 1) * QUAD) * HD, cols]
                        sp.dma_start(q_rows[u][n * HD:(n + 1) * HD, :, :],
                                     src.rearrange("(h w) n -> w h n", w=HD)).then_inc(loaded_q[u], 16)
                    sp.dma_start(q_rows[u][ROWS:ROWS_M, :, :],
                                 dram["negmax"][b * H + q * QUAD:b * H + (q + 1) * QUAD, :, cols]
                                 .rearrange("h t n -> t h n")).then_inc(loaded_q[u], 16)

                def load_x(i):
                    sp.wait_ge(x_biased, i + 1)
                    sp.dma_start(x_in[:, :, :], x_rows[bass.ds(i * 512, 512), :].rearrange("(a p) n -> p a n", p=P)
                                 ).then_inc(loaded_x, 16)

                sp.sem_inc(scored, 2 * NG)
                load_k(0, 0)
                load_q(0, 0, 0, 0)
                sp.wait_ge(ones_ready, 1)
                for q in range(1, UNITS):
                    load_k(0, q)
                    sp.dma_start(k_rows[ROWS:ROWS_M, q * QUAD:(q + 1) * QUAD, :], k_rows[ROWS:ROWS_M, 0:QUAD, :]
                                 ).then_inc(loaded_k[q], 16)
                    if q == 1:
                        load_q(0, 0, 1, 1)
                for dst, src in ((out_w, "out_w"), (mix_w, "mix_w"), (router_w, "router_w")):
                    sp.dma_start(dst[:, :, :], dram[src].rearrange("(s p) n -> p s n", p=P)).then_inc(loaded_w, 16)
                for name in rows:
                    sp.dma_start(rows[name][:, :], dram[name].partition_broadcast(P)).then_inc(loaded_w, 16)
                for q in range(2, UNITS):
                    load_q(0, 0, q, q)
                load_x(0)
                with sp.Fori(1, QC) as c:
                    for q in range(UNITS):
                        load_q(0, c, q, c * UNITS + q)
                    load_x(c)
                for q in range(UNITS):
                    sp.wait_ge(scored, 2 * NG + (QC - 1) * NB + (q + 1) * NG)
                    load_k(1, q)
                    load_q(1, 0, q, QC * UNITS + q)
                load_x(QC)
                with sp.Fori(1, QC) as c:
                    for q in range(UNITS):
                        load_q(1, c, q, (c + QC) * UNITS + q)
                    load_x(c + QC)
                sp.wait_ge(scored, GROUPS * NB + 2 * NG)
                for e in range(E):
                    sp.dma_start(keep["w1"][:, e, :, :], dram["w1"][e].rearrange("(s p) n -> p s n", p=P)
                                 ).then_inc(keep["loaded_w1"], 16)
                sp.wait_ge(weighed, GROUPS * NB + 2 * NG)
                for e in range(E):
                    sp.dma_start(keep["w2"][:, e, :, :], dram["w2"][e].rearrange("(s p) n -> p s n", p=P)
                                 ).then_inc(keep["loaded_w2"], 16)
                sp.wait_ge(mapped, 1)
                sp.wait_ge(sent, GROUPS + 1)
                for e in range(E):
                    end = sp.value_load(keep["ends"][0:1, e:e + 1], min_val=0, max_val=E * REGION - P)
                    sp.dma_start(dram["rows_in"][bass.ds(end, P), 0:D], zero_rows[:, :]).then_inc(padded, 16)
                    sp.dma_start(dram["rows_in"][bass.ds(end, P), D:ROW], pad_home[:, e, :].bitcast(F32)
                                 ).then_inc(padded, 16)
                sp.wait_ge(padded, 32 * E)

            @block.gpsimd
            def _(pool):
                def copy_v(unit, heads):
                    pool.wait_ge(weighed, unit * NG + NG)
                    nc.gpsimd.tensor_copy(v_one[heads[1] % 2][:, :, :, 0:HD],
                                          v_all[:, bass.ds(heads[0] * H + heads[1] * QUAD, QUAD), :, :]
                                          ).then_inc(v_copied, 1)

                def route(i, q):
                    if q == 0:
                        pool.wait_ge(loaded_x, i * 16 + 16)
                        pool.wait_ge(kept_stored, i * 16 + 16)
                        nc.gpsimd.tensor_tensor(total[:, :, :], x_in[:, :, :], spread("out_b"), ALU.add
                                                ).then_inc(x_biased, 1)
                    if q == 1:
                        pool.wait_ge(norm1_ready, i + 1)
                        nc.gpsimd.tensor_tensor(total[:, :, :], x1[:, :, :], norm1[:, :, :], ALU.add
                                                ).then_inc(total_ready, 1)
                        pool.wait_ge(total_ready, i * 2 + 1)
                        nc.gpsimd.tensor_tensor(total[:, :, :], total[:, :, :], spread("mix_b"), ALU.add
                                                ).then_inc(total_ready, 1)
                        pool.wait_ge(x2_ready, i + 1)
                        nc.gpsimd.tensor_tensor(total[:, :, :], x1[:, :, :], x2[:, :, :], ALU.add
                                                ).then_inc(kept, 1)
                        pool.wait_ge(norm2_ready, i + 1)
                        nc.gpsimd.tensor_tensor(sent_rows[:, 1, :, 0:D], x2[:, :, :], spread("be2"), ALU.add
                                                ).then_inc(doubled, 1)
                    if q == 3:
                        pool.wait_ge(placed, i + 1)
                        nc.gpsimd.tensor_tensor(spare[:, :], lmax[:, 0:1], lmax[:, 1:2], ALU.add)
                        for n in range(2):
                            for a in range(GT):
                                nc.gpsimd.indirect_dma_start(
                                    out=dram["rows_in"], in_=sent_rows[:, n, a, :], in_offset=None,
                                    out_offset=bass.IndirectOffsetOnAxis(ap=pos[:, n, a:a + 1], axis=0)
                                ).then_inc(scattered, 16)
                        pool.wait_ge(scattered, (i + 1) * (16 * 2 * GT))
                        pool.sem_inc(sent, 1)

                g = nc.gpsimd
                g.memset(ones[:, :], 1.0).then_inc(constants_ready, 1)
                pool.wait_ge(constants_ready, 1)
                g.affine_select(out=lower[:, :], in_=ones[:, :], compare_op=ALU.is_gt, fill=0.0, base=0,
                                pattern=[[1, P]], channel_multiplier=-1).then_inc(constants_ready, 1)
                g.iota(iota_e[:, :], pattern=[[1, E]], base=0, channel_multiplier=0,
                       allow_small_or_imprecise_dtypes=True).then_inc(constants_ready, 1)
                g.iota(scratch["iota_t"][:, :], pattern=[[1, TILES]], base=0, channel_multiplier=0,
                       allow_small_or_imprecise_dtypes=True).then_inc(constants_ready, 1)
                g.iota(home[:, :, :], pattern=[[T, 2], [P, GT]], base=0, channel_multiplier=1
                       ).then_inc(constants_ready, 1)
                g.iota(pad_home[:, :, :], pattern=[[P, E], [0, 2]], base=2 * T, channel_multiplier=1
                       ).then_inc(constants_ready, 1)
                g.memset(zero_rows[:, :], 0.0).then_inc(constants_ready, 1)
                pool.wait_ge(constants_ready, 7)
                g.memset(pad_home[:, :, 1:2], 0).then_inc(constants_ready, 1)
                pool.wait_ge(v_ones, 2)
                pool.sem_inc(weighed, 2 * NG)
                copy_v(0, (0, 0))
                for q in range(1, UNITS):
                    copy_v(q, (0, q))
                copy_v(UNITS, (1 // QC, 0))
                pool.wait_ge(loaded_w, 16 * 9)
                pool.sem_inc(kept, 1)
                pool.sem_inc(sent, 1)
                pool.sem_inc(x_biased, 1)
                pool.sem_inc(kept_stored, 16)
                with pool.Fori(1, GROUPS - 1) as i:
                    for q in range(UNITS):
                        copy_v(i * UNITS + q + 1, ((i + (q + 1) // UNITS) // QC, (q + 1) % UNITS))
                        route(i - 1, q)
                for q in range(UNITS):
                    if q + 1 < UNITS:
                        copy_v((GROUPS - 1) * UNITS + q + 1, (B - 1, q + 1))
                    route(GROUPS - 2, q)
                for q in range(UNITS):
                    route(GROUPS - 1, q)

            @block.scalar
            def _(act):
                def exponentials(i, routed):
                    for n in range(NB):
                        width = 512 * len(chunks(n % NG))
                        act.wait_ge(scored, i * NB + n + 1 + 2 * NG)
                        act.wait_ge(weighed, i * NB + n + 1 - RING + 2 * NG)
                        nc.scalar.activation(probs[:, n % RING, 0:width], p_s[n % 2][:, 0:width], ACT.Exp
                                             ).then_inc(exp_done, 1)
                        if routed and n == 46:
                            keep_sum(i - 1)
                        if routed and n == 60:
                            router(i - 1)

                def keep_sum(i):
                    act.wait_ge(kept, i + 2)
                    act.dma_start(dram["kept"][bass.ds(i * 512, 512), :].rearrange("(a p) n -> p a n", p=P),
                                  total[:, :, :]).then_inc(kept_stored, 16)

                def router(i):
                    act.wait_ge(shifted, i + 1)
                    nc.scalar.activation(prob[:, :, :], logit[:, :, :], ACT.Exp).then_inc(router_exp, 1)

                exponentials(0, False)
                with act.Fori(1, GROUPS) as i:
                    exponentials(i, True)
                keep_sum(GROUPS - 1)
                router(GROUPS - 1)
                act.wait_ge(kept_stored, 16 * (GROUPS + 1))

            @block.tensor
            def _(pe):
                def score(i, n):
                    q, g = n // NG, n % NG
                    if g == 0:
                        pe.wait_ge(loaded_k[q], (i // QC) * (16 * 6) + 16 * (6 if q == 0 else 7))
                        pe.wait_ge(loaded_q[q % 2], i * (2 * 16 * 7) + (q // 2 + 1) * (16 * 7))
                    for s, c in enumerate(chunks(g)):
                        kt, h = c // QUAD, c % QUAD
                        last = nc.tensor.matmul(p_s[n % 2][:, s * 512:(s + 1) * 512],
                                                k_rows[0:ROWS_M, q * QUAD + h, kt * P:(kt + 1) * P],
                                                q_rows[q % 2][0:ROWS_M, h, :], start=True, stop=True)
                    last.then_inc(scored, 1)

                def weigh(i, n):
                    q, g = n // NG, n % NG
                    if g == 0:
                        pe.wait_ge(v_copied, i * UNITS + q + 1)
                        pe.wait_ge(o_copied, i * UNITS + q + 1)
                    for s, c in enumerate(chunks(g)):
                        kt, h = c // QUAD, c % QUAD
                        last = nc.tensor.matmul(p_o[32 * h:32 * h + 32, :], v_one[q % 2][:, h, kt, :],
                                                probs[:, n % RING, s * 512:(s + 1) * 512],
                                                start=(kt == 0), stop=(kt == KT - 1))
                    last.then_inc(weighed, 1)

                def turn_out(i, q, job):
                    pe.wait_ge(o_copied, i * UNITS + q + 2)
                    pe.wait_ge(small_read, job + 1)
                    for a in range(GT):
                        last = nc.tensor.transpose(small[:, a * P:(a + 1) * P], o_sb[q % 2][:, a * P:(a + 1) * P],
                                                   keep["identity"][:, :])
                    last.then_inc(small_done, 1)

                def turn(src, kc, job):
                    pe.wait_ge(small_read, job + 1)
                    for a in range(GT):
                        last = nc.tensor.transpose(small[:, a * P:(a + 1) * P], src[:, a, kc * P:(kc + 1) * P],
                                                   keep["identity"][:, :])
                    last.then_inc(small_done, 1)

                def product(weights, tiles, width, job):
                    pe.wait_ge(small_read, job + 1)
                    for n, a in enumerate(tiles):
                        for kc in range(KC):
                            last = nc.tensor.matmul(small[:, n * width:(n + 1) * width],
                                                    turned[:, kc, a * P:(a + 1) * P], weights[:, kc, :],
                                                    start=(kc == 0), stop=(kc == KC - 1))
                    last.then_inc(small_done, 1)

                def count(i, job):
                    pe.wait_ge(both_ready, i + 1)
                    pe.wait_ge(small_read, job + 1)
                    nc.tensor.matmul(small[:, 0:GT * E], lower[:, :], both[:, :, :], start=True, stop=True)
                    nc.tensor.matmul(small[:, GT * E:2 * GT * E], ones[:, :], both[:, :, :], start=True, stop=True,
                                     skip_group_check=True).then_inc(small_done, 1)

                def route(i, at, job):
                    if at == 5:
                        pe.wait_ge(rden_ready, i * (2 * UNITS) + 2 * UNITS)
                        turn(attn, 0, job)
                    elif at == 7:
                        turn(attn, 1, job)
                    elif at == 9:
                        product(out_w, (0, 1), D, job)
                    elif at == 11:
                        product(out_w, (2, 3), D, job)
                    elif at == 27:
                        pe.wait_ge(norm1_ready, i + 1)
                        turn(norm1, 0, job)
                    elif at == 29:
                        turn(norm1, 1, job)
                    elif at == 31:
                        product(mix_w, (0, 1), D, job)
                    elif at == 33:
                        product(mix_w, (2, 3), D, job)
                    elif at == 49:
                        pe.wait_ge(norm2_ready, i + 1)
                        turn(sent_rows[:, 0, :, 0:D], 0, job)
                    elif at == 51:
                        turn(sent_rows[:, 0, :, 0:D], 1, job)
                    elif at == 53:
                        product(router_w, range(GT), E, job)
                    elif at == 71:
                        count(i, job)
                    else:
                        return 0
                    return 1

                def attend(i, routed, is_last, job):
                    for n in range(NB):
                        pe.wait_ge(exp_done, i * NB + n + 1)
                        if n + 2 < NB:
                            score(i, n + 2)
                        elif not is_last:
                            score(i + 1, n + 2 - NB)
                        weigh(i, n)
                        q, g = n // NG, n % NG
                        if g == 3 and q > 0:
                            turn_out(i, q - 1, job)
                            job = job + 1
                        if g == 3 and q == 0 and routed:
                            turn_out(i - 1, UNITS - 1, job)
                            job = job + 1
                        if routed:
                            job = job + route(i - 1, n, job)
                    return job

                pe.sem_inc(o_copied, 1)
                pe.sem_inc(small_read, 1)
                pe.wait_ge(ones_ready, 1)
                score(0, 0)
                score(0, 1)
                attend(0, False, False, 0)
                pe.wait_ge(loaded_w, 16 * 9)
                pe.wait_ge(constants_ready, 8)
                with pe.Fori(1, GROUPS - 1) as i:
                    attend(i, True, False, first_job(i))
                job = attend(GROUPS - 1, True, True, first_job(GROUPS - 1))
                turn_out(GROUPS - 1, UNITS - 1, job)
                job += 1
                for at in range(NB):
                    job += route(GROUPS - 1, at, job)

            @block.vector
            def _(dve):
                v = nc.vector

                class Job:
                    def __init__(self, first):
                        self.first, self.n = first, 0

                    def arrived(self):
                        dve.wait_ge(small_done, self.first + self.n + 1)
                        self.n += 1

                def head_output(i, q, job):
                    dve.wait_ge(weighed, i * NB + (q + 1) * NG + 2 * NG)
                    v.tensor_copy(o_sb[q % 2][:, :], p_o[:, :]).then_inc(o_copied, 1)
                    job.arrived()
                    out = small[:, :].rearrange("p (a h w) -> p a h w", a=GT, h=QUAD)
                    v.reciprocal(rden[:, :, :], out[:, :, :, HD]).then_inc(rden_ready, 1)
                    dve.wait_ge(rden_ready, i * (2 * UNITS) + 2 * q + 1)
                    v.tensor_tensor(attn[:, :, q * QUAD * HD:(q + 1) * QUAD * HD]
                                    .rearrange("p a (h w) -> p a h w", w=HD), out[:, :, :, 0:HD],
                                    rden[:, :, :].unsqueeze(3).broadcast_to([P, GT, QUAD, HD]), ALU.mult
                                    ).then_inc(rden_ready, 1)
                    dve.wait_ge(rden_ready, i * (2 * UNITS) + 2 * q + 2)
                    dve.sem_inc(small_read, 1)

                def route(i, q, steps, job):
                    def turned_half(kc):
                        job.arrived()
                        v.tensor_copy(turned[:, kc, :], small[:, :]).then_inc(small_read, 1)

                    def add_total(out):
                        for half in range(2):
                            job.arrived()
                            tiles = slice(2 * half, 2 * half + 2)
                            v.tensor_tensor(out[:, tiles, :], small[:, :].rearrange("p (a n) -> p a n", a=2),
                                            total[:, tiles, :], ALU.add).then_inc(small_read, 1)
                        dve.wait_ge(small_read, job.first + job.n + 1)

                    if q == 0:
                        turned_half(0)
                        turned_half(1)
                        dve.wait_ge(x_biased, i + 2)
                        dve.wait_ge(kept, i + 1)
                        add_total(x1)
                        layer_norm(v, steps, x1, x1, w)
                        layer_norm(v, steps, norm1, x1, w)
                        steps.then(v.tensor_tensor(norm1[:, :, :], norm1[:, :, :], spread("g1"), ALU.mult))
                        v.tensor_tensor(norm1[:, :, :], norm1[:, :, :], spread("be1"), ALU.add
                                        ).then_inc(norm1_ready, 1)
                    if q == 1:
                        turned_half(0)
                        turned_half(1)
                        dve.wait_ge(total_ready, i * 2 + 2)
                        dve.wait_ge(doubled, i + 1)
                        add_total(x2)
                        dve.sem_inc(x2_ready, 1)
                        dve.wait_ge(sent, i + 1)
                        layer_norm(v, steps, sent_rows[:, 0, :, 0:D], x2, w)
                        dve.wait_ge(kept, i + 2)
                        steps.then(v.tensor_tensor(x2[:, :, :], sent_rows[:, 0, :, 0:D], spread("g2"), ALU.mult))
                        v.tensor_tensor(sent_rows[:, 0, :, 0:D], x2[:, :, :], spread("be2"), ALU.add
                                        ).then_inc(norm2_ready, 1)
                    if q == 2:
                        turned_half(0)
                        turned_half(1)
                        job.arrived()
                        logits = small[:, 0:GT * E].rearrange("p (a e) -> p a e", a=GT)
                        steps.then(v.tensor_reduce(lmax[:, :], logits, AX.X, ALU.max))
                        steps.then(v.tensor_tensor(logit[:, :, :], logits,
                                                   lmax[:, :].unsqueeze(2).broadcast_to([P, GT, E]), ALU.subtract))
                        dve.sem_inc(shifted, 1)
                        dve.sem_inc(small_read, 1)
                        dve.wait_ge(router_exp, i + 1)
                        steps.then(v.tensor_reduce(prob_sum[:, :], prob[:, :, :], AX.X, ALU.add))
                        steps.then(v.reciprocal(prob_sum[:, :], prob_sum[:, :]))
                        steps.then(v.tensor_tensor(prob[:, :, :], prob[:, :, :],
                                                   prob_sum[:, :].unsqueeze(2).broadcast_to([P, GT, E]), ALU.mult))
                        v.tensor_copy(spare_v[:, :], prob[:, 0, 0:1])
                        for a in range(GT):
                            last = v.max(top[:, a, :], prob[:, a, :])
                        steps.then(last)
                        v.tensor_copy(spare_v[:, :], prob[:, 0, 0:1])
                        for a in range(GT):
                            last = v.max_index(top_i[:, a, :], top[:, a, :], prob[:, a, :])
                        steps.then(last)
                        steps.then(v.tensor_copy(top_f[:, :, :], top_i[:, :, 0:2].rearrange("p a n -> p n a")))
                        for n in range(2):
                            last = v.tensor_tensor(chosen[:, n, :, :],
                                                   iota_e[:, :].unsqueeze(1).broadcast_to([P, GT, E]),
                                                   top_f[:, n, :].unsqueeze(2).broadcast_to([P, GT, E]),
                                                   ALU.is_equal)
                        steps.then(last)
                        v.tensor_tensor(both[:, :, :], chosen[:, 0, :, :], chosen[:, 1, :, :], ALU.add
                                        ).then_inc(both_ready, 1)
                        v.tensor_copy(sent_rows[:, :, :, D + 1], top[:, :, 0:2].rearrange("p a n -> p n a"))
                        steps.then(v.tensor_copy(sent_rows[:, :, :, :].bitcast(I32)[:, :, :, D], home[:, :, :]))
                        steps.then(v.tensor_scalar(home[:, :, :], home[:, :, :], float(512), None, ALU.add))
                    if q == 3:
                        job.arrived()
                        counts = small[:, 0:2 * GT * E].rearrange("p (n a e) -> p n a e", n=2, a=GT)
                        for a in range(GT):
                            v.tensor_tensor(place[:, a, :], counts[:, 0, a, :], carry[:, :], ALU.add)
                            steps.then(v.tensor_tensor(carry[:, :], carry[:, :], counts[:, 1, a, :], ALU.add))
                        dve.sem_inc(small_read, 1)
                        for n in range(2):
                            last = v.tensor_tensor(picked[:, n, :, :], chosen[:, n, :, :], place[:, :, :], ALU.mult)
                        steps.then(last)
                        steps.then(v.tensor_reduce(pos_f[:, :, :], picked[:, :, :, :], AX.X, ALU.add))
                        dve.wait_ge(doubled, i + 2)
                        v.tensor_copy(pos[:, :, :], pos_f[:, :, :]).then_inc(placed, 1)

                for u in range(2):
                    v.memset(v_one[u][:, :, :, HD:], 1.0).then_inc(v_ones, 1)
                v.memset(k_rows[ROWS:ROWS_M, 0:QUAD, :], 1.0).then_inc(ones_ready, 1)
                dve.wait_ge(constants_ready, 8)
                v.tensor_scalar(carry[:, :], iota_e[:, :], float(REGION), None, ALU.mult).then_inc(carry_ready, 1)
                dve.wait_ge(carry_ready, 1)
                dve.sem_inc(doubled, 1)
                job = Job(0)
                for q in range(UNITS - 1):
                    head_output(0, q, job)
                dve.wait_ge(loaded_w, 16 * 9)
                with dve.Fori(1, GROUPS) as i:
                    job = Job(first_job(i))
                    steps = Chain(dve, step, (i - 1) * STEPS)
                    head_output(i - 1, UNITS - 1, job)
                    for q in range(UNITS):
                        route(i - 1, q, steps, job)
                        if q < UNITS - 1:
                            head_output(i, q, job)
                    assert job.n == JOBS and steps.n == STEPS, (job.n, steps.n)
                job = Job(first_job(GROUPS))
                steps = Chain(dve, step, (GROUPS - 1) * STEPS)
                head_output(GROUPS - 1, UNITS - 1, job)
                for q in range(UNITS):
                    route(GROUPS - 1, q, steps, job)
                plan(nc, dve, carry, keep, scratch, made, mapped)


def plan(nc, dve, carry, keep, scratch, made, mapped):
    v = nc.vector
    steps = Chain(dve, made)
    iota_e, iota_t = scratch["iota_e"], scratch["iota_t"]
    count, tiles_i, tiles, cum, cum2, last, tile = (scratch[n] for n in (
        "count", "tiles_i", "tiles", "cum", "cum2", "last", "tile"))
    passed, row = scratch["passed"], scratch["row"]
    steps.then(v.tensor_copy(keep["ends"][:, :], carry[:, :]))
    steps.then(v.scalar_tensor_tensor(count[:, :], iota_e[:, :], -float(REGION), carry[:, :], ALU.mult, ALU.add))
    steps.then(v.tensor_scalar(tiles_i[:, :], count[:, :], float(P - 1), None, ALU.add))
    steps.then(v.tensor_scalar(tiles_i[:, :], tiles_i[:, :], 7, None, ALU.logical_shift_right))
    steps.then(v.tensor_copy(tiles[:, :], tiles_i[:, :]))
    steps.then(v.tensor_copy(cum[:, :], tiles[:, :]))
    for k in (1, 2, 4):
        steps.then(v.tensor_copy(cum2[:, 0:k], cum[:, 0:k]))
        steps.then(v.tensor_tensor(cum2[:, k:], cum[:, k:], cum[:, 0:E - k], ALU.add))
        cum, cum2 = cum2, cum
    steps.then(v.tensor_scalar(last[:, :], cum[:, E - 1:E], -1.0, None, ALU.add))
    steps.then(v.tensor_scalar(tile[:, :], iota_t[:, :], last[:, 0:1], None, ALU.min))
    steps.then(v.tensor_tensor(passed[:, :, :], cum[:, :].unsqueeze(1).broadcast_to([P, TILES, E]),
                               tile[:, :].unsqueeze(2).broadcast_to([P, TILES, E]), ALU.is_le))
    steps.then(v.tensor_reduce(row[:, :], passed[:, :, :], AX.X, ALU.add))
    steps.then(v.tensor_copy(keep["tile_expert"][:, :], row[:, :]))
    steps.then(v.tensor_scalar(count[:, :], tiles[:, :], -float(P), float(REGION), ALU.mult, ALU.add))
    steps.then(v.tensor_tensor(passed[:, :, :], passed[:, :, :],
                               count[:, :].unsqueeze(1).broadcast_to([P, TILES, E]), ALU.mult))
    steps.then(v.tensor_reduce(row[:, :], passed[:, :, :], AX.X, ALU.add))
    steps.then(v.scalar_tensor_tensor(row[:, :], tile[:, :], float(P), row[:, :], ALU.mult, ALU.add))
    v.tensor_copy(keep["tile_row"][:, :], row[:, :]).then_inc(mapped, 1)


def experts(nc, dram, keep):
    FC = F // P
    RING = 6
    with ExitStack() as stack:
        m = Mem(nc, stack)
        x_in = m.sb("ex_x_in", [P, RING, ROW], F32)
        xT = m.sb("ex_xT", [P, 2, KC, P], F32)
        w1_now = m.sb("ex_w1_now", [P, 2, KC, F], F32)
        b1_now = m.sb("ex_b1_now", [P, RING, FC], F32)
        hT = m.sb("ex_hT", [P, 2, FC, P], F32)
        y = m.sb("ex_y", [P, 2, D], F32)
        b2 = m.sb("ex_b2", [P, E, D], F32)
        spare = m.sb("ex_spare", [P, 2], F32)
        p_x = m.ps("ex_px", [P, KC, P])
        p_h = [m.ps(f"ex_ph{u}", [P, FC, P]) for u in range(2)]
        p_y = [m.ps(f"ex_py{u}", [P, 512]) for u in range(2)]
        loaded_x = [m.sem(f"ex_loaded_x{r}") for r in range(RING)]
        loaded_b2 = m.sem("ex_loaded_b2")
        x_turned = m.sem("ex_x_turned")
        xT_ready = m.sem("ex_xT_ready")
        w1_ready = m.sem("ex_w1_ready")
        b1_ready = m.sem("ex_b1_ready")
        hidden = m.sem("ex_hidden")
        h_ready = m.sem("ex_h_ready")
        y_done = m.sem("ex_y_done")
        y_sum = m.sem("ex_y_sum")
        y_ready = m.sem("ex_y_ready")
        scattered = m.sem("ex_scattered")
        y_free = m.sem("ex_y_free")
        y_seen = m.sem("ex_y_seen")
        identity, w1, w2 = keep["identity"], keep["w1"], keep["w2"]

        with nc.Block() as block:

            @block.sync
            def _(sp):
                def load(turn, r):
                    i = turn * RING + r
                    row = sp.value_load(keep["tile_row"][0:1, bass.ds(i, 1)], min_val=0, max_val=E * REGION - P)
                    sp.wait_ge(y_free, i + 1)
                    sp.dma_start(x_in[:, r, :], dram["rows_in"][bass.ds(row, P), :]).then_inc(loaded_x[r], 16)

                for r in range(RING):
                    load(0, r)
                sp.dma_start(b2[:, :, :], dram["b2"].partition_broadcast(P)).then_inc(loaded_b2, 16)
                with sp.Fori(1, TILES // RING) as turn:
                    for r in range(RING):
                        load(turn, r)

            @block.gpsimd
            def _(pool):
                pool.sem_inc(y_free, RING)
                with pool.Fori(0, TILES // RING) as turn:
                    for r in range(RING):
                        i = turn * RING + r
                        pool.wait_ge(y_ready, i + 3)
                        pool.wait_ge(y_free, i + RING)
                        nc.gpsimd.tensor_tensor(spare[:, 0:1], y[:, r % 2, 0:1], y[:, r % 2, 1:2], ALU.add
                                                ).then_inc(y_seen, 1)
                        nc.gpsimd.indirect_dma_start(
                            out=dram["rows_out"], in_=y[:, r % 2, :], in_offset=None,
                            out_offset=bass.IndirectOffsetOnAxis(ap=x_in[:, r, D:D + 1].bitcast(U32), axis=0)
                        ).then_inc(scattered, 16)
                        pool.wait_ge(scattered, i * 16 + 16)
                        pool.wait_ge(y_seen, i + 1)
                        nc.gpsimd.tensor_tensor(spare[:, 1:2], y[:, r % 2, 0:1], y[:, r % 2, 1:2], ALU.add
                                                ).then_inc(y_free, 1)

            @block.scalar
            def _(act):
                act.sem_inc(h_ready, 4)
                with act.Fori(0, TILES // RING) as turn:
                    for r in range(RING):
                        i, u = turn * RING + r, r % 2
                        act.wait_ge(y_done, i + 1)
                        act.wait_ge(b1_ready, i + 1)
                        for fc in range(FC):
                            act.wait_ge(hidden, i * 2 + 1 + fc // (FC // 2))
                            last = nc.scalar.activation(hT[:, u, fc, :], p_h[u][:, fc, :], ACT.Silu,
                                                        bias=b1_now[:, r, fc:fc + 1])
                            if fc % (FC // 2) == FC // 2 - 1:
                                last.then_inc(h_ready, 1)

            @block.vector
            def _(dve):
                v = nc.vector

                def fetch(turn, r, i):
                    e = dve.value_load(keep["tile_expert"][0:1, bass.ds(i, 1)], min_val=0, max_val=E - 1)
                    dve.wait_ge(x_turned, i + 1)
                    v.tensor_copy(xT[:, r % 2, :, :], p_x[:, :, :]).then_inc(xT_ready, 1)
                    v.tensor_copy(b1_now[:, r, :], keep["b1"][:, bass.ds(e, 1), :].rearrange("p o c -> p (o c)")
                                  ).then_inc(b1_ready, 1)
                    v.tensor_copy(w1_now[:, r % 2, :, :], w1[:, bass.ds(e, 1), :, :]
                                  .rearrange("p o s n -> p (o s) n")).then_inc(w1_ready, 1)

                dve.sem_inc(y_ready, 2)
                dve.wait_ge(keep["loaded_w1"], 16 * E)
                fetch(None, 0, 0)
                fetch(None, 1, 1)
                dve.wait_ge(hidden, 2)
                fetch(None, 2, 2)

                def tile(turn, r, is_last):
                    i, u = turn * RING + r, r % 2
                    if not (is_last and r >= RING - 3):
                        dve.wait_ge(hidden, i * 2 + 4)
                        fetch(turn, (r + 3) % RING, i + 3)
                    e = dve.value_load(keep["tile_expert"][0:1, bass.ds(i, 1)], min_val=0, max_val=E - 1)
                    dve.wait_ge(y_done, i + 3)
                    dve.wait_ge(y_free, i + RING - 1)
                    v.tensor_tensor(y[:, u, :], p_y[u][:, 0:D], b2[:, bass.ds(e, 1), :]
                                    .rearrange("p o n -> p (o n)"), ALU.add).then_inc(y_sum, 1)
                    dve.wait_ge(y_sum, i + 1)
                    v.tensor_scalar(y[:, u, :], y[:, u, :], x_in[:, r, D + 1:D + 2], None, ALU.mult
                                    ).then_inc(y_ready, 1)

                dve.wait_ge(loaded_b2, 16)
                with dve.Fori(0, TILES // RING - 1) as turn:
                    for r in range(RING):
                        tile(turn, r, False)
                for r in range(RING):
                    tile(TILES // RING - 1, r, True)

            @block.tensor
            def _(pe):
                def turn_x(turn, r, i, first=False):
                    pe.wait_ge(loaded_x[r], turn * 16 + 16)
                    if not first:
                        pe.wait_ge(xT_ready, i)
                    for kc in range(KC):
                        last = nc.tensor.transpose(p_x[:, kc, :], x_in[:, r, kc * P:(kc + 1) * P], identity[:, :])
                    last.then_inc(x_turned, 1)

                def hide(u, i):
                    pe.wait_ge(xT_ready, i + 1)
                    pe.wait_ge(w1_ready, i + 1)
                    pe.wait_ge(h_ready, i * 2 + 2)
                    for fc in range(FC):
                        for kc in range(KC):
                            last = nc.tensor.matmul(p_h[u][:, fc, :], w1_now[:, u, kc, fc * P:(fc + 1) * P],
                                                    xT[:, u, kc, :], start=(kc == 0), stop=(kc == KC - 1))
                        if fc % (FC // 2) == FC // 2 - 1:
                            last.then_inc(hidden, 1)

                def reduce(u, i):
                    e = pe.value_load(keep["tile_expert"][0:1, bass.ds(i, 1)], min_val=0, max_val=E - 1)
                    pe.wait_ge(y_ready, i + 1)
                    for fc in range(FC):
                        pe.wait_ge(h_ready, i * 2 + 5 + fc // (FC // 2))
                        last = nc.tensor.matmul(p_y[u][:, 0:D], hT[:, u, fc, :],
                                                w2[:, bass.ds(e, 1), fc, :].rearrange("p o n -> p (o n)"),
                                                start=(fc == 0), stop=(fc == FC - 1))
                    last.then_inc(y_done, 1)

                def tile(turn, r, is_last):
                    i, u = turn * RING + r, r % 2
                    if not (is_last and r == RING - 1):
                        hide(1 - u, i + 1)
                    if not (is_last and r >= RING - 3):
                        turn_x(turn + (r + 3) // RING, (r + 3) % RING, i + 3)
                    reduce(u, i)

                pe.sem_inc(y_done, 2)
                turn_x(0, 0, 0, first=True)
                turn_x(0, 1, 1)
                hide(0, 0)
                turn_x(0, 2, 2)
                pe.wait_ge(keep["loaded_w2"], 16 * E)
                with pe.Fori(0, TILES // RING - 1) as turn:
                    for r in range(RING):
                        tile(turn, r, False)
                for r in range(RING):
                    tile(TILES // RING - 1, r, True)


def combine(nc, dram, keep):
    with ExitStack() as stack:
        m = Mem(nc, stack)
        got = m.sb("cb_got", [P, 2, 3, GT, D], F32)
        half = m.sb("cb_half", [P, 2, GT, D], F32)
        total = m.sb("cb_total", [P, GT, D], F32)
        out = m.sb("cb_out", [P, 2, GT, D], F32)
        w = norm_scratch(m, "cb_ln")
        loaded = [m.sem(f"cb_loaded{u}") for u in range(2)]
        halved = m.sem("cb_halved")
        added = m.sem("cb_added")
        step = m.sem("cb_step")
        normed = m.sem("cb_normed")
        stored = [m.sem(f"cb_stored{u}") for u in range(2)]
        STEPS = LN_STEPS
        out_rows = dram["out"].rearrange("b s c -> (b s) c")

        with nc.Block() as block:

            @block.sync
            def _(sp):
                sp.sem_inc(added, 2)
                with sp.Fori(0, GROUPS // 2) as pair:
                    for u in range(2):
                        g = pair * 2 + u
                        sp.wait_ge(added, g + 1)
                        for n, src in enumerate((dram["kept"][bass.ds(g * 512, 512), :],
                                                 dram["rows_out"][bass.ds(g * 512, 512), :],
                                                 dram["rows_out"][bass.ds(g * 512 + T, 512), :])):
                            sp.dma_start(got[:, u, n, :, :], src.rearrange("(a p) n -> p a n", p=P)
                                         ).then_inc(loaded[u], 16)

            @block.gpsimd
            def _(pool):
                with pool.Fori(0, GROUPS // 2) as pair:
                    for u in range(2):
                        pool.wait_ge(added, pair * 2 + u + 1)
                        pool.wait_ge(loaded[u], pair * 48 + 48)
                        nc.gpsimd.tensor_tensor(half[:, u, :, :], got[:, u, 0, :, :], got[:, u, 1, :, :], ALU.add
                                                ).then_inc(halved, 1)

            @block.vector
            def _(dve):
                v = nc.vector
                with dve.Fori(0, GROUPS // 2) as pair:
                    for u in range(2):
                        g = pair * 2 + u
                        steps = Chain(dve, step, g * STEPS)
                        dve.wait_ge(halved, g + 1)
                        v.tensor_tensor(total[:, :, :], half[:, u, :, :], got[:, u, 2, :, :], ALU.add
                                        ).then_inc(added, 1)
                        dve.wait_ge(added, g + 3)
                        dve.wait_ge(stored[u], pair * 16 + 16)
                        layer_norm(v, steps, out[:, u, :, :], total, w)
                        assert steps.n == STEPS, steps.n

            @block.scalar
            def _(act):
                for u in range(2):
                    act.sem_inc(stored[u], 16)
                with act.Fori(0, GROUPS // 2) as pair:
                    for u in range(2):
                        g = pair * 2 + u
                        act.wait_ge(step, (g + 1) * STEPS)
                        act.dma_start(out_rows[bass.ds(g * 512, 512), :].rearrange("(a p) n -> p a n", p=P),
                                      out[:, u, :, :]).then_inc(stored[u], 16)
                for u in range(2):
                    act.wait_ge(stored[u], 16 * (GROUPS // 2 + 1))


def program(nc, dram):
    with ExitStack() as stack:
        m = Mem(nc, stack)
        keep = {
            "identity": m.sb("identity", [P, P], F32),
            "identity16": m.sb("identity16", [P, P], BF16),
            "ends": m.sb("ends", [P, E], I32),
            "tile_expert": m.sb("tile_expert", [P, TILES], I32),
            "tile_row": m.sb("tile_row", [P, TILES], I32),
            "wide": m.sb("wide", [P, 1], I32),
            "wide_ready": m.sem("wide_ready"),
            "loaded_w1": m.sem("loaded_w1"),
            "loaded_w2": m.sem("loaded_w2"),
            "b1": m.sb("b1_turned", [P, E, F // P], F32),
            "w1_place": m.sb("w1_place", [P, E * KC * F], F32),
            "w2_place": m.sb("w2_place", [P, E * F // P * D], F32),
        }
        keep["w1"] = keep["w1_place"][:, :].rearrange("p (e s n) -> p e s n", e=E, s=KC)
        keep["w2"] = keep["w2_place"][:, :].rearrange("p (e s n) -> p e s n", e=E, s=F // P)
        keep["v_all"] = keep["w2_place"][:, 0:BH * KT * HD].rearrange("p (h a w) -> p h a w", h=BH, a=KT)
        constants(nc, dram, keep)
        with ExitStack() as first:
            f = Mem(nc, first)
            hi_all = keep["w1_place"][:, 0:2 * T].bitcast(BF16).rearrange("p (k n) -> p k n", k=4)
            squares = keep["w1_place"][:, 2 * T:4 * T].bitcast(BF16).rearrange("p (k n) -> p k n", k=4)
            key_sum = f.sb("key_sum", [P, KC, GROUPS], F32)
            project(nc, dram, keep, hi_all, squares, key_sum)
            bounds(nc, dram, keep, hi_all, squares, key_sum)
        maxima(nc, dram, keep)
        attend_and_route(nc, dram, keep)
        experts(nc, dram, keep)
        combine(nc, dram, keep)


_NAMES = {'x': 'L0_attn_x', 'qkv_w': 'L0_attn_qkv_w', 'qkv_b': 'L0_attn_qkv_b', 'out_w': 'L0_attn_out_w',
          'out_b': 'L0_attn_out_b', 'g1': 'L0_ffn_g1', 'be1': 'L0_ffn_be1', 'mix_w': 'L0_ffn_mix_w',
          'mix_b': 'L0_ffn_mix_b', 'g2': 'L0_ffn_g2', 'be2': 'L0_ffn_be2', 'router_w': 'L0_ffn_router_w',
          'w1': 'L0_ffn_w1', 'b1': 'L0_ffn_b1', 'w2': 'L0_ffn_w2', 'b2': 'L0_ffn_b2'}


def _trig_table():
    import numpy as np
    inv_freq = (1.0 / 10000.0 ** (np.arange(0, HD, 2, dtype=np.float32) / np.float32(HD))).astype(np.float32)
    angle = np.arange(H, dtype=np.float32)[:, None] * inv_freq[None, :]
    return np.stack([np.cos(angle), np.sin(angle)]).astype(np.float32).reshape(-1)


def kernel(**inputs):
    import numpy as _np
    import concourse.bacc as _bacc
    from concourse import mybir as _mybir
    from concourse.bass_utils import run_bass_kernel_spmd as _run

    nc = _bacc.Bacc("TRN2", target_bir_lowering=False, num_devices=1)
    arrays, dram = {}, {}
    for short, name in _NAMES.items():
        arrays["in_" + short] = _np.ascontiguousarray(inputs[name])
    arrays["in_trig"] = _trig_table()
    for name, a in arrays.items():
        dram[name[3:]] = nc.dram_tensor(name, a.shape, _mybir.dt.from_np(a.dtype), kind="ExternalInput").ap()
    dram["out"] = nc.dram_tensor("out_0", (B, S, D), F32, kind="ExternalOutput").ap()
    dram["qk"] = [nc.dram_tensor(f"{n}_parts", (PARTS, BH * HD, S), BF16, kind="Internal").ap() for n in "qk"]
    dram["negmax"] = nc.dram_tensor("negmax", (BH, PARTS, S), BF16, kind="Internal").ap()
    dram["rows_in"] = nc.dram_tensor("rows_in", (E * REGION, ROW), F32, kind="Internal").ap()
    dram["rows_out"] = nc.dram_tensor("rows_out", (2 * T + E * P, D), F32, kind="Internal").ap()
    dram["kept"] = nc.dram_tensor("kept", (T, D), F32, kind="Internal").ap()
    program(nc, dram)
    r = _run(nc, [arrays], core_ids=[0])
    return r.results[0]["out_0"]
```

```python
import concourse.bass as bass
from concourse import mybir
from contextlib import ExitStack

F32 = mybir.dt.float32
BF16 = mybir.dt.bfloat16
I32 = mybir.dt.int32
U32 = mybir.dt.uint32
ALU = mybir.AluOpType
ACT = mybir.ActivationFunctionType
AX = mybir.AxisListType

B, S, D = 2, 2048, 256
H, HD = 16, 16
E, F = 8, 1024
P = 128
BH = B * H
T = B * S
NT = T // P
KT = S // P
QC = S // 512
KC = D // P
GT = 4
GROUPS = NT // GT
PARTS = 3
Q_ORDER = (0, 0, 0, 1, 1, 2)
K_ORDER = (0, 1, 2, 0, 1, 0)
ROWS = HD * len(Q_ORDER)
ROWS_M = ROWS + PARTS
EPS = 1e-5
GAP = 110.0
QUAD = 4
UNITS = H // QUAD
REGION = T + P
ROW = D + 2
TILES = 72


class Mem:

    def __init__(self, nc, stack):
        self.nc, self.stack = nc, stack

    def sb(self, name, shape, dtype):
        return self.stack.enter_context(self.nc.sbuf_tensor(name, shape, dtype))

    def ps(self, name, shape, dtype=F32):
        return self.stack.enter_context(self.nc.psum_tensor(name, shape, dtype))

    def sem(self, name):
        return self.stack.enter_context(self.nc.semaphore(name))


class Chain:

    def __init__(self, engine, sem, base=0):
        self.engine, self.sem, self.base, self.n = engine, sem, base, 0

    def then(self, instruction):
        instruction.then_inc(self.sem, 1)
        self.n += 1
        self.engine.wait_ge(self.sem, self.base + self.n)


def constants(nc, dram, keep):
    with ExitStack() as stack:
        m = Mem(nc, stack)
        lines = E * F // P
        b_in = m.sb("co_b_in", [P, P], F32)
        p_b = m.ps("co_pb", [P, P])
        zeroed = m.sem("co_zeroed")
        filled = m.sem("co_filled")
        loaded = m.sem("co_loaded")
        turned = m.sem("co_turned")
        with nc.Block() as block:

            @block.sync
            def _(sp):
                sp.wait_ge(zeroed, 1)
                sp.dma_start(b_in[0:lines, :], dram["b1"].rearrange("e (c p) -> (e c) p", p=P)
                             ).then_inc(loaded, 16)

            @block.tensor
            def _(pe):
                pe.wait_ge(filled, 4)
                pe.wait_ge(loaded, 16)
                nc.tensor.transpose(p_b[:, :], b_in[:, :], keep["identity"][:, :]).then_inc(turned, 1)

            @block.vector
            def _(dve):
                nc.vector.memset(b_in[:, :], 0.0).then_inc(zeroed, 1)
                dve.wait_ge(turned, 1)
                nc.vector.tensor_copy(keep["b1"][:, :, :].rearrange("p e c -> p (e c)"), p_b[:, 0:lines])

            @block.gpsimd
            def _(pool):
                for tile in (keep["identity"], keep["identity16"]):
                    nc.gpsimd.memset(tile[:, :], 0.0).then_inc(filled, 1)
                pool.wait_ge(filled, 2)
                for tile in (keep["identity"], keep["identity16"]):
                    nc.gpsimd.affine_select(out=tile[:, :], in_=tile[:, :], compare_op=ALU.not_equal, fill=1.0,
                                            base=0, pattern=[[-1, P]], channel_multiplier=1).then_inc(filled, 1)


def project(nc, dram, keep, hi_all, squares, key_sum, select):
    with ExitStack() as stack:
        m = Mem(nc, stack)
        raw = m.sb("qkv_raw", [P, KC + 1, H * 3 * HD], F32)
        trig = m.sb("trig", [P, 2, H, HD // 2], F32)
        rot_a = m.sb("rot_a", [P, KC + 1, H, HD // 2], F32)
        rot_b = m.sb("rot_b", [P, KC + 1, H, HD // 2], F32)
        w_qk = m.sb("w_qk", [P, KC + 1, 4, P], F32)
        w_v = m.sb("w_v", [P, KC + 1, D], F32)
        bias_qk = m.sb("bias_qk", [P, 4], F32)
        x_in = m.sb("x_in", [P, 2, GT, D], F32)
        xT = m.sb("xT", [P, 2, KC, 512], F32)
        lower = m.sb("qk_lower", [P, 4, PARTS - 1, 512], BF16)
        rest = m.sb("qk_rest", [P, 4, 512], F32)
        p_x = [m.ps(f"p_x{i}", [P, 512]) for i in range(KC)]
        p_qk = [m.ps(f"p_qk{i}", [P, 512]) for i in range(4)]
        p_v = [m.ps(f"p_v{i}", [P, 2, D]) for i in range(2)]

        loaded_w = m.sem("pj_loaded_w")
        loaded_x = [m.sem(f"pj_loaded_x{i}") for i in range(2)]
        rot_step = m.sem("pj_rot_step")
        weights_rotated = m.sem("pj_weights_rotated")
        bias_turned = m.sem("pj_bias_turned")
        bias_ready = m.sem("pj_bias_ready")
        x_turned = m.sem("pj_x_turned")
        xT_ready = [m.sem(f"pj_xT_ready{i}") for i in range(KC)]
        qk_done = m.sem("pj_qk_done")
        v_done = m.sem("pj_v_done")
        hi_ready = m.sem("pj_hi_ready")
        rest_ready = m.sem("pj_rest_ready")
        mid_ready = m.sem("pj_mid_ready")
        lo_ready = m.sem("pj_lo_ready")
        v_ready = m.sem("pj_v_ready")
        filled = m.sem("pj_filled")
        stored = [m.sem(f"pj_stored{i}") for i in range(4)]

        x_rows = dram["x"].rearrange("b s c -> (b s) c")
        identity, v_all = keep["identity"], keep["v_all"]

        with nc.Block() as block:

            def store_parts(sp, b, c):
                for ft in range(4):
                    sp.wait_ge(lo_ready, b * (4 * QC) + 4 * c + ft + 1 + 4)
                    rows = bass.ds(b * D + (ft % 2) * P, P)
                    cols = slice(c * 512, (c + 1) * 512)
                    sp.dma_start(dram["qk"][ft // 2][0, rows, cols], hi_all[:, ft, bass.ds(b * S + c * 512, 512)]
                                 ).then_inc(stored[ft], 16)
                    sp.dma_start(dram["qk"][ft // 2][1:, rows, cols].rearrange("t r n -> r t n"), lower[:, ft, :, :]
                                 ).then_inc(stored[ft], 16)

            @block.sync
            def _(sp):
                sp.dma_start(raw[:, 0:KC, :], dram["qkv_w"].rearrange("(s p) n -> p s n", p=P)).then_inc(loaded_w, 16)
                sp.dma_start(raw[:, KC, :], dram["qkv_b"].partition_broadcast(P)).then_inc(loaded_w, 16)
                sp.dma_start(trig[:, :, :, :].rearrange("p t h j -> p (t h j)"),
                             dram["trig"].partition_broadcast(P)).then_inc(loaded_w, 16)
                sp.sem_inc(x_turned, 4)
                for i in range(4):
                    sp.sem_inc(stored[i], 32)

                def load_x(u, g):
                    sp.dma_start(x_in[:, u, :, :], x_rows[bass.ds(g * 512, 512), :].rearrange("(a p) n -> p a n", p=P)
                                 ).then_inc(loaded_x[u], 16)

                load_x(0, 0)
                with sp.Fori(0, B) as b:
                    for c in range(QC):
                        sp.wait_ge(x_turned, b * (2 * QC) + 2 * c + 4)
                        load_x((c + 1) % 2, b * QC + c + 1 if c < QC - 1 else b * -QC + QC)
                        if c == 0:
                            continue
                        store_parts(sp, b, c - 1)
                    store_parts(sp, b, QC - 1)
                for i in range(4):
                    sp.wait_ge(stored[i], 32 * (GROUPS + 1))

            @block.vector
            def _(dve):
                steps = Chain(dve, rot_step)
                dve.wait_ge(loaded_w, 48)
                heads = raw[:, :, :].rearrange("p s (h w) -> p s h w", w=3 * HD)
                cos = trig[:, 0, :, :].unsqueeze(1).broadcast_to([P, KC + 1, H, HD // 2])
                sin = trig[:, 1, :, :].unsqueeze(1).broadcast_to([P, KC + 1, H, HD // 2])
                for n in range(2):
                    u1 = heads[:, :, :, n * HD:n * HD + 8]
                    u2 = heads[:, :, :, n * HD + 8:n * HD + 16]
                    out = w_qk[:, :, 2 * n:2 * n + 2, :].rearrange("p s t (h w) -> p s (t h) w", w=HD)
                    nc.vector.tensor_tensor(rot_a[:, :, :, :], u1, cos, ALU.mult)
                    steps.then(nc.vector.tensor_tensor(rot_b[:, :, :, :], u2, sin, ALU.mult))
                    steps.then(nc.vector.tensor_tensor(out[:, :, :, 0:8], rot_a[:, :, :, :], rot_b[:, :, :, :],
                                                       ALU.subtract))
                    nc.vector.tensor_tensor(rot_a[:, :, :, :], u2, cos, ALU.mult)
                    steps.then(nc.vector.tensor_tensor(rot_b[:, :, :, :], u1, sin, ALU.mult))
                    steps.then(nc.vector.tensor_tensor(out[:, :, :, 8:16], rot_a[:, :, :, :], rot_b[:, :, :, :],
                                                       ALU.add))
                nc.vector.tensor_scalar(w_qk[:, :, 0:2, :], w_qk[:, :, 0:2, :], HD ** -0.5, None, ALU.mult)
                nc.vector.tensor_copy(w_v[:, :, :].rearrange("p s (h w) -> p s h w", w=HD),
                                      heads[:, :, :, 2 * HD:]).then_inc(weights_rotated, 1)
                dve.wait_ge(bias_turned, 1)
                nc.vector.tensor_copy(bias_qk[:, :], p_qk[0][:, :].rearrange("p (t n) -> p t n", t=4)[:, :, 0]
                                      ).then_inc(bias_ready, 1)
                dve.sem_inc(rest_ready, 4)
                dve.sem_inc(xT_ready[1], 1)
                dve.sem_inc(v_ready, 2)

                def copy_xT(u, g):
                    dve.wait_ge(x_turned, g * 2 + 2 + 4)
                    nc.vector.tensor_copy(xT[:, u, 1, :], p_x[1][:, :]).then_inc(xT_ready[1], 1)

                copy_xT(0, 0)
                with dve.Fori(0, B) as b:
                    for c in range(QC):
                        for ft in range(4):
                            at = b * (4 * QC) + 4 * c + ft
                            dve.wait_ge(hi_ready, at + 1)
                            dve.wait_ge(lo_ready, at + 1)
                            nc.vector.scalar_tensor_tensor(rest[:, ft, :], p_qk[ft][:, :], bias_qk[:, ft:ft + 1],
                                                           hi_all[:, ft, bass.ds(b * S + c * 512, 512)], ALU.add, ALU.subtract
                                                           ).then_inc(rest_ready, 1)
                        copy_xT((c + 1) % 2, b * QC + c + 1)
                        for i in range(2):
                            dve.wait_ge(v_done, b * (2 * QC) + 2 * c + i + 1)
                            dst = v_all[:, bass.ds(b * H, H), 4 * c + 2 * i:4 * c + 2 * i + 2, :]
                            nc.vector.tensor_tensor(
                                dst.rearrange("p h a w -> p a h w"),
                                p_v[i][:, :, :].rearrange("p a (h w) -> p a h w", w=HD),
                                w_v[:, KC, :].rearrange("p (h w) -> p h w", w=HD).unsqueeze(1)
                                .broadcast_to([P, 2, H, HD]), ALU.add).then_inc(v_ready, 1)

            @block.scalar
            def _(act):
                act.sem_inc(xT_ready[0], 1)
                act.wait_ge(bias_ready, 1)

                def copy_xT(u, g):
                    act.wait_ge(x_turned, g * 2 + 1 + 4)
                    nc.scalar.activation(xT[:, u, 0, :], p_x[0][:, :], ACT.Identity).then_inc(xT_ready[0], 1)

                copy_xT(0, 0)
                with act.Fori(0, B) as b:
                    for c in range(QC):
                        for ft in range(5):
                            if ft < 4:
                                at = b * (4 * QC) + 4 * c + ft
                                act.wait_ge(qk_done, at + 1)
                                hi = hi_all[:, ft, bass.ds(b * S + c * 512, 512)]
                                total = key_sum[:, ft - 2, bass.ds(b * QC + c, 1)] if ft >= 2 else None
                                nc.scalar.activation(hi, p_qk[ft][:, :], ACT.Identity, bias=bias_qk[:, ft:ft + 1],
                                                     accum_out=total).then_inc(hi_ready, 1)
                            if ft > 0:
                                at = b * (4 * QC) + 4 * c + ft - 1
                                act.wait_ge(rest_ready, at + 1 + 4)
                                act.wait_ge(stored[ft - 1], b * (32 * QC) + 32 * c + 32)
                                nc.scalar.activation(lower[:, ft - 1, 0, :], rest[:, ft - 1, :], ACT.Identity
                                                     ).then_inc(mid_ready, 1)
                        copy_xT((c + 1) % 2, b * QC + c + 1)

            @block.gpsimd
            def _(pool):
                nc.gpsimd.memset(select[:, :, :], 1.0).then_inc(filled, 1)
                for kc in range(KC):
                    pool.wait_ge(filled, 2 * kc + 1)
                    nc.gpsimd.affine_select(out=select[:, kc, :], in_=select[:, kc, :], compare_op=ALU.is_ge,
                                            fill=0.0, base=P * kc, pattern=[[-HD, 32]], channel_multiplier=1
                                            ).then_inc(filled, 1)
                    pool.wait_ge(filled, 2 * kc + 2)
                    nc.gpsimd.affine_select(out=select[:, kc, :], in_=select[:, kc, :], compare_op=ALU.is_ge,
                                            fill=0.0, base=HD - 1 - P * kc, pattern=[[HD, 32]],
                                            channel_multiplier=-1).then_inc(filled, 1)
                pool.wait_ge(filled, 5)
                nc.gpsimd.memset(keep["k_rows"][ROWS:ROWS_M, 0:QUAD, :], 1.0).then_inc(filled, 1)
                pool.wait_ge(filled, 6)
                pool.sem_inc(lo_ready, 4)
                with pool.Fori(0, B) as b:
                    for c in range(QC):
                        for ft in range(4):
                            pool.wait_ge(mid_ready, b * (4 * QC) + 4 * c + ft + 1)
                            nc.gpsimd.tensor_tensor(lower[:, ft, 1, :], rest[:, ft, :], lower[:, ft, 0, :],
                                                    ALU.subtract).then_inc(lo_ready, 1)
                            hi = hi_all[:, ft, bass.ds(b * S + c * 512, 512)]
                            nc.gpsimd.tensor_tensor(squares[:, ft, bass.ds(b * S + c * 512, 512)], hi, hi, ALU.mult)

            @block.tensor
            def _(pe):
                pe.wait_ge(weights_rotated, 1)
                for ft in range(4):
                    last = nc.tensor.transpose(p_qk[0][:, ft * P:(ft + 1) * P], w_qk[:, KC, ft, :], identity[:, :])
                last.then_inc(bias_turned, 1)

                def turn_x(u, pairs, g):
                    pe.wait_ge(loaded_x[u], pairs * 16 + 16)
                    for kc in range(KC):
                        pe.wait_ge(xT_ready[kc], g + 1)
                        for a in range(GT):
                            last = nc.tensor.transpose(p_x[kc][:, a * P:(a + 1) * P],
                                                       x_in[:, u, a, kc * P:(kc + 1) * P], identity[:, :])
                        last.then_inc(x_turned, 1)

                turn_x(0, 0, 0)
                pe.wait_ge(bias_ready, 1)
                with pe.Fori(0, B) as b:
                    for c in range(QC):
                        for kc in range(KC):
                            pe.wait_ge(xT_ready[kc], b * QC + c + 2)
                        for ft in range(4):
                            pe.wait_ge(rest_ready, b * (4 * QC) + 4 * c + ft + 1)
                            for kc in range(KC):
                                last = nc.tensor.matmul(p_qk[ft][:, :], w_qk[:, kc, ft, :], xT[:, c % 2, kc, :],
                                                        start=(kc == 0), stop=(kc == KC - 1))
                            last.then_inc(qk_done, 1)
                        turn_x((c + 1) % 2, b * (QC // 2) + (c + 1) // 2, b * QC + c + 1)
                        for i in range(2):
                            pe.wait_ge(v_ready, b * (2 * QC) + 2 * c + i + 1)
                            for a in range(2):
                                tok = (2 * i + a) * P
                                for kc in range(KC):
                                    last = nc.tensor.matmul(p_v[i][:, a, :], xT[:, c % 2, kc, tok:tok + P],
                                                            w_v[:, kc, :], start=(kc == 0), stop=(kc == KC - 1))
                            last.then_inc(v_done, 1)


def load_head(engine, dram, bh, q_rows, k_rows, loaded):
    for n, (part_q, part_k) in enumerate(zip(Q_ORDER, K_ORDER)):
        rows = slice(n * HD, (n + 1) * HD)
        engine.dma_start(q_rows[rows, :], dram["qk"][0][part_q, bass.ds(bh * HD, HD), :]).then_inc(loaded, 16)
        engine.dma_start(k_rows[rows, :], dram["qk"][1][part_k, bass.ds(bh * HD, HD), :]).then_inc(loaded, 16)


def maxima(nc, dram, keep):
    with ExitStack() as stack:
        m = Mem(nc, stack)
        q_rows = m.sb("mx_q", [P, S], BF16)
        k_rows = m.sb("mx_k", [P, S], BF16)
        negmax = m.sb("mx_negmax", [P, KT], F32)
        rest1 = m.sb("mx_rest1", [P, KT], F32)
        rest2 = m.sb("mx_rest2", [P, KT], F32)
        columns = m.sb("mx_columns", [P, P], BF16)
        parts = columns[:, 0:PARTS * KT].rearrange("p (t a) -> p t a", t=PARTS)
        turned = m.sb("mx_turned", [PARTS * KT, P], BF16)
        p_s = [m.ps(f"mx_s{i}", [P, S]) for i in range(2)]
        loaded = m.sem("mx_loaded")
        scored = m.sem("mx_scored")
        reduced = m.sem("mx_reduced")
        split = m.sem("mx_split")
        parts_ready = m.sem("mx_parts_ready")
        parts_turned = m.sem("mx_parts_turned")
        row_ready = m.sem("mx_row_ready")
        stored = m.sem("mx_stored")
        p_turn = p_s[0][:, 0:P // 2].bitcast(BF16)

        with nc.Block() as block:

            @block.sync
            def _(sp):
                wide = sp.value_load(keep["wide"][0:1, 0:1], min_val=0, max_val=P)
                with sp.If(wide > 0):
                    sp.sem_inc(stored, 16)
                    sp.sem_inc(parts_turned, 1)
                    with sp.Fori(0, BH) as bh:
                        sp.wait_ge(parts_turned, bh + 1)
                        load_head(sp, dram, bh, q_rows, k_rows, loaded)
                        sp.wait_ge(row_ready, bh + 1)
                        sp.dma_start(dram["negmax"][bass.ds(bh, 1), :, :].rearrange("o t (a n) -> (o t a) n", n=P),
                                     turned[:, :]).then_inc(stored, 16)
                    sp.wait_ge(stored, 16 * (BH + 1))

            @block.tensor
            def _(pe):
                wide = pe.value_load(keep["wide"][0:1, 0:1], min_val=0, max_val=P)
                with pe.If(wide > 0):
                    with pe.Fori(0, BH) as bh:
                        pe.wait_ge(loaded, (bh + 1) * (16 * 12))
                        for qt in range(KT):
                            if qt >= 2:
                                pe.wait_ge(reduced, bh * KT + qt - 1)
                            for c in range(QC):
                                last = nc.tensor.matmul(p_s[qt % 2][:, c * 512:(c + 1) * 512],
                                                        q_rows[0:ROWS, qt * P:(qt + 1) * P],
                                                        k_rows[0:ROWS, c * 512:(c + 1) * 512], start=True, stop=True)
                            last.then_inc(scored, 1)
                        pe.wait_ge(parts_ready, bh + 1)
                        nc.tensor.transpose(p_turn, columns[:, :],
                                            keep["identity16"][:, :]).then_inc(parts_turned, 1)
                        pe.wait_ge(row_ready, bh + 1)

            @block.vector
            def _(dve):
                wide = dve.value_load(keep["wide"][0:1, 0:1], min_val=0, max_val=P)
                with dve.If(wide > 0):
                    nc.vector.memset(columns[:, :], 0.0)
                    with dve.Fori(0, BH) as bh:
                        steps = Chain(dve, split, bh * 4)
                        for qt in range(KT):
                            dve.wait_ge(scored, bh * KT + qt + 1)
                            nc.vector.tensor_reduce(negmax[:, qt:qt + 1], p_s[qt % 2][:, :], AX.X, ALU.max, negate=True
                                                    ).then_inc(reduced, 1)
                        dve.wait_ge(reduced, bh * KT + KT)
                        dve.wait_ge(parts_turned, bh + 1)
                        steps.then(nc.vector.tensor_copy(parts[:, 0, :], negmax[:, :]))
                        steps.then(nc.vector.tensor_tensor(rest1[:, :], negmax[:, :], parts[:, 0, :], ALU.subtract))
                        steps.then(nc.vector.tensor_copy(parts[:, 1, :], rest1[:, :]))
                        steps.then(nc.vector.tensor_tensor(rest2[:, :], rest1[:, :], parts[:, 1, :], ALU.subtract))
                        nc.vector.tensor_copy(parts[:, 2, :], rest2[:, :]).then_inc(parts_ready, 1)
                        dve.wait_ge(parts_turned, bh + 2)
                        dve.wait_ge(stored, bh * 16 + 16)
                        nc.vector.tensor_copy(turned[:, :], p_turn[0:PARTS * KT, :]).then_inc(row_ready, 1)


def bounds(nc, dram, keep, hi_all, squares, key_sum, select):
    with ExitStack() as stack:
        m = Mem(nc, stack)
        R = 32 * B
        key_mean = m.sb("bd_key_mean", [P, KC, B, 32], BF16)
        mean = m.sb("bd_mean", [P, KC, B], F32)
        longest = m.sb("bd_longest", [R, 1], F32)
        bound = m.sb("bd_bound", [R, S], F32)
        negmid = m.sb("bd_negmid", [R, S], BF16)
        zeros = m.sb("bd_zeros", [BH, (PARTS - 1) * S], BF16)
        widest = m.sb("bd_widest", [P, 1], F32)
        narrow = m.sb("bd_narrow", [P, 1], BF16)
        ones = m.sb("bd_ones", [P, P], BF16)
        p_q = m.ps("bd_pq", [P, S])
        p_k = m.ps("bd_pk", [P, S])
        zeroed = m.sem("bd_zeroed")
        step = m.sem("bd_step")
        mean_ready = m.sem("bd_mean_ready")
        k_normed = m.sem("bd_k_normed")
        q_normed = m.sem("bd_q_normed")
        longest_ready = m.sem("bd_longest_ready")
        averaged = m.sem("bd_averaged")
        bound_ready = m.sem("bd_bound_ready")
        mid_ready = m.sem("bd_mid_ready")
        narrow_ready = m.sem("bd_narrow_ready")
        counted = m.sem("bd_counted")
        stored = m.sem("bd_stored")

        with nc.Block() as block:

            @block.gpsimd
            def _(pool):
                nc.gpsimd.memset(zeros[:, :].bitcast(U32), 0).then_inc(zeroed, 1)

            @block.sync
            def _(sp):
                load_k(sp, dram, keep, 0, 0)
                sp.wait_ge(zeroed, 1)
                sp.dma_start(dram["negmax"][:, 1:, :].rearrange("h t n -> h (t n)"), zeros[:, :]).then_inc(stored, 16)
                sp.wait_ge(mid_ready, 1)
                for b in range(B):
                    sp.dma_start(dram["negmax"][b * H:(b + 1) * H, 0, :], negmid[32 * b:32 * b + H, :]
                                 ).then_inc(stored, 16)
                sp.wait_ge(stored, 16 * (1 + B))

            @block.tensor
            def _(pe):
                def per_head(dst, b, weights, moving, sem):
                    for c in range(QC):
                        tok = slice(b * S + c * 512, b * S + (c + 1) * 512)
                        for kc in range(KC):
                            last = nc.tensor.matmul(dst[32 * b:32 * b + 32, c * 512:(c + 1) * 512],
                                                    weights(kc, b), moving(kc, tok),
                                                    start=(kc == 0), stop=(kc == KC - 1))
                    last.then_inc(sem, 1)

                for b in range(B):
                    per_head(p_k, b, lambda kc, b: select[:, kc, :], lambda kc, t: squares[:, 2 + kc, t], k_normed)
                for b in range(B):
                    per_head(p_q, b, lambda kc, b: select[:, kc, :], lambda kc, t: squares[:, kc, t], q_normed)
                pe.wait_ge(longest_ready, 1)
                pe.wait_ge(mean_ready, 1)
                for b in range(B):
                    per_head(p_k, b, lambda kc, b: key_mean[:, kc, b, :], lambda kc, t: hi_all[:, kc, t], averaged)
                pe.wait_ge(narrow_ready, 1)
                nc.tensor.matmul(p_q[:, 0:1], ones[:, :], narrow[:, :], start=True, stop=True).then_inc(counted, 1)

            @block.scalar
            def _(act):
                act.wait_ge(longest_ready, 1)
                act.wait_ge(q_normed, B)
                nc.scalar.activation(bound[:, :], p_q[0:R, :], ACT.Sqrt, scale=longest[:, 0:1]
                                     ).then_inc(bound_ready, 1)

            @block.vector
            def _(dve):
                v = nc.vector
                steps = Chain(dve, step)
                v.memset(ones[:, :], 1.0)
                v.memset(widest[:, :], 0.0)
                steps.then(v.tensor_reduce(mean[:, :, :], key_sum[:, :, :].rearrange("p k (b c) -> p k b c", b=B),
                                           AX.X, ALU.add))
                steps.then(v.tensor_scalar(mean[:, :, :], mean[:, :, :], -0.5 / S, None, ALU.mult))
                for kc in range(KC):
                    for b in range(B):
                        last = v.tensor_scalar(key_mean[:, kc, b, :], select[:, kc, :], mean[:, kc, b:b + 1], None,
                                               ALU.mult)
                last.then_inc(mean_ready, 1)
                dve.wait_ge(k_normed, B)
                v.tensor_reduce(longest[:, :], p_k[0:R, :], AX.X, ALU.max).then_inc(longest_ready, 1)
                dve.wait_ge(bound_ready, 1)
                dve.wait_ge(averaged, B)
                v.scalar_tensor_tensor(negmid[:, :], bound[:, :], -0.5, p_k[0:R, :], ALU.mult, ALU.add
                                       ).then_inc(mid_ready, 1)
                steps.then(v.scalar_tensor_tensor(bound[:, :], p_k[0:R, :], 2.0, bound[:, :], ALU.mult, ALU.add))
                steps.then(v.tensor_reduce(widest[0:R, :], bound[:, :], AX.X, ALU.max))
                v.tensor_scalar(narrow[:, :], widest[:, :], GAP, None, ALU.is_le).then_inc(narrow_ready, 1)
                dve.wait_ge(counted, 1)
                v.tensor_scalar(keep["wide"][:, :], p_q[:, 0:1], -1.0, float(P), ALU.mult, ALU.add
                                ).then_inc(keep["wide_ready"], 1)


def inverse_root(dve, steps, out, var, w):
    v, half, y = dve, w["half"], out
    v.tensor_scalar(half, var, -0.5, None, ALU.mult)
    steps.then(v.tensor_scalar(w["bits"], var.bitcast(I32), 1, None, ALU.logical_shift_right))
    steps.then(v.tensor_scalar(y.bitcast(I32), w["bits"], -1.0, float(0x5F3759DF), ALU.mult, ALU.add))
    for _ in range(2):
        steps.then(v.tensor_tensor(w["t"], y, y, ALU.mult))
        steps.then(v.tensor_tensor(w["t"], w["t"], half, ALU.mult))
        steps.then(v.scalar_tensor_tensor(y, w["t"], 1.5, y, ALU.add, ALU.mult))
    steps.then(v.tensor_tensor(w["t"], y, y, ALU.mult))
    steps.then(v.tensor_tensor(w["t"], w["t"], half, ALU.mult))
    steps.then(v.scalar_tensor_tensor(w["t"], w["t"], 0.5, y, ALU.add, ALU.mult))
    steps.then(v.tensor_tensor(y, y, w["t"], ALU.add))


ROOT_STEPS = 2 + 2 * 3 + 4
LN_SCALE_STEPS = 1 + 3 + ROOT_STEPS + 1
LN_STEPS = LN_SCALE_STEPS + 1


def norm_scale(dve, steps, inp, w):
    for a in range(GT):
        last = dve.bn_stats(w["stats"][:, a, :], inp[:, a, :])
    steps.then(last)
    stats = w["stats"]
    dve.tensor_tensor(w["mean2"], stats[:, :, 1], stats[:, :, 4], ALU.add)
    dve.scalar_tensor_tensor(w["var"], stats[:, :, 2], D * EPS, stats[:, :, 5], ALU.add, ALU.add)
    steps.then(dve.tensor_tensor(w["apart"], stats[:, :, 1], stats[:, :, 4], ALU.subtract))
    steps.then(dve.scalar_tensor_tensor(w["apart"], w["apart"], 0.25, w["apart"], ALU.mult, ALU.mult))
    steps.then(dve.scalar_tensor_tensor(w["var"], w["var"], 1.0 / D, w["apart"], ALU.mult, ALU.add))
    inverse_root(dve, steps, w["rstd"], w["var"], w)
    steps.then(dve.scalar_tensor_tensor(w["shift"], w["mean2"], -0.5, w["rstd"], ALU.mult, ALU.mult))


def layer_norm(dve, steps, out, inp, w):
    norm_scale(dve, steps, inp, w)
    for a in range(GT):
        last = dve.tensor_scalar(out[:, a, :], inp[:, a, :], w["rstd"][:, a:a + 1], w["shift"][:, a:a + 1],
                                 ALU.mult, ALU.add)
    steps.then(last)


def norm_scratch(m, name):
    w = {"stats": m.sb(name + "_stats", [P, GT, 6], F32),
         "bits": m.sb(name + "_bits", [P, GT], I32)}
    for n in ("var", "apart", "mean2", "rstd", "shift", "half", "t"):
        w[n] = m.sb(f"{name}_{n}", [P, GT], F32)
    return {n: t[tuple(slice(None) for _ in t.shape)] for n, t in w.items()}


def load_k(sp, dram, keep, b, q):
    for n, part in enumerate(K_ORDER):
        src = dram["qk"][1][part, (b * H + q * QUAD) * HD:(b * H + (q + 1) * QUAD) * HD, :]
        sp.dma_start(keep["k_rows"][n * HD:(n + 1) * HD, q * QUAD:(q + 1) * QUAD, :],
                     src.rearrange("(h w) n -> w h n", w=HD)).then_inc(keep["loaded_k"][q], 16)


def attend_and_route(nc, dram, keep):
    G3 = 3
    CHUNKS = KT * QUAD
    NG = -(-CHUNKS // G3)
    RING = 4
    NB = UNITS * NG
    JOBS0, JOBS = UNITS - 1, 16
    OUT_AT = (9, 11, 13, 14, 16, 18, 20, 21)
    MIX_AT = (40, 41, 42, 43, 44, 45, 46, 47)
    assert NB % RING == 0
    with ExitStack() as stack:
        m = Mem(nc, stack)
        k_rows = keep["k_rows"]
        probs_at = BH * KT * HD
        q_at = probs_at + RING * G3 * 512
        probs = keep["w2_place"][:, probs_at:q_at].rearrange("p (r n) -> p r n", r=RING)
        q_rows = [keep["w2_place"][:, q_at + u * 1024:q_at + (u + 1) * 1024].bitcast(BF16)
                  .rearrange("p (h n) -> p h n", h=QUAD) for u in range(2)]
        v_one = [m.sb(f"at_v{u}", [P, QUAD, KT, 2 * HD], F32) for u in range(2)]
        o_sb = [m.sb(f"at_o{u}", [P, 512], F32) for u in range(2)]
        rden = m.sb("at_rden", [P, GT, QUAD], F32)
        attn = m.sb("at_attn", [P, GT, D], F32)
        p_s = [m.ps(f"at_s{i}", [P, G3 * 512]) for i in range(2)]
        p_o = m.ps("at_po", [P, 512])
        small = m.ps("at_small", [P, 512])

        out_w = m.sb("rt_out_w", [P, KC, D], F32)
        mix_w = m.sb("rt_mix_w", [P, KC, D], F32)
        router_w = m.sb("rt_router_w", [P, KC, E], F32)
        rows = {n: m.sb("rt_" + n, [P, D], F32) for n in ("out_b", "g1", "be1", "mix_b", "g2", "be2")}
        x_in = m.sb("rt_x_in", [P, GT, D], F32)
        x1 = m.sb("rt_x1", [P, GT, D], F32)
        norm1 = m.sb("rt_norm1", [P, GT, D], F32)
        total = m.sb("rt_total", [P, GT, D], F32)
        x2 = m.sb("rt_x2", [P, GT, D], F32)
        sent_rows = m.sb("rt_sent_rows", [P, 2, GT, ROW], F32)
        turned = m.sb("rt_turned", [P, KC, 512], F32)
        w = norm_scratch(m, "rt_ln")
        logit = m.sb("rt_logit", [P, GT, E], F32)
        lmax = m.sb("rt_lmax", [P, GT], F32)
        prob = m.sb("rt_prob", [P, GT, E], F32)
        prob_sum = m.sb("rt_prob_sum", [P, GT], F32)
        top = m.sb("rt_top", [P, GT, 8], F32)
        top_i = m.sb("rt_top_i", [P, GT, 8], U32)
        top_f = m.sb("rt_top_f", [P, 2, GT], F32)
        chosen = m.sb("rt_chosen", [P, 2, GT, E], F32)
        both = m.sb("rt_both", [P, GT, E], BF16)
        place = m.sb("rt_place", [P, GT, E], F32)
        picked = m.sb("rt_picked", [P, 2, GT, E], F32)
        pos_f = m.sb("rt_pos_f", [P, 2, GT], F32)
        pos = m.sb("rt_pos", [P, 2, GT], U32)
        home = m.sb("rt_home", [P, 2, GT], I32)
        iota_e = m.sb("rt_iota_e", [P, E], F32)
        lower = m.sb("rt_lower", [P, P], BF16)
        ones = m.sb("rt_ones", [P, P], BF16)
        zero_rows = m.sb("rt_zero_rows", [P, D], F32)
        pad_home = m.sb("rt_pad_home", [P, E, 2], I32)
        spare = m.sb("rt_spare", [P, 1], F32)
        spare_v = m.sb("rt_spare_v", [P, 1], F32)
        carry = m.sb("rt_carry", [P, E], F32)
        scratch = {"iota_e": iota_e, "iota_t": m.sb("rt_iota_t", [P, TILES], F32),
                   "tiles_i": m.sb("rt_tiles_i", [P, E], I32), "last": m.sb("rt_last", [P, 1], F32),
                   "tile": m.sb("rt_tile", [P, TILES], F32), "row": m.sb("rt_row", [P, TILES], F32),
                   "passed": m.sb("rt_passed", [P, TILES, E], F32)}
        scratch.update({n: m.sb("rt_" + n, [P, E], F32) for n in ("count", "tiles", "cum", "cum2")})

        loaded_q = [m.sem(f"at_loaded_q{u}") for u in range(2)]
        loaded_k = keep["loaded_k"]
        v_ones = m.sem("at_v_ones")
        v_copied = m.sem("at_v_copied")
        scored = m.sem("at_scored")
        exp_done = m.sem("at_exp_done")
        weighed = m.sem("at_weighed")
        o_copied = m.sem("at_o_copied")
        rden_ready = m.sem("at_rden_ready")
        small_done = m.sem("at_small_done")
        small_read = m.sem("at_small_read")
        loaded_w = m.sem("rt_loaded_w")
        loaded_x = m.sem("rt_loaded_x")
        constants_ready = m.sem("rt_constants_ready")
        carry_ready = m.sem("rt_carry_ready")
        step = m.sem("rt_step")
        x_biased = m.sem("rt_x_biased")
        norm1_ready = m.sem("rt_norm1_ready")
        total_ready = m.sem("rt_total_ready")
        x2_ready = m.sem("rt_x2_ready")
        kept = m.sem("rt_kept")
        kept_stored = m.sem("rt_kept_stored")
        norm2_ready = m.sem("rt_norm2_ready")
        doubled = m.sem("rt_doubled")
        shifted = m.sem("rt_shifted")
        router_exp = m.sem("rt_router_exp")
        both_ready = m.sem("rt_both_ready")
        placed = m.sem("rt_placed")
        scattered = m.sem("rt_scattered")
        sent = m.sem("rt_sent")
        padded = m.sem("rt_padded")
        made = m.sem("rt_made")
        ended = m.sem("rt_ended")
        x_rows = dram["x"].rearrange("b s c -> (b s) c")
        v_all = keep["v_all"]
        STEPS = 3 * LN_STEPS + 19

        def chunks(g):
            return range(g * G3, min((g + 1) * G3, CHUNKS))

        def spread(name):
            return rows[name][:, :].unsqueeze(1).broadcast_to([P, GT, D])

        def first_job(i):
            return (i - 1) * JOBS + JOBS0

        with nc.Block() as block:

            @block.sync
            def _(sp):
                def load_q(b, c, q, unit):
                    u = q % 2
                    sp.wait_ge(scored, unit * NG + NG)
                    cols = bass.ds(c * 512, 512)
                    for n, part in enumerate(Q_ORDER):
                        src = dram["qk"][0][part, (b * H + q * QUAD) * HD:(b * H + (q + 1) * QUAD) * HD, cols]
                        sp.dma_start(q_rows[u][n * HD:(n + 1) * HD, :, :],
                                     src.rearrange("(h w) n -> w h n", w=HD)).then_inc(loaded_q[u], 16)
                    sp.dma_start(q_rows[u][ROWS:ROWS_M, :, :],
                                 dram["negmax"][b * H + q * QUAD:b * H + (q + 1) * QUAD, :, cols]
                                 .rearrange("h t n -> t h n")).then_inc(loaded_q[u], 16)

                def load_x(i):
                    sp.wait_ge(x_biased, i + 1)
                    sp.dma_start(x_in[:, :, :], x_rows[bass.ds(i * 512, 512), :].rearrange("(a p) n -> p a n", p=P)
                                 ).then_inc(loaded_x, 16)

                def keep_sum(i):
                    sp.wait_ge(kept, i + 2)
                    sp.dma_start(dram["kept"][bass.ds(i * 512, 512), :].rearrange("(a p) n -> p a n", p=P),
                                 total[:, :, :]).then_inc(kept_stored, 16)

                sp.sem_inc(scored, 2 * NG)
                load_q(0, 0, 0, 0)
                for q in range(1, UNITS):
                    load_k(sp, dram, keep, 0, q)
                    sp.dma_start(k_rows[ROWS:ROWS_M, q * QUAD:(q + 1) * QUAD, :], k_rows[ROWS:ROWS_M, 0:QUAD, :]
                                 ).then_inc(loaded_k[q], 16)
                    if q == 1:
                        load_q(0, 0, 1, 1)
                for dst, src in ((out_w, "out_w"), (mix_w, "mix_w"), (router_w, "router_w")):
                    sp.dma_start(dst[:, :, :], dram[src].rearrange("(s p) n -> p s n", p=P)).then_inc(loaded_w, 16)
                for name in rows:
                    sp.dma_start(rows[name][:, :], dram[name].partition_broadcast(P)).then_inc(loaded_w, 16)
                for q in range(2, UNITS):
                    load_q(0, 0, q, q)
                load_x(0)
                with sp.Fori(1, QC) as c:
                    for q in range(UNITS):
                        load_q(0, c, q, c * UNITS + q)
                    load_x(c)
                    keep_sum(c - 1)
                for q in range(UNITS):
                    sp.wait_ge(scored, 2 * NG + (QC - 1) * NB + (q + 1) * NG)
                    load_k(sp, dram, keep, 1, q)
                    load_q(1, 0, q, QC * UNITS + q)
                load_x(QC)
                keep_sum(QC - 1)
                with sp.Fori(1, QC) as c:
                    for q in range(UNITS):
                        load_q(1, c, q, (c + QC) * UNITS + q)
                    load_x(c + QC)
                    keep_sum(c + QC - 1)
                def load_w(name, experts):
                    for e in experts:
                        sp.dma_start(keep[name][:, e, :, :], dram[name][e].rearrange("(s p) n -> p s n", p=P)
                                     ).then_inc(keep["loaded_" + name], 16)

                w1_on_quad = E // UNITS
                w2_on_v = BH * KT * HD // (F // P * D)
                for q in range(UNITS):
                    if q == UNITS - 1:
                        sp.wait_ge(v_copied, GROUPS * UNITS)
                        load_w("w2", range(w2_on_v))
                    sp.wait_ge(scored, 2 * NG + (GROUPS - 1) * NB + (q + 1) * NG)
                    load_w("w1", range(q * w1_on_quad, (q + 1) * w1_on_quad))
                sp.wait_ge(weighed, GROUPS * NB + 2 * NG)
                load_w("w2", range(w2_on_v, E))
                keep_sum(GROUPS - 1)
                sp.wait_ge(ended, 1)
                for e in range(E):
                    end = sp.value_load(keep["ends"][0:1, e:e + 1], min_val=0, max_val=E * REGION - P)
                    sp.dma_start(dram["rows_in"][bass.ds(end, P), 0:D], zero_rows[:, :]).then_inc(padded, 16)
                    sp.dma_start(dram["rows_in"][bass.ds(end, P), D:ROW], pad_home[:, e, :].bitcast(F32)
                                 ).then_inc(padded, 16)
                sp.wait_ge(padded, 32 * E)
                sp.wait_ge(sent, GROUPS + 1)
                sp.wait_ge(kept_stored, 16 * (GROUPS + 1))

            @block.gpsimd
            def _(pool):
                def copy_v(unit, heads):
                    pool.wait_ge(weighed, unit * NG + NG)
                    nc.gpsimd.tensor_copy(v_one[heads[1] % 2][:, :, :, 0:HD],
                                          v_all[:, bass.ds(heads[0] * H + heads[1] * QUAD, QUAD), :, :]
                                          ).then_inc(v_copied, 1)

                def route(i, q):
                    if q == 0:
                        pool.wait_ge(loaded_x, i * 16 + 16)
                        pool.wait_ge(kept_stored, i * 16 + 16)
                        nc.gpsimd.tensor_tensor(total[:, :, :], x_in[:, :, :], spread("out_b"), ALU.add
                                                ).then_inc(x_biased, 1)
                    if q == 1:
                        pool.wait_ge(norm1_ready, i + 1)
                        nc.gpsimd.tensor_tensor(total[:, :, :], x1[:, :, :], norm1[:, :, :], ALU.add
                                                ).then_inc(total_ready, 1)
                        pool.wait_ge(total_ready, i * 2 + 1)
                        nc.gpsimd.tensor_tensor(total[:, :, :], total[:, :, :], spread("mix_b"), ALU.add
                                                ).then_inc(total_ready, 1)
                        pool.wait_ge(x2_ready, i + 1)
                        nc.gpsimd.tensor_tensor(total[:, :, :], x1[:, :, :], x2[:, :, :], ALU.add
                                                ).then_inc(kept, 1)
                        pool.wait_ge(norm2_ready, i + 1)
                        nc.gpsimd.tensor_tensor(sent_rows[:, 1, :, 0:D], norm1[:, :, :], spread("be2"), ALU.add
                                                ).then_inc(doubled, 1)
                    if q == 3:
                        pool.wait_ge(placed, i + 1)
                        nc.gpsimd.tensor_tensor(spare[:, :], lmax[:, 0:1], lmax[:, 1:2], ALU.add)
                        for n in range(2):
                            for a in range(GT):
                                nc.gpsimd.indirect_dma_start(
                                    out=dram["rows_in"], in_=sent_rows[:, n, a, :], in_offset=None,
                                    out_offset=bass.IndirectOffsetOnAxis(ap=pos[:, n, a:a + 1], axis=0)
                                ).then_inc(scattered, 16)
                        pool.wait_ge(scattered, (i + 1) * (16 * 2 * GT))
                        pool.sem_inc(sent, 1)

                g = nc.gpsimd
                g.memset(ones[:, :], 1.0).then_inc(constants_ready, 1)
                pool.wait_ge(constants_ready, 1)
                g.affine_select(out=lower[:, :], in_=ones[:, :], compare_op=ALU.is_gt, fill=0.0, base=0,
                                pattern=[[1, P]], channel_multiplier=-1).then_inc(constants_ready, 1)
                g.iota(iota_e[:, :], pattern=[[1, E]], base=0, channel_multiplier=0,
                       allow_small_or_imprecise_dtypes=True).then_inc(constants_ready, 1)
                g.iota(scratch["iota_t"][:, :], pattern=[[1, TILES]], base=0, channel_multiplier=0,
                       allow_small_or_imprecise_dtypes=True).then_inc(constants_ready, 1)
                g.iota(home[:, :, :], pattern=[[T, 2], [P, GT]], base=0, channel_multiplier=1
                       ).then_inc(constants_ready, 1)
                g.iota(pad_home[:, :, :], pattern=[[P, E], [0, 2]], base=2 * T, channel_multiplier=1
                       ).then_inc(constants_ready, 1)
                g.memset(zero_rows[:, :], 0.0).then_inc(constants_ready, 1)
                pool.wait_ge(constants_ready, 7)
                g.memset(pad_home[:, :, 1:2], 0).then_inc(constants_ready, 1)
                pool.wait_ge(v_ones, 2)
                pool.sem_inc(weighed, 2 * NG)
                copy_v(0, (0, 0))
                for q in range(1, UNITS):
                    copy_v(q, (0, q))
                copy_v(UNITS, (1 // QC, 0))
                pool.wait_ge(loaded_w, 16 * 9)
                pool.sem_inc(kept, 1)
                pool.sem_inc(sent, 1)
                pool.sem_inc(x_biased, 1)
                pool.sem_inc(kept_stored, 16)
                with pool.Fori(1, GROUPS - 1) as i:
                    for q in range(UNITS):
                        copy_v(i * UNITS + q + 1, ((i + (q + 1) // UNITS) // QC, (q + 1) % UNITS))
                        route(i - 1, q)
                for q in range(UNITS):
                    if q + 1 < UNITS:
                        copy_v((GROUPS - 1) * UNITS + q + 1, (B - 1, q + 1))
                    route(GROUPS - 2, q)
                for q in range(UNITS):
                    route(GROUPS - 1, q)

            @block.scalar
            def _(act):
                def exponentials(i, routed):
                    for n in range(NB):
                        width = 512 * len(chunks(n % NG))
                        act.wait_ge(scored, i * NB + n + 1 + 2 * NG)
                        act.wait_ge(weighed, i * NB + n + 1 - RING + 2 * NG)
                        nc.scalar.activation(probs[:, n % RING, 0:width], p_s[n % 2][:, 0:width], ACT.Exp
                                             ).then_inc(exp_done, 1)
                        if routed and n == 67:
                            router(i - 1)

                def router(i):
                    act.wait_ge(shifted, i + 1)
                    nc.scalar.activation(prob[:, :, :], logit[:, :, :], ACT.Exp).then_inc(router_exp, 1)

                exponentials(0, False)
                with act.Fori(1, GROUPS) as i:
                    exponentials(i, True)
                router(GROUPS - 1)

            @block.tensor
            def _(pe):
                def score(i, n):
                    q, g = n // NG, n % NG
                    if g == 0:
                        pe.wait_ge(loaded_k[q], (i // QC) * (16 * 6) + 16 * (6 if q == 0 else 7))
                        pe.wait_ge(loaded_q[q % 2], i * (2 * 16 * 7) + (q // 2 + 1) * (16 * 7))
                    for s, c in enumerate(chunks(g)):
                        kt, h = c // QUAD, c % QUAD
                        last = nc.tensor.matmul(p_s[n % 2][:, s * 512:(s + 1) * 512],
                                                k_rows[0:ROWS_M, q * QUAD + h, kt * P:(kt + 1) * P],
                                                q_rows[q % 2][0:ROWS_M, h, :], start=True, stop=True)
                    last.then_inc(scored, 1)

                def weigh(i, n):
                    q, g = n // NG, n % NG
                    if g == 0:
                        pe.wait_ge(v_copied, i * UNITS + q + 1)
                        pe.wait_ge(o_copied, i * UNITS + q + 1)
                    for s, c in enumerate(chunks(g)):
                        kt, h = c // QUAD, c % QUAD
                        last = nc.tensor.matmul(p_o[32 * h:32 * h + 32, :], v_one[q % 2][:, h, kt, :],
                                                probs[:, n % RING, s * 512:(s + 1) * 512],
                                                start=(kt == 0), stop=(kt == KT - 1))
                    last.then_inc(weighed, 1)

                def turn_out(i, q, job):
                    pe.wait_ge(o_copied, i * UNITS + q + 2)
                    pe.wait_ge(small_read, job + 1)
                    for a in range(GT):
                        last = nc.tensor.transpose(small[:, a * P:(a + 1) * P], o_sb[q % 2][:, a * P:(a + 1) * P],
                                                   keep["identity"][:, :])
                    last.then_inc(small_done, 1)

                def turn(src, kc, job):
                    pe.wait_ge(small_read, job + 1)
                    for a in range(GT):
                        last = nc.tensor.transpose(small[:, a * P:(a + 1) * P], src[:, a, kc * P:(kc + 1) * P],
                                                   keep["identity"][:, :])
                    last.then_inc(small_done, 1)

                def product(weights, tiles, width, job, pieces):
                    for piece in pieces:
                        n, kc = piece // KC, piece % KC
                        a = tiles[n]
                        if piece == 0:
                            pe.wait_ge(small_read, job + 1)
                        last = nc.tensor.matmul(small[:, n * width:(n + 1) * width],
                                                turned[:, kc, a * P:(a + 1) * P], weights[:, kc, :],
                                                start=(kc == 0), stop=(kc == KC - 1))
                    done = pieces[-1] == len(tiles) * KC - 1
                    if done:
                        last.then_inc(small_done, 1)
                    return int(done)

                def count(i, job):
                    pe.wait_ge(both_ready, i + 1)
                    pe.wait_ge(small_read, job + 1)
                    nc.tensor.matmul(small[:, 0:GT * E], lower[:, :], both[:, :, :], start=True, stop=True)
                    nc.tensor.matmul(small[:, GT * E:2 * GT * E], ones[:, :], both[:, :, :], start=True, stop=True,
                                     skip_group_check=True).then_inc(small_done, 1)

                def route(i, at, job):
                    if at == 5:
                        pe.wait_ge(rden_ready, i * (2 * UNITS) + 2 * UNITS)
                        turn(attn, 0, job)
                    elif at == 7:
                        turn(attn, 1, job)
                    elif at in OUT_AT:
                        n = OUT_AT.index(at)
                        return product(out_w, (0, 1) if n < 4 else (2, 3), D, job, (n % 4,))
                    elif at == 36:
                        pe.wait_ge(norm1_ready, i + 1)
                        turn(norm1, 0, job)
                    elif at == 38:
                        turn(norm1, 1, job)
                    elif at in MIX_AT:
                        n = MIX_AT.index(at)
                        return product(mix_w, (0, 1) if n < 4 else (2, 3), D, job, (n % 4,))
                    elif at == 58:
                        pe.wait_ge(norm2_ready, i + 1)
                        turn(sent_rows[:, 0, :, 0:D], 0, job)
                    elif at == 60:
                        turn(sent_rows[:, 0, :, 0:D], 1, job)
                    elif at in (61, 63):
                        return product(router_w, range(GT), E, job, range(4) if at == 61 else range(4, 8))
                    elif at == 76:
                        count(i, job)
                    else:
                        return 0
                    return 1

                def attend(i, routed, is_last, job):
                    for n in range(NB):
                        pe.wait_ge(exp_done, i * NB + n + 1)
                        if n + 2 < NB:
                            score(i, n + 2)
                        elif not is_last:
                            score(i + 1, n + 2 - NB)
                        weigh(i, n)
                        q, g = n // NG, n % NG
                        if q > 0 and g == (5 if q == 2 else 3):
                            turn_out(i, q - 1, job)
                            job = job + 1
                        if g == 3 and q == 0 and routed:
                            turn_out(i - 1, UNITS - 1, job)
                            job = job + 1
                        if routed:
                            job = job + route(i - 1, n, job)
                    return job

                pe.sem_inc(o_copied, 1)
                pe.sem_inc(small_read, 1)
                score(0, 0)
                score(0, 1)
                attend(0, False, False, 0)
                pe.wait_ge(loaded_w, 16 * 9)
                pe.wait_ge(constants_ready, 8)
                with pe.Fori(1, GROUPS - 1) as i:
                    attend(i, True, False, first_job(i))
                job = attend(GROUPS - 1, True, True, first_job(GROUPS - 1))
                turn_out(GROUPS - 1, UNITS - 1, job)
                job += 1
                for at in range(NB):
                    job += route(GROUPS - 1, at, job)

            @block.vector
            def _(dve):
                v = nc.vector

                class Job:
                    def __init__(self, first):
                        self.first, self.n = first, 0

                    def arrived(self):
                        dve.wait_ge(small_done, self.first + self.n + 1)
                        self.n += 1

                def copy_out(i, q):
                    dve.wait_ge(weighed, i * NB + (q + 1) * NG + 2 * NG)
                    v.tensor_copy(o_sb[q % 2][:, :], p_o[:, :]).then_inc(o_copied, 1)

                def divide(i, q, job):
                    job.arrived()
                    out = small[:, :].rearrange("p (a h w) -> p a h w", a=GT, h=QUAD)
                    v.reciprocal(rden[:, :, :], out[:, :, :, HD]).then_inc(rden_ready, 1)
                    dve.wait_ge(rden_ready, i * (2 * UNITS) + 2 * q + 1)
                    v.tensor_tensor(attn[:, :, q * QUAD * HD:(q + 1) * QUAD * HD]
                                    .rearrange("p a (h w) -> p a h w", w=HD), out[:, :, :, 0:HD],
                                    rden[:, :, :].unsqueeze(3).broadcast_to([P, GT, QUAD, HD]), ALU.mult
                                    ).then_inc(rden_ready, 1)
                    dve.wait_ge(rden_ready, i * (2 * UNITS) + 2 * q + 2)
                    dve.sem_inc(small_read, 1)

                def route(i, steps, job, beside):
                    def turned_half(kc):
                        job.arrived()
                        v.tensor_copy(turned[:, kc, :], small[:, :]).then_inc(small_read, 1)

                    def add_total(out, half):
                        job.arrived()
                        tiles = slice(2 * half, 2 * half + 2)
                        v.tensor_tensor(out[:, tiles, :], small[:, :].rearrange("p (a n) -> p a n", a=2),
                                        total[:, tiles, :], ALU.add).then_inc(small_read, 1)

                    turned_half(0)
                    turned_half(1)
                    dve.wait_ge(x_biased, i + 2)
                    dve.wait_ge(kept, i + 1)
                    add_total(x1, 0)
                    if beside:
                        copy_out(i + 1, 0)
                    add_total(x1, 1)
                    dve.wait_ge(small_read, job.first + job.n + 1)
                    if beside:
                        divide(i + 1, 0, job)
                    layer_norm(v, steps, x1, x1, w)
                    layer_norm(v, steps, norm1, x1, w)
                    steps.then(v.tensor_tensor(norm1[:, :, :], norm1[:, :, :], spread("g1"), ALU.mult))
                    v.tensor_tensor(norm1[:, :, :], norm1[:, :, :], spread("be1"), ALU.add
                                    ).then_inc(norm1_ready, 1)
                    turned_half(0)
                    turned_half(1)
                    dve.wait_ge(total_ready, i * 2 + 2)
                    add_total(x2, 0)
                    if beside:
                        copy_out(i + 1, 1)
                    add_total(x2, 1)
                    dve.wait_ge(small_read, job.first + job.n + 1)
                    dve.sem_inc(x2_ready, 1)
                    if beside:
                        divide(i + 1, 1, job)
                    dve.wait_ge(sent, i + 1)
                    layer_norm(v, steps, sent_rows[:, 0, :, 0:D], x2, w)
                    steps.then(v.tensor_tensor(norm1[:, :, :], sent_rows[:, 0, :, 0:D], spread("g2"), ALU.mult))
                    v.tensor_tensor(sent_rows[:, 0, :, 0:D], norm1[:, :, :], spread("be2"), ALU.add
                                    ).then_inc(norm2_ready, 1)
                    turned_half(0)
                    turned_half(1)
                    job.arrived()
                    logits = small[:, 0:GT * E].rearrange("p (a e) -> p a e", a=GT)
                    steps.then(v.tensor_reduce(lmax[:, :], logits, AX.X, ALU.max))
                    steps.then(v.tensor_tensor(logit[:, :, :], logits,
                                               lmax[:, :].unsqueeze(2).broadcast_to([P, GT, E]), ALU.subtract))
                    dve.sem_inc(shifted, 1)
                    dve.sem_inc(small_read, 1)
                    if beside:
                        copy_out(i + 1, 2)
                    dve.wait_ge(router_exp, i + 1)
                    steps.then(v.tensor_reduce(prob_sum[:, :], prob[:, :, :], AX.X, ALU.add))
                    steps.then(v.reciprocal(prob_sum[:, :], prob_sum[:, :]))
                    steps.then(v.tensor_tensor(prob[:, :, :], prob[:, :, :],
                                               prob_sum[:, :].unsqueeze(2).broadcast_to([P, GT, E]), ALU.mult))
                    v.tensor_copy(spare_v[:, :], prob[:, 0, 0:1])
                    for a in range(GT):
                        last = v.max(top[:, a, :], prob[:, a, :])
                    steps.then(last)
                    v.tensor_copy(spare_v[:, :], prob[:, 0, 0:1])
                    for a in range(GT):
                        last = v.max_index(top_i[:, a, :], top[:, a, :], prob[:, a, :])
                    steps.then(last)
                    steps.then(v.tensor_copy(top_f[:, :, :], top_i[:, :, 0:2].rearrange("p a n -> p n a")))
                    for n in range(2):
                        last = v.tensor_tensor(chosen[:, n, :, :],
                                               iota_e[:, :].unsqueeze(1).broadcast_to([P, GT, E]),
                                               top_f[:, n, :].unsqueeze(2).broadcast_to([P, GT, E]),
                                               ALU.is_equal)
                    steps.then(last)
                    v.tensor_tensor(both[:, :, :], chosen[:, 0, :, :], chosen[:, 1, :, :], ALU.add
                                    ).then_inc(both_ready, 1)
                    v.tensor_copy(sent_rows[:, :, :, D + 1], top[:, :, 0:2].rearrange("p a n -> p n a"))
                    steps.then(v.tensor_copy(sent_rows[:, :, :, :].bitcast(I32)[:, :, :, D], home[:, :, :]))
                    steps.then(v.tensor_scalar(home[:, :, :], home[:, :, :], float(512), None, ALU.add))
                    if beside:
                        divide(i + 1, 2, job)
                    job.arrived()
                    counts = small[:, 0:2 * GT * E].rearrange("p (n a e) -> p n a e", n=2, a=GT)
                    for a in range(GT):
                        v.tensor_tensor(place[:, a, :], counts[:, 0, a, :], carry[:, :], ALU.add)
                        steps.then(v.tensor_tensor(carry[:, :], carry[:, :], counts[:, 1, a, :], ALU.add))
                    dve.sem_inc(small_read, 1)
                    for n in range(2):
                        last = v.tensor_tensor(picked[:, n, :, :], chosen[:, n, :, :], place[:, :, :], ALU.mult)
                    steps.then(last)
                    steps.then(v.tensor_reduce(pos_f[:, :, :], picked[:, :, :, :], AX.X, ALU.add))
                    dve.wait_ge(doubled, i + 2)
                    v.tensor_copy(pos[:, :, :], pos_f[:, :, :]).then_inc(placed, 1)

                for u in range(2):
                    v.memset(v_one[u][:, :, :, HD:], 1.0).then_inc(v_ones, 1)
                dve.wait_ge(constants_ready, 8)
                v.tensor_scalar(carry[:, :], iota_e[:, :], float(REGION), None, ALU.mult).then_inc(carry_ready, 1)
                dve.wait_ge(carry_ready, 1)
                dve.sem_inc(doubled, 1)
                job = Job(0)
                for q in range(UNITS - 1):
                    copy_out(0, q)
                    divide(0, q, job)
                dve.wait_ge(loaded_w, 16 * 9)
                with dve.Fori(1, GROUPS) as i:
                    job = Job(first_job(i))
                    steps = Chain(dve, step, (i - 1) * STEPS)
                    copy_out(i - 1, UNITS - 1)
                    divide(i - 1, UNITS - 1, job)
                    route(i - 1, steps, job, True)
                    assert job.n == JOBS and steps.n == STEPS, (job.n, steps.n)
                job = Job(first_job(GROUPS))
                steps = Chain(dve, step, (GROUPS - 1) * STEPS)
                copy_out(GROUPS - 1, UNITS - 1)
                divide(GROUPS - 1, UNITS - 1, job)
                route(GROUPS - 1, steps, job, False)
                plan(nc, dve, carry, keep, scratch, made, ended)


def plan(nc, dve, carry, keep, scratch, made, ended):
    v = nc.vector
    steps = Chain(dve, made)
    iota_e, iota_t = scratch["iota_e"], scratch["iota_t"]
    count, tiles_i, tiles, cum, cum2, last, tile = (scratch[n] for n in (
        "count", "tiles_i", "tiles", "cum", "cum2", "last", "tile"))
    passed, row = scratch["passed"], scratch["row"]
    v.tensor_copy(keep["ends"][:, :], carry[:, :]).then_inc(ended, 1)
    steps.then(v.scalar_tensor_tensor(count[:, :], iota_e[:, :], -float(REGION), carry[:, :], ALU.mult, ALU.add))
    steps.then(v.tensor_scalar(tiles_i[:, :], count[:, :], float(P - 1), None, ALU.add))
    steps.then(v.tensor_scalar(tiles_i[:, :], tiles_i[:, :], 7, None, ALU.logical_shift_right))
    steps.then(v.tensor_copy(tiles[:, :], tiles_i[:, :]))
    steps.then(v.tensor_copy(cum[:, :], tiles[:, :]))
    for k in (1, 2, 4):
        steps.then(v.tensor_copy(cum2[:, 0:k], cum[:, 0:k]))
        steps.then(v.tensor_tensor(cum2[:, k:], cum[:, k:], cum[:, 0:E - k], ALU.add))
        cum, cum2 = cum2, cum
    steps.then(v.tensor_scalar(last[:, :], cum[:, E - 1:E], -1.0, None, ALU.add))
    steps.then(v.tensor_scalar(tile[:, :], iota_t[:, :], last[:, 0:1], None, ALU.min))
    steps.then(v.tensor_tensor(passed[:, :, :], cum[:, :].unsqueeze(1).broadcast_to([P, TILES, E]),
                               tile[:, :].unsqueeze(2).broadcast_to([P, TILES, E]), ALU.is_le))
    steps.then(v.tensor_reduce(row[:, :], passed[:, :, :], AX.X, ALU.add))
    steps.then(v.tensor_copy(keep["tile_expert"][:, :], row[:, :]))
    steps.then(v.tensor_scalar(count[:, :], tiles[:, :], -float(P), float(REGION), ALU.mult, ALU.add))
    steps.then(v.tensor_tensor(passed[:, :, :], passed[:, :, :],
                               count[:, :].unsqueeze(1).broadcast_to([P, TILES, E]), ALU.mult))
    steps.then(v.tensor_reduce(row[:, :], passed[:, :, :], AX.X, ALU.add))
    steps.then(v.scalar_tensor_tensor(row[:, :], tile[:, :], float(P), row[:, :], ALU.mult, ALU.add))
    v.tensor_copy(keep["tile_row"][:, :], row[:, :])


def experts(nc, dram, keep, kept):
    FC = F // P
    RING = 6
    with ExitStack() as stack:
        m = Mem(nc, stack)
        x_in = m.sb("ex_x_in", [P, RING, ROW], F32)
        xT = m.sb("ex_xT", [P, 2, KC, P], F32)
        w1_now = m.sb("ex_w1_now", [P, 2, KC, F], F32)
        b1_now = m.sb("ex_b1_now", [P, RING, FC], F32)
        hT = m.sb("ex_hT", [P, 2, FC, P], F32)
        y = m.sb("ex_y", [P, 2, D], F32)
        b2 = m.sb("ex_b2", [P, E, D], F32)
        spare = m.sb("ex_spare", [P, 2], F32)
        p_x = m.ps("ex_px", [P, KC, P])
        p_h = [m.ps(f"ex_ph{u}", [P, FC, P]) for u in range(2)]
        p_y = [m.ps(f"ex_py{u}", [P, 512]) for u in range(2)]
        loaded_x = [m.sem(f"ex_loaded_x{r}") for r in range(RING)]
        loaded_b2 = m.sem("ex_loaded_b2")
        x_turned = m.sem("ex_x_turned")
        xT_ready = m.sem("ex_xT_ready")
        w1_ready = m.sem("ex_w1_ready")
        b1_ready = m.sem("ex_b1_ready")
        hidden = m.sem("ex_hidden")
        h_ready = m.sem("ex_h_ready")
        y_done = m.sem("ex_y_done")
        y_sum = m.sem("ex_y_sum")
        y_ready = m.sem("ex_y_ready")
        scattered = m.sem("ex_scattered")
        y_free = m.sem("ex_y_free")
        y_seen = m.sem("ex_y_seen")
        identity, w1, w2 = keep["identity"], keep["w1"], keep["w2"]

        with nc.Block() as block:

            @block.sync
            def _(sp):
                def load(turn, r):
                    i = turn * RING + r
                    row = sp.value_load(keep["tile_row"][0:1, bass.ds(i, 1)], min_val=0, max_val=E * REGION - P)
                    sp.wait_ge(y_free, i + 1)
                    sp.dma_start(x_in[:, r, :], dram["rows_in"][bass.ds(row, P), :]).then_inc(loaded_x[r], 16)

                for r in range(RING):
                    load(0, r)
                sp.dma_start(b2[:, :, :], dram["b2"].partition_broadcast(P)).then_inc(loaded_b2, 16)
                sp.dma_start(kept[:, :, :], dram["kept"].rearrange("(a p) n -> p a n", p=P)
                             ).then_inc(keep["loaded_kept"], 16)
                with sp.Fori(1, TILES // RING) as turn:
                    for r in range(RING):
                        load(turn, r)

            @block.gpsimd
            def _(pool):
                pool.sem_inc(y_free, RING)
                with pool.Fori(0, TILES // RING) as turn:
                    for r in range(RING):
                        i = turn * RING + r
                        pool.wait_ge(y_ready, i + 3)
                        pool.wait_ge(y_free, i + RING)
                        nc.gpsimd.tensor_tensor(spare[:, 0:1], y[:, r % 2, 0:1], y[:, r % 2, 1:2], ALU.add
                                                ).then_inc(y_seen, 1)
                        nc.gpsimd.indirect_dma_start(
                            out=dram["rows_out"], in_=y[:, r % 2, :], in_offset=None,
                            out_offset=bass.IndirectOffsetOnAxis(ap=x_in[:, r, D:D + 1].bitcast(U32), axis=0)
                        ).then_inc(scattered, 16)
                        pool.wait_ge(scattered, i * 16 + 16)
                        pool.wait_ge(y_seen, i + 1)
                        nc.gpsimd.tensor_tensor(spare[:, 1:2], y[:, r % 2, 0:1], y[:, r % 2, 1:2], ALU.add
                                                ).then_inc(y_free, 1)

            @block.scalar
            def _(act):
                act.sem_inc(h_ready, 4)
                with act.Fori(0, TILES // RING) as turn:
                    for r in range(RING):
                        i, u = turn * RING + r, r % 2
                        act.wait_ge(y_done, i + 1)
                        act.wait_ge(b1_ready, i + 1)
                        for fc in range(FC):
                            act.wait_ge(hidden, i * 2 + 1 + fc // (FC // 2))
                            last = nc.scalar.activation(hT[:, u, fc, :], p_h[u][:, fc, :], ACT.Silu,
                                                        bias=b1_now[:, r, fc:fc + 1])
                            if fc % (FC // 2) == FC // 2 - 1:
                                last.then_inc(h_ready, 1)

            @block.vector
            def _(dve):
                v = nc.vector

                def fetch_rows(r, i):
                    dve.wait_ge(x_turned, i + 1)
                    v.tensor_copy(xT[:, r % 2, :, :], p_x[:, :, :]).then_inc(xT_ready, 1)

                def fetch_weights(r, i):
                    e = dve.value_load(keep["tile_expert"][0:1, bass.ds(i, 1)], min_val=0, max_val=E - 1)
                    v.tensor_copy(b1_now[:, r, :], keep["b1"][:, bass.ds(e, 1), :].rearrange("p o c -> p (o c)")
                                  ).then_inc(b1_ready, 1)
                    v.tensor_copy(w1_now[:, r % 2, :, :], w1[:, bass.ds(e, 1), :, :]
                                  .rearrange("p o s n -> p (o s) n")).then_inc(w1_ready, 1)

                dve.sem_inc(y_ready, 2)
                dve.wait_ge(keep["loaded_w1"], 16 * E)
                fetch_weights(0, 0)
                fetch_weights(1, 1)
                fetch_rows(0, 0)
                fetch_rows(1, 1)
                dve.wait_ge(hidden, 2)
                fetch_rows(2, 2)
                fetch_weights(2, 2)

                def tile(turn, r, is_last):
                    i, u = turn * RING + r, r % 2
                    if not (is_last and r >= RING - 3):
                        dve.wait_ge(hidden, i * 2 + 4)
                        fetch_rows((r + 3) % RING, i + 3)
                        fetch_weights((r + 3) % RING, i + 3)
                    e = dve.value_load(keep["tile_expert"][0:1, bass.ds(i, 1)], min_val=0, max_val=E - 1)
                    dve.wait_ge(y_done, i + 3)
                    dve.wait_ge(y_free, i + RING - 1)
                    v.tensor_tensor(y[:, u, :], p_y[u][:, 0:D], b2[:, bass.ds(e, 1), :]
                                    .rearrange("p o n -> p (o n)"), ALU.add).then_inc(y_sum, 1)
                    dve.wait_ge(y_sum, i + 1)
                    v.tensor_scalar(y[:, u, :], y[:, u, :], x_in[:, r, D + 1:D + 2], None, ALU.mult
                                    ).then_inc(y_ready, 1)

                dve.wait_ge(loaded_b2, 16)
                with dve.Fori(0, TILES // RING - 1) as turn:
                    for r in range(RING):
                        tile(turn, r, False)
                for r in range(RING):
                    tile(TILES // RING - 1, r, True)

            @block.tensor
            def _(pe):
                def turn_x(turn, r, i, first=False):
                    pe.wait_ge(loaded_x[r], turn * 16 + 16)
                    if not first:
                        pe.wait_ge(xT_ready, i)
                    for kc in range(KC):
                        last = nc.tensor.transpose(p_x[:, kc, :], x_in[:, r, kc * P:(kc + 1) * P], identity[:, :])
                    last.then_inc(x_turned, 1)

                def hide(u, i):
                    pe.wait_ge(xT_ready, i + 1)
                    pe.wait_ge(w1_ready, i + 1)
                    pe.wait_ge(h_ready, i * 2 + 2)
                    for fc in range(FC):
                        for kc in range(KC):
                            last = nc.tensor.matmul(p_h[u][:, fc, :], w1_now[:, u, kc, fc * P:(fc + 1) * P],
                                                    xT[:, u, kc, :], start=(kc == 0), stop=(kc == KC - 1))
                        if fc % (FC // 2) == FC // 2 - 1:
                            last.then_inc(hidden, 1)

                def reduce(u, i):
                    e = pe.value_load(keep["tile_expert"][0:1, bass.ds(i, 1)], min_val=0, max_val=E - 1)
                    pe.wait_ge(y_ready, i + 1)
                    for fc in range(FC):
                        pe.wait_ge(h_ready, i * 2 + 5 + fc // (FC // 2))
                        last = nc.tensor.matmul(p_y[u][:, 0:D], hT[:, u, fc, :],
                                                w2[:, bass.ds(e, 1), fc, :].rearrange("p o n -> p (o n)"),
                                                start=(fc == 0), stop=(fc == FC - 1))
                    last.then_inc(y_done, 1)

                def tile(turn, r, is_last):
                    i, u = turn * RING + r, r % 2
                    if not (is_last and r == RING - 1):
                        hide(1 - u, i + 1)
                    if not (is_last and r >= RING - 3):
                        turn_x(turn + (r + 3) // RING, (r + 3) % RING, i + 3)
                    reduce(u, i)

                pe.sem_inc(y_done, 2)
                turn_x(0, 0, 0, first=True)
                turn_x(0, 1, 1)
                hide(0, 0)
                turn_x(0, 2, 2)
                pe.wait_ge(keep["loaded_w2"], 16 * E)
                with pe.Fori(0, TILES // RING - 1) as turn:
                    for r in range(RING):
                        tile(turn, r, False)
                for r in range(RING):
                    tile(TILES // RING - 1, r, True)


def combine(nc, dram, keep, kept):
    RING = 4
    with ExitStack() as stack:
        m = Mem(nc, stack)
        total = m.sb("cb_total", [P, RING, GT, D], F32)
        w = [norm_scratch(m, f"cb_ln{u}") for u in range(2)]
        loaded = [m.sem(f"cb_loaded{r}") for r in range(RING)]
        halved = m.sem("cb_halved")
        added = m.sem("cb_added")
        step = m.sem("cb_step")
        normed = m.sem("cb_normed")
        stored = [m.sem(f"cb_stored{r}") for r in range(RING)]
        got = keep["w1_place"][:, 0:RING * 2 * GT * D].rearrange("p (r n a c) -> p r n a c", r=RING, n=2, a=GT)
        out_rows = dram["out"].rearrange("b s c -> (b s) c")

        with nc.Block() as block:

            @block.sync
            def _(sp):
                sp.sem_inc(added, RING)
                with sp.Fori(0, GROUPS // RING) as turn:
                    for r in range(RING):
                        g = turn * RING + r
                        sp.wait_ge(added, g + 1)
                        for n in range(2):
                            sp.dma_start(got[:, r, n, :, :], dram["rows_out"][bass.ds(g * 512 + n * T, 512), :]
                                         .rearrange("(a p) n -> p a n", p=P)).then_inc(loaded[r], 16)

            @block.gpsimd
            def _(pool):
                pool.wait_ge(keep["loaded_kept"], 16)
                with pool.Fori(0, GROUPS // RING) as turn:
                    for r in range(RING):
                        g = turn * RING + r
                        pool.wait_ge(loaded[r], turn * 32 + 32)
                        pool.wait_ge(stored[r], turn * 16 + 16)
                        nc.gpsimd.tensor_tensor(total[:, r, :, :], kept[:, bass.ds(g * GT, GT), :],
                                                got[:, r, 0, :, :], ALU.add).then_inc(halved, 1)

            @block.vector
            def _(dve):
                v = nc.vector
                with dve.Fori(0, GROUPS // RING) as turn:
                    for r in range(RING):
                        g = turn * RING + r
                        steps = Chain(dve, step, g * LN_SCALE_STEPS)
                        dve.wait_ge(halved, g + 1)
                        dve.wait_ge(normed, g + 1)
                        v.tensor_tensor(total[:, r, :, :], total[:, r, :, :], got[:, r, 1, :, :], ALU.add
                                        ).then_inc(added, 1)
                        dve.wait_ge(added, g + RING + 1)
                        norm_scale(v, steps, total[:, r, :, :], w[r % 2])
                        assert steps.n == LN_SCALE_STEPS, steps.n

            @block.scalar
            def _(act):
                for r in range(RING):
                    act.sem_inc(stored[r], 16)
                act.sem_inc(normed, 2)
                with act.Fori(0, GROUPS // RING) as turn:
                    for r in range(RING):
                        g = turn * RING + r
                        act.wait_ge(step, (g + 1) * LN_SCALE_STEPS)
                        for a in range(GT):
                            last = nc.scalar.activation(total[:, r, a, :], total[:, r, a, :], ACT.Identity,
                                                        bias=w[r % 2]["shift"][:, a:a + 1],
                                                        scale=w[r % 2]["rstd"][:, a:a + 1])
                        last.then_inc(normed, 1)
                        act.wait_ge(normed, g + 3)
                        act.dma_start(out_rows[bass.ds(g * 512, 512), :].rearrange("(a p) n -> p a n", p=P),
                                      total[:, r, :, :]).then_inc(stored[r], 16)
                for r in range(RING):
                    act.wait_ge(stored[r], 16 * (GROUPS // RING + 1))


def program(nc, dram):
    with ExitStack() as stack:
        m = Mem(nc, stack)
        keep = {
            "identity": m.sb("identity", [P, P], F32),
            "identity16": m.sb("identity16", [P, P], BF16),
            "ends": m.sb("ends", [P, E], I32),
            "tile_expert": m.sb("tile_expert", [P, TILES], I32),
            "tile_row": m.sb("tile_row", [P, TILES], I32),
            "wide": m.sb("wide", [P, 1], I32),
            "wide_ready": m.sem("wide_ready"),
            "loaded_w1": m.sem("loaded_w1"),
            "loaded_w2": m.sem("loaded_w2"),
            "loaded_kept": m.sem("loaded_kept"),
            "loaded_k": [m.sem(f"loaded_k{q}") for q in range(UNITS)],
            "b1": m.sb("b1_turned", [P, E, F // P], F32),
            "w1_place": m.sb("w1_place", [P, E * KC * F], F32),
            "w2_place": m.sb("w2_place", [P, E * F // P * D], F32),
        }
        keep["w1"] = keep["w1_place"][:, :].rearrange("p (e s n) -> p e s n", e=E, s=KC)
        keep["w2"] = keep["w2_place"][:, :].rearrange("p (e s n) -> p e s n", e=E, s=F // P)
        keep["v_all"] = keep["w2_place"][:, 0:BH * KT * HD].rearrange("p (h a w) -> p h a w", h=BH, a=KT)
        keep["k_rows"] = keep["w1_place"][:, :].bitcast(BF16).rearrange("p (h n) -> p h n", h=H)
        constants(nc, dram, keep)
        with ExitStack() as first:
            f = Mem(nc, first)
            hi_all = keep["w2_place"][:, BH * KT * HD:].bitcast(BF16).rearrange("p (k n) -> p k n", k=4)
            squares = keep["w1_place"][:, 2 * T:4 * T].bitcast(BF16).rearrange("p (k n) -> p k n", k=4)
            key_sum = f.sb("key_sum", [P, KC, GROUPS], F32)
            select = f.sb("select", [P, KC, 32], BF16)
            project(nc, dram, keep, hi_all, squares, key_sum, select)
            bounds(nc, dram, keep, hi_all, squares, key_sum, select)
        maxima(nc, dram, keep)
        attend_and_route(nc, dram, keep)
        with ExitStack() as last:
            kept = Mem(nc, last).sb("kept_rows", [P, NT, D], F32)
            experts(nc, dram, keep, kept)
            combine(nc, dram, keep, kept)


_NAMES = {'x': 'L0_attn_x', 'qkv_w': 'L0_attn_qkv_w', 'qkv_b': 'L0_attn_qkv_b', 'out_w': 'L0_attn_out_w',
          'out_b': 'L0_attn_out_b', 'g1': 'L0_ffn_g1', 'be1': 'L0_ffn_be1', 'mix_w': 'L0_ffn_mix_w',
          'mix_b': 'L0_ffn_mix_b', 'g2': 'L0_ffn_g2', 'be2': 'L0_ffn_be2', 'router_w': 'L0_ffn_router_w',
          'w1': 'L0_ffn_w1', 'b1': 'L0_ffn_b1', 'w2': 'L0_ffn_w2', 'b2': 'L0_ffn_b2'}


def _trig_table():
    import numpy as np
    inv_freq = (1.0 / 10000.0 ** (np.arange(0, HD, 2, dtype=np.float32) / np.float32(HD))).astype(np.float32)
    angle = np.arange(H, dtype=np.float32)[:, None] * inv_freq[None, :]
    return np.stack([np.cos(angle), np.sin(angle)]).astype(np.float32).reshape(-1)


def kernel(**inputs):
    import numpy as _np
    import concourse.bacc as _bacc
    from concourse import mybir as _mybir
    from concourse.bass_utils import run_bass_kernel_spmd as _run

    nc = _bacc.Bacc("TRN2", target_bir_lowering=False, num_devices=1)
    arrays, dram = {}, {}
    for short, name in _NAMES.items():
        arrays["in_" + short] = _np.ascontiguousarray(inputs[name])
    arrays["in_trig"] = _trig_table()
    for name, a in arrays.items():
        dram[name[3:]] = nc.dram_tensor(name, a.shape, _mybir.dt.from_np(a.dtype), kind="ExternalInput").ap()
    dram["out"] = nc.dram_tensor("out_0", (B, S, D), F32, kind="ExternalOutput").ap()
    dram["qk"] = [nc.dram_tensor(f"{n}_parts", (PARTS, BH * HD, S), BF16, kind="Internal").ap() for n in "qk"]
    dram["negmax"] = nc.dram_tensor("negmax", (BH, PARTS, S), BF16, kind="Internal").ap()
    dram["rows_in"] = nc.dram_tensor("rows_in", (E * REGION, ROW), F32, kind="Internal").ap()
    dram["rows_out"] = nc.dram_tensor("rows_out", (2 * T + E * P, D), F32, kind="Internal").ap()
    dram["kept"] = nc.dram_tensor("kept", (T, D), F32, kind="Internal").ap()
    program(nc, dram)
    r = _run(nc, [arrays], core_ids=[0])
    return r.results[0]["out_0"]
```
